# Optimizing a Trainium2 kernel written in Bass

```python
import numpy as np
import jax
import jax.numpy as jnp

def _softmax(x, axis=-1):
    return jax.nn.softmax(x, axis=axis)

def _gelu(x):
    return jax.nn.gelu(x, approximate=True)

def _silu(x):
    return jax.nn.silu(x)

def _sigmoid(x):
    return jax.nn.sigmoid(x)

def _layernorm(x, axis=-1, eps=1e-05):
    m = jnp.mean(x, axis=axis, keepdims=True)
    v = jnp.var(x, axis=axis, keepdims=True)
    return (x - m) / jnp.sqrt(v + eps)

def _scatter_add(tgt, idx, src, axis=0):
    return tgt.at[idx].add(src)

def _segment_sum(src, seg, n):
    return jax.ops.segment_sum(src, seg, n)
kernel_name = 'mk_perceiver_d2_seqx_r8_5a59be'

def setup_inputs(seed: int=0):
    np.random.seed(seed)
    _w = jnp.asarray

    def _rec_inputs():
        import jax
        import jax.numpy as jnp
        _rk = jax.random.key(seed)
        x = -0.0002928 + 1 * jax.random.normal(jax.random.fold_in(_rk, 1), (16, 64, 256), jnp.float32)
        _lenS = 64 - jax.random.randint(jax.random.fold_in(_rk, 7), (16,), 0, max(1, 64 // 4) + 1, jnp.int32)
        _lenS2 = 1601 - jax.random.randint(jax.random.fold_in(_rk, 8), (16,), 0, max(1, 1601 // 4) + 1, jnp.int32)
        _ctx_512P = jax.random.normal(jax.random.fold_in(_rk, 11), (16, 16, 64), jnp.float32)
        _ctx_512c = jax.random.dirichlet(jax.random.fold_in(_rk, 511), 0.3 * jnp.ones((16,), jnp.float32), (16, 1601))
        _ctx_512t = jnp.einsum('bsk,bkd->bsd', _ctx_512c, _ctx_512P)
        _ctx_512t = _ctx_512t * jax.lax.rsqrt(jnp.mean(jnp.square(_ctx_512t)) + 1e-12) * 0.953939
        ctx_512 = 0.000227908 + 0.99994 * (_ctx_512t + 0.3 * jax.random.normal(jax.random.fold_in(_rk, 611), (16, 1601, 64), jnp.float32))
        return (x, ctx_512)
    x, ctx_512 = _rec_inputs()

    def _L0_xattn_setup():
        import jax, jax.numpy as jnp
        import numpy as np
        B, S, L = (2, 128, 128)
        DIM_Q, H, K, D_C, D_CQ, R = (256, 16, 128, 64, 192, 64)

        def _rope_tables(seq_len, dim, dtype):
            inv_freq = 1.0 / 10000.0 ** (jnp.arange(0, dim, 2, dtype=dtype) / dim)
            t = jnp.arange(seq_len, dtype=dtype)
            freqs = t[:, None] * inv_freq[None, :]
            sin = jnp.repeat(jnp.sin(freqs), 2, axis=-1)
            cos = jnp.repeat(jnp.cos(freqs), 2, axis=-1)
            return (sin, cos)

        def _rotate_half(x):
            h = x.shape[-1] // 2
            return jnp.concatenate([-x[..., h:], x[..., :h]], axis=-1)
        key = jax.random.key(seed)
        ks = jax.random.split(key, 8)
        s_in = 1.0 / np.sqrt(DIM_Q)
        s_k = 1.0 / np.sqrt(K)
        s_cq = 1.0 / np.sqrt(D_CQ)
        s_c = 1.0 / np.sqrt(D_C)
        return {'hidden_q': jax.random.normal(ks[0], (B, S, DIM_Q), jnp.float32), 'kv_c': jax.random.normal(ks[1], (B, L, D_C), jnp.float32), 'Wq': jax.random.normal(ks[2], (H * K, DIM_Q), jnp.float32) * s_in, 'w_kc_q': jax.random.normal(ks[3], (H, K, D_CQ), jnp.float32) * s_k, 'w_kc_kv': jax.random.normal(ks[4], (H, K, D_C), jnp.float32) * s_k, 'W_qr': jax.random.normal(ks[5], (H, D_CQ, R), jnp.float32) * s_cq / np.sqrt(R), 'W_kr': jax.random.normal(ks[6], (H, D_C, R), jnp.float32) * s_c, 'Wo': jax.random.normal(ks[7], (DIM_Q, H * K), jnp.float32) * s_k}
    _L0_xattn_all = _L0_xattn_setup()
    _L0_xattn_in = {k: v for k, v in _L0_xattn_all.items() if k in ('Wq', 'w_kc_q', 'w_kc_kv', 'W_qr', 'W_kr', 'Wo')}
    del _L0_xattn_all

    def _L0_attn_setup():
        import jax, jax.numpy as jnp
        import numpy as np
        import math
        D_MODEL = 256
        N_HEADS = 16
        D_HEAD = D_MODEL // N_HEADS
        SCALE = 1.0 / math.sqrt(D_HEAD)
        key = jax.random.key(seed)
        kx, kq, kk, kv, ko = jax.random.split(key, 5)
        x = jax.random.normal(kx, (2, 256, D_MODEL), dtype=jnp.float32)
        W_q = jax.random.normal(kq, (D_MODEL, D_MODEL), dtype=jnp.float32)
        W_k = jax.random.normal(kk, (D_MODEL, D_MODEL), dtype=jnp.float32)
        W_v = jax.random.normal(kv, (D_MODEL, D_MODEL), dtype=jnp.float32) * math.sqrt(2.0 / D_MODEL)
        W_o = jax.random.normal(ko, (D_MODEL, D_MODEL), dtype=jnp.float32) * math.sqrt(2.0 / D_MODEL)
        return {'x': x, 'W_q': W_q, 'W_k': W_k, 'W_v': W_v, 'W_o': W_o}
    _L0_attn_all = _L0_attn_setup()
    _L0_attn_in = {k: v for k, v in _L0_attn_all.items() if k in ('W_q', 'W_k', 'W_v', 'W_o')}
    del _L0_attn_all

    def _L0_ffn_setup():
        import jax, jax.numpy as jnp
        import numpy as np
        H = 256
        E = 16
        K = 4
        I = 176
        IS = 176 * 2
        B, S = (1, 128)
        key = jax.random.key(seed)
        ks = jax.random.split(key, 9)
        scale = 0.02
        return {'hidden_states': jax.random.normal(ks[0], (B, S, H), dtype=jnp.float32), 'gate_w': jax.random.normal(ks[1], (E, H), dtype=jnp.float32) * scale, 'w_gate': jax.random.normal(ks[2], (E, H, I), dtype=jnp.float32) * scale, 'w_up': jax.random.normal(ks[3], (E, H, I), dtype=jnp.float32) * scale, 'w_down': jax.random.normal(ks[4], (E, I, H), dtype=jnp.float32) * scale, 'sw_gate': jax.random.normal(ks[5], (H, IS), dtype=jnp.float32) * scale, 'sw_up': jax.random.normal(ks[6], (H, IS), dtype=jnp.float32) * scale, 'sw_down': jax.random.normal(ks[7], (IS, H), dtype=jnp.float32) * scale}
    _L0_ffn_all = _L0_ffn_setup()
    _L0_ffn_in = {k: v for k, v in _L0_ffn_all.items() if k in ('gate_w', 'w_gate', 'w_up', 'w_down', 'sw_gate', 'sw_up', 'sw_down')}
    del _L0_ffn_all

    def _L1_xattn_setup():
        import jax, jax.numpy as jnp
        import numpy as np
        B, S, H, NH, L = (2, 256, 256, 16, 64)
        HD = H // NH
        key = jax.random.key(seed)
        k1, k2, k3, k4, k5 = jax.random.split(key, 5)
        scale = 0.02
        return {'q': jax.random.normal(k1, (B, S, H), dtype=jnp.float32), 'latent_kv': jax.random.normal(k2, (B, S, L), dtype=jnp.float32), 'Wq': jax.random.normal(k3, (H, H), dtype=jnp.float32) * scale, 'Wkv_expand': jax.random.normal(k4, (2 * H, L), dtype=jnp.float32) * scale, 'Wout': jax.random.normal(k5, (H, H), dtype=jnp.float32) * scale}
    _L1_xattn_all = _L1_xattn_setup()
    _L1_xattn_in = {k: v for k, v in _L1_xattn_all.items() if k in ('Wq', 'Wkv_expand', 'Wout')}
    del _L1_xattn_all

    def _L1_attn_setup():
        import jax, jax.numpy as jnp
        import numpy as np
        EPS = 1e-05

        def _layer_norm(x, w, b):
            mu = jnp.mean(x, axis=-1, keepdims=True)
            var = jnp.mean((x - mu) ** 2, axis=-1, keepdims=True)
            return (x - mu) * jax.lax.rsqrt(var + EPS) * w + b

        def _wkv(k, v, time_decay, curr_w):
            B, T, H = k.shape
            decay = -jnp.exp(time_decay)
            num0 = jnp.zeros((B, H), k.dtype)
            den0 = jnp.zeros((B, H), k.dtype)
            norm0 = jnp.full((B, H), -jnp.inf, k.dtype)

            def step(carry, kv):
                num, den, norm = carry
                kt, vt = kv
                ct = curr_w + kt
                cn = jnp.maximum(ct, norm)
                e_prev = jnp.exp(norm - cn)
                e_cur = jnp.exp(ct - cn)
                out = (e_prev * num + e_cur * vt) / (e_prev * den + e_cur)
                dpn = decay + norm
                new_norm = jnp.maximum(dpn, kt)
                e_d = jnp.exp(dpn - new_norm)
                e_k = jnp.exp(kt - new_norm)
                return ((e_d * num + e_k * vt, e_d * den + e_k, new_norm), out)
            kT = jnp.swapaxes(k, 0, 1)
            vT = jnp.swapaxes(v, 0, 1)
            (num, den, norm), outs = jax.lax.scan(step, (num0, den0, norm0), (kT, vT))
            return (jnp.swapaxes(outs, 0, 1), num, den, norm)

        def _reference_tuple_inner(hidden_state, ln_w, ln_b, Wk, Wv, Wr, Wo, mix_k, mix_v, mix_r, time_decay, current_token_weight):
            residual = hidden_state
            x = _layer_norm(hidden_state, ln_w, ln_b)
            B, T, H = x.shape
            sx = jnp.concatenate([jnp.zeros((B, 1, H), x.dtype), x[:, :-1, :]], axis=1)
            xk = sx + mix_k * (x - sx)
            xv = sx + mix_v * (x - sx)
            xr = sx + mix_r * (x - sx)
            r = jax.nn.sigmoid(jnp.einsum('bth,oh->bto', xr, Wr))
            k = jnp.einsum('bth,oh->bto', xk, Wk)
            v = jnp.einsum('bth,oh->bto', xv, Wv)
            wkv, num, den, norm = _wkv(k, v, time_decay, current_token_weight)
            rwkv = jnp.einsum('bth,oh->bto', r * wkv, Wo)
            out = residual + rwkv
            return (out, (x[:, -1, :], num, den, norm))
        H = 256
        B, T = (4, 256)
        key = jax.random.key(seed)
        ks = jax.random.split(key, 12)
        s = 0.02
        return {'hidden_state': jax.random.normal(ks[0], (B, T, H), dtype=jnp.float32), 'ln_w': jnp.ones((H,), jnp.float32), 'ln_b': jnp.zeros((H,), jnp.float32), 'Wk': jax.random.normal(ks[1], (H, H), jnp.float32) * s, 'Wv': jax.random.normal(ks[2], (H, H), jnp.float32) * s, 'Wr': jax.random.normal(ks[3], (H, H), jnp.float32) * s, 'Wo': jax.random.normal(ks[4], (H, H), jnp.float32) * s, 'mix_k': jax.random.uniform(ks[5], (H,), jnp.float32), 'mix_v': jax.random.uniform(ks[6], (H,), jnp.float32), 'mix_r': jax.random.uniform(ks[7], (H,), jnp.float32), 'time_decay': jax.random.normal(ks[8], (H,), jnp.float32) * 0.5, 'current_token_weight': jax.random.normal(ks[9], (H,), jnp.float32) * 0.5}
    _L1_attn_all = _L1_attn_setup()
    _L1_attn_in = {k: v for k, v in _L1_attn_all.items() if k in ('ln_w', 'ln_b', 'Wk', 'Wv', 'Wr', 'Wo', 'mix_k', 'mix_v', 'mix_r', 'time_decay', 'current_token_weight')}
    del _L1_attn_all

    def _L1_ffn_setup():
        import jax, jax.numpy as jnp
        import numpy as np
        H = 256
        E = 64
        I = 64
        SI = 64
        TOP_K = 8
        B, T = (2, 64)
        key = jax.random.key(seed)
        ks = jax.random.split(key, 8)
        s = 0.02
        return {'h': jax.random.normal(ks[0], (B, T, H), jnp.float32), 'gate_w': jax.random.normal(ks[1], (E, H), jnp.float32) * s, 'gu_w': jax.random.normal(ks[2], (E, 2 * I, H), jnp.float32) * s, 'dp_w': jax.random.normal(ks[3], (E, H, I), jnp.float32) * s, 'sh_gate_w': jax.random.normal(ks[4], (SI, H), jnp.float32) * s, 'sh_up_w': jax.random.normal(ks[5], (SI, H), jnp.float32) * s, 'sh_down_w': jax.random.normal(ks[6], (H, SI), jnp.float32) * s, 'sh_gate1_w': jax.random.normal(ks[7], (1, H), jnp.float32) * s}
    _L1_ffn_all = _L1_ffn_setup()
    _L1_ffn_in = {k: v for k, v in _L1_ffn_all.items() if k in ('gate_w', 'gu_w', 'dp_w', 'sh_gate_w', 'sh_up_w', 'sh_down_w', 'sh_gate1_w')}
    del _L1_ffn_all
    return {'x': x, 'ctx_512': ctx_512, 'L0_xattn_Wq': _L0_xattn_in['Wq'], 'L0_xattn_w_kc_q': _L0_xattn_in['w_kc_q'], 'L0_xattn_w_kc_kv': _L0_xattn_in['w_kc_kv'], 'L0_xattn_W_qr': _L0_xattn_in['W_qr'], 'L0_xattn_W_kr': _L0_xattn_in['W_kr'], 'L0_xattn_Wo': _L0_xattn_in['Wo'], 'L0_attn_W_q': _L0_attn_in['W_q'], 'L0_attn_W_k': _L0_attn_in['W_k'], 'L0_attn_W_v': _L0_attn_in['W_v'], 'L0_attn_W_o': _L0_attn_in['W_o'], 'L0_ffn_gate_w': _L0_ffn_in['gate_w'], 'L0_ffn_w_gate': _L0_ffn_in['w_gate'], 'L0_ffn_w_up': _L0_ffn_in['w_up'], 'L0_ffn_w_down': _L0_ffn_in['w_down'], 'L0_ffn_sw_gate': _L0_ffn_in['sw_gate'], 'L0_ffn_sw_up': _L0_ffn_in['sw_up'], 'L0_ffn_sw_down': _L0_ffn_in['sw_down'], 'L1_xattn_Wq': _L1_xattn_in['Wq'], 'L1_xattn_Wkv_expand': _L1_xattn_in['Wkv_expand'], 'L1_xattn_Wout': _L1_xattn_in['Wout'], 'L1_attn_ln_w': _L1_attn_in['ln_w'], 'L1_attn_ln_b': _L1_attn_in['ln_b'], 'L1_attn_Wk': _L1_attn_in['Wk'], 'L1_attn_Wv': _L1_attn_in['Wv'], 'L1_attn_Wr': _L1_attn_in['Wr'], 'L1_attn_Wo': _L1_attn_in['Wo'], 'L1_attn_mix_k': _L1_attn_in['mix_k'], 'L1_attn_mix_v': _L1_attn_in['mix_v'], 'L1_attn_mix_r': _L1_attn_in['mix_r'], 'L1_attn_time_decay': _L1_attn_in['time_decay'], 'L1_attn_current_token_weight': _L1_attn_in['current_token_weight'], 'L1_ffn_gate_w': _L1_ffn_in['gate_w'], 'L1_ffn_gu_w': _L1_ffn_in['gu_w'], 'L1_ffn_dp_w': _L1_ffn_in['dp_w'], 'L1_ffn_sh_gate_w': _L1_ffn_in['sh_gate_w'], 'L1_ffn_sh_up_w': _L1_ffn_in['sh_up_w'], 'L1_ffn_sh_down_w': _L1_ffn_in['sh_down_w'], 'L1_ffn_sh_gate1_w': _L1_ffn_in['sh_gate1_w']}

def reference(x, ctx_512, L0_xattn_Wq, L0_xattn_w_kc_q, L0_xattn_w_kc_kv, L0_xattn_W_qr, L0_xattn_W_kr, L0_xattn_Wo, L0_attn_W_q, L0_attn_W_k, L0_attn_W_v, L0_attn_W_o, L0_ffn_gate_w, L0_ffn_w_gate, L0_ffn_w_up, L0_ffn_w_down, L0_ffn_sw_gate, L0_ffn_sw_up, L0_ffn_sw_down, L1_xattn_Wq, L1_xattn_Wkv_expand, L1_xattn_Wout, L1_attn_ln_w, L1_attn_ln_b, L1_attn_Wk, L1_attn_Wv, L1_attn_Wr, L1_attn_Wo, L1_attn_mix_k, L1_attn_mix_v, L1_attn_mix_r, L1_attn_time_decay, L1_attn_current_token_weight, L1_ffn_gate_w, L1_ffn_gu_w, L1_ffn_dp_w, L1_ffn_sh_gate_w, L1_ffn_sh_up_w, L1_ffn_sh_down_w, L1_ffn_sh_gate1_w):
    import jax
    import jax.numpy as jnp

    def _L0_xattn_ref(hidden_q, kv_c, Wq, w_kc_q, w_kc_kv, W_qr, W_kr, Wo):
        import jax, jax.numpy as jnp
        import numpy as np
        B, S, L = (2, 128, 128)
        DIM_Q, H, K, D_C, D_CQ, R = (256, 16, 128, 64, 192, 64)

        def _rope_tables(seq_len, dim, dtype):
            inv_freq = 1.0 / 10000.0 ** (jnp.arange(0, dim, 2, dtype=dtype) / dim)
            t = jnp.arange(seq_len, dtype=dtype)
            freqs = t[:, None] * inv_freq[None, :]
            sin = jnp.repeat(jnp.sin(freqs), 2, axis=-1)
            cos = jnp.repeat(jnp.cos(freqs), 2, axis=-1)
            return (sin, cos)

        def _rotate_half(x):
            h = x.shape[-1] // 2
            return jnp.concatenate([-x[..., h:], x[..., :h]], axis=-1)
        b, s, _ = hidden_q.shape
        l = kv_c.shape[1]
        q_hk = (hidden_q @ Wq.T).reshape(b, s, H, K)
        q_big = jnp.einsum('bshk,hkq->bshq', q_hk, w_kc_q)
        sin, cos = _rope_tables(l, D_C, kv_c.dtype)
        kv_rope = kv_c * cos[None] + _rotate_half(kv_c) * sin[None]
        q_r = jnp.einsum('bshq,hqr->bhsr', q_big, W_qr)
        k_r = jnp.einsum('bld,hdr->bhlr', kv_rope, W_kr)
        scores = jnp.einsum('bhsr,bhlr->bhsl', q_r, k_r)
        attn = jax.nn.softmax(scores, axis=-1)
        ctx_c = jnp.einsum('bhsl,bld->bhsd', attn, kv_rope)
        ctx_lat = jnp.einsum('bhsd,hkd->bshk', ctx_c, w_kc_kv)
        out = ctx_lat.reshape(b, s, H * K) @ Wo.T
        return out

    def _L0_attn_ref(x, W_q, W_k, W_v, W_o):
        import jax, jax.numpy as jnp
        import numpy as np
        import math
        D_MODEL = 256
        N_HEADS = 16
        D_HEAD = D_MODEL // N_HEADS
        SCALE = 1.0 / math.sqrt(D_HEAD)
        B, S, D = x.shape
        q = (x @ W_q).reshape(B, S, N_HEADS, D_HEAD)
        k = (x @ W_k).reshape(B, S, N_HEADS, D_HEAD)
        v = x @ W_v
        scores = jnp.einsum('bqhd,bkhd->bhqk', q, k)
        mask = jnp.triu(jnp.full((S, S), -1000000000.0, dtype=scores.dtype), k=1)
        scores = (scores + mask) * SCALE
        probs = jax.nn.softmax(scores, axis=-1)
        out = jnp.einsum('bhqk,bkd->bqd', probs, v)
        return out @ W_o

    def _L0_ffn_ref(hidden_states, gate_w, w_gate, w_up, w_down, sw_gate, sw_up, sw_down):
        import jax, jax.numpy as jnp
        import numpy as np
        H = 256
        E = 16
        K = 4
        I = 176
        IS = 176 * 2
        B, S = (1, 128)
        orig_shape = hidden_states.shape
        x = hidden_states.reshape(-1, H)
        T = x.shape[0]
        logits = jnp.einsum('th,eh->te', x, gate_w)
        scores = jax.nn.softmax(logits, axis=-1)
        topk_w, topk_idx = jax.lax.top_k(scores, K)
        topk_w = topk_w / jnp.sum(topk_w, axis=-1, keepdims=True)
        combine = jnp.zeros((T, E), dtype=x.dtype)
        combine = combine.at[jnp.arange(T)[:, None], topk_idx].add(topk_w)
        g = jnp.einsum('th,ehi->tei', x, w_gate)
        u = jnp.einsum('th,ehi->tei', x, w_up)
        a = jax.nn.silu(g) * u
        a = a * combine[:, :, None]
        y = jnp.einsum('tei,eih->th', a, w_down)
        sg = x @ sw_gate
        su = x @ sw_up
        y = y + jax.nn.silu(sg) * su @ sw_down
        return y.reshape(orig_shape)

    def _L1_xattn_ref(q, latent_kv, Wq, Wkv_expand, Wout):
        import jax, jax.numpy as jnp
        import numpy as np
        B, S, H, NH, L = (2, 256, 256, 16, 64)
        HD = H // NH
        b, sq, _ = q.shape
        sk = latent_kv.shape[1]
        qp = q @ Wq.T
        kv = latent_kv @ Wkv_expand.T
        k, v = jnp.split(kv, 2, axis=-1)
        qh = qp.reshape(b, sq, NH, HD).transpose(0, 2, 1, 3)
        kh = k.reshape(b, sk, NH, HD).transpose(0, 2, 1, 3)
        vh = v.reshape(b, sk, NH, HD).transpose(0, 2, 1, 3)
        inv_sqrt_d = 1.0 / jnp.sqrt(jnp.float32(HD))
        scores = jnp.einsum('bhqd,bhkd->bhqk', qh, kh) * inv_sqrt_d
        causal = jnp.tril(jnp.ones((sq, sk), dtype=bool))
        scores = jnp.where(causal, scores, jnp.finfo(scores.dtype).min)
        attn = jax.nn.softmax(scores, axis=-1)
        out = jnp.einsum('bhqk,bhkd->bhqd', attn, vh)
        out = out.transpose(0, 2, 1, 3).reshape(b, sq, H)
        return out @ Wout.T

    def _L1_attn_ref(hidden_state, ln_w, ln_b, Wk, Wv, Wr, Wo, mix_k, mix_v, mix_r, time_decay, current_token_weight):
        import jax, jax.numpy as jnp
        import numpy as np
        EPS = 1e-05

        def _layer_norm(x, w, b):
            mu = jnp.mean(x, axis=-1, keepdims=True)
            var = jnp.mean((x - mu) ** 2, axis=-1, keepdims=True)
            return (x - mu) * jax.lax.rsqrt(var + EPS) * w + b

        def _wkv(k, v, time_decay, curr_w):
            B, T, H = k.shape
            decay = -jnp.exp(time_decay)
            num0 = jnp.zeros((B, H), k.dtype)
            den0 = jnp.zeros((B, H), k.dtype)
            norm0 = jnp.full((B, H), -jnp.inf, k.dtype)

            def step(carry, kv):
                num, den, norm = carry
                kt, vt = kv
                ct = curr_w + kt
                cn = jnp.maximum(ct, norm)
                e_prev = jnp.exp(norm - cn)
                e_cur = jnp.exp(ct - cn)
                out = (e_prev * num + e_cur * vt) / (e_prev * den + e_cur)
                dpn = decay + norm
                new_norm = jnp.maximum(dpn, kt)
                e_d = jnp.exp(dpn - new_norm)
                e_k = jnp.exp(kt - new_norm)
                return ((e_d * num + e_k * vt, e_d * den + e_k, new_norm), out)
            kT = jnp.swapaxes(k, 0, 1)
            vT = jnp.swapaxes(v, 0, 1)
            (num, den, norm), outs = jax.lax.scan(step, (num0, den0, norm0), (kT, vT))
            return (jnp.swapaxes(outs, 0, 1), num, den, norm)

        def _reference_tuple_inner(hidden_state, ln_w, ln_b, Wk, Wv, Wr, Wo, mix_k, mix_v, mix_r, time_decay, current_token_weight):
            residual = hidden_state
            x = _layer_norm(hidden_state, ln_w, ln_b)
            B, T, H = x.shape
            sx = jnp.concatenate([jnp.zeros((B, 1, H), x.dtype), x[:, :-1, :]], axis=1)
            xk = sx + mix_k * (x - sx)
            xv = sx + mix_v * (x - sx)
            xr = sx + mix_r * (x - sx)
            r = jax.nn.sigmoid(jnp.einsum('bth,oh->bto', xr, Wr))
            k = jnp.einsum('bth,oh->bto', xk, Wk)
            v = jnp.einsum('bth,oh->bto', xv, Wv)
            wkv, num, den, norm = _wkv(k, v, time_decay, current_token_weight)
            rwkv = jnp.einsum('bth,oh->bto', r * wkv, Wo)
            out = residual + rwkv
            return (out, (x[:, -1, :], num, den, norm))
        return _reference_tuple_inner(hidden_state, ln_w, ln_b, Wk, Wv, Wr, Wo, mix_k, mix_v, mix_r, time_decay, current_token_weight)[0]

    def _L1_ffn_ref(h, gate_w, gu_w, dp_w, sh_gate_w, sh_up_w, sh_down_w, sh_gate1_w):
        import jax, jax.numpy as jnp
        import numpy as np
        H = 256
        E = 64
        I = 64
        SI = 64
        TOP_K = 8
        B, T = (2, 64)
        Bb, Tt, Hh = h.shape
        x = h.reshape(Bb * Tt, Hh)
        N = x.shape[0]
        logits = x @ gate_w.T
        topv, topi = jax.lax.top_k(logits, TOP_K)
        rw = jax.nn.softmax(topv.astype(jnp.float32), axis=-1).astype(x.dtype)
        W = jnp.zeros((N, E), x.dtype).at[jnp.arange(N)[:, None], topi].set(rw)
        gu = jnp.einsum('nh,eih->nei', x, gu_w)
        gate, up = (gu[..., :I], gu[..., I:])
        inter = jax.nn.silu(gate) * up
        inter_w = inter * W[:, :, None]
        out = jnp.einsum('nei,ehi->nh', inter_w, dp_w)
        sh_inter = jax.nn.silu(x @ sh_gate_w.T) * (x @ sh_up_w.T)
        sh_out = sh_inter @ sh_down_w.T
        sh_g = jax.nn.sigmoid(x @ sh_gate1_w.T)
        out = out + sh_g * sh_out
        return out.reshape(Bb, Tt, Hh)
    x = x + _L0_xattn_ref(_layernorm(x, axis=-1), ctx_512, L0_xattn_Wq, L0_xattn_w_kc_q, L0_xattn_w_kc_kv, L0_xattn_W_qr, L0_xattn_W_kr, L0_xattn_Wo)
    x = x + _L0_attn_ref(_layernorm(x, axis=-1), L0_attn_W_q, L0_attn_W_k, L0_attn_W_v, L0_attn_W_o)
    x = x + _L0_ffn_ref(_layernorm(x, axis=-1), L0_ffn_gate_w, L0_ffn_w_gate, L0_ffn_w_up, L0_ffn_w_down, L0_ffn_sw_gate, L0_ffn_sw_up, L0_ffn_sw_down)
    x = x + _L1_xattn_ref(_layernorm(x, axis=-1), ctx_512, L1_xattn_Wq, L1_xattn_Wkv_expand, L1_xattn_Wout)
    x = x + _L1_attn_ref(_layernorm(x, axis=-1), L1_attn_ln_w, L1_attn_ln_b, L1_attn_Wk, L1_attn_Wv, L1_attn_Wr, L1_attn_Wo, L1_attn_mix_k, L1_attn_mix_v, L1_attn_mix_r, L1_attn_time_decay, L1_attn_current_token_weight)
    x = x + _L1_ffn_ref(_layernorm(x, axis=-1), L1_ffn_gate_w, L1_ffn_gu_w, L1_ffn_dp_w, L1_ffn_sh_gate_w, L1_ffn_sh_up_w, L1_ffn_sh_down_w, L1_ffn_sh_gate1_w)
    return x

_drawn_inputs = setup_inputs


def setup_inputs(seed=0):
    import zlib

    import numpy as np

    out = dict(_drawn_inputs(seed))
    spreads = {'L1_attn_ln_w': (1.0, 0.6), 'L1_attn_ln_b': (0.0, 0.8)}
    factors = {'L0_ffn_gate_w': 8.0,
     'L0_ffn_w_gate': 8.0,
     'L0_ffn_w_up': 8.0,
     'L0_ffn_w_down': 8.0,
     'L0_ffn_sw_gate': 8.0,
     'L0_ffn_sw_up': 8.0,
     'L0_ffn_sw_down': 8.0,
     'L1_xattn_Wq': 8.0,
     'L1_xattn_Wkv_expand': 8.0,
     'L1_xattn_Wout': 8.0,
     'L1_attn_Wk': 8.0,
     'L1_attn_Wv': 8.0,
     'L1_attn_Wr': 8.0,
     'L1_attn_Wo': 8.0,
     'L1_attn_mix_k': 8.0,
     'L1_attn_mix_v': 8.0,
     'L1_attn_mix_r': 8.0,
     'L1_attn_time_decay': 8.0,
     'L1_attn_current_token_weight': 8.0,
     'L1_ffn_gate_w': 8.0,
     'L1_ffn_gu_w': 8.0,
     'L1_ffn_dp_w': 8.0,
     'L1_ffn_sh_gate_w': 8.0,
     'L1_ffn_sh_up_w': 8.0,
     'L1_ffn_sh_down_w': 8.0,
     'L1_ffn_sh_gate1_w': 8.0}
    for name, (base, spread) in spreads.items():
        noise = np.random.default_rng([zlib.crc32(name.encode()), seed]).standard_normal(out[name].shape)
        drawn = base * np.exp(spread * noise) if base else spread * noise
        out[name] = jnp.asarray(drawn.astype(out[name].dtype))
    for name, factor in factors.items():
        out[name] = (out[name] * factor).astype(out[name].dtype)
    return out
```

```python
from contextlib import ExitStack

import concourse.bass as bass
from concourse import mybir

F32 = mybir.dt.float32
F32R = mybir.dt.float32r
BF16 = mybir.dt.bfloat16
ALU = mybir.AluOpType
ACT = mybir.ActivationFunctionType
AX = mybir.AxisListType

P = 128
BATCH, SEQ, HID = 16, 64, 256
TOK = BATCH * SEQ
TILES = TOK // P
HC = HID // P
BLK = 512
EPS = 1e-5
NEG = -1.0e30

HEADS = 16
KEYS, DC, DCQ, RR, DK = 1601, 64, 192, 64, 128
KT = -(-KEYS // P)
KLAST = KEYS - (KT - 1) * P
KPAD = KEYS + KEYS % 2
KA = 6 * P
KB = KEYS - KA
UPB = HEADS // 2
DH = HID // HEADS


class Semaphores:

    def __init__(self, nc):
        self.nc, self.held = nc, []

    def __call__(self, name):
        self.held.append(self.nc.alloc_semaphore(name))
        return self.held[-1]

    def recycle(self):
        self.nc.clear_and_free_semaphores(self.held)
        self.nc.all_engine_barrier()
        self.held = []


def chain(eng, sem):
    n = [0]

    def link(ins):
        n[0] += 1
        ins.then_inc(sem, 1)
        eng.wait_ge(sem, n[0])
    return link


def layernorm(nc, sems, name, X, ident, outs, affine=None, s_affine=None, twice=False, loads=None, x_load=None):
    with ExitStack() as ctx:
        sb = lambda n, s, d=F32: ctx.enter_context(nc.sbuf_tensor(f"{name}_{n}", s, d))
        sem = lambda n: sems(f"{name}_{n}")
        xn = sb("xn", [P, TILES, HID])
        stats = sb("stats", [P, TILES, 6])
        mv = sb("mv", [P, TILES, 2])
        var, sd, r0, t0, rstd = (sb(n, [P, TILES]) for n in ("var", "sd", "r0", "t0", "rstd"))
        psT = [ctx.enter_context(nc.psum_tensor(f"{name}_psT{i}", [P, BLK], F32)) for i in range(4)]
        s_dve, s_var, s_sd, s_xn, s_tr, s_hi, s_lo = (
            sem(n) for n in ("dve", "var", "sd", "xn", "tr", "hi", "lo"))
        with nc.Block() as block:
            @block.sync
            def _(sp):
                if loads is not None:
                    loads(sp)

            @block.vector
            def _(dve):
                link = chain(dve, s_dve)

                def normalise(n, x, signal):
                    for t in range(TILES):
                        if x_load is not None and t % 4 == 0:
                            dve.wait_ge(x_load[t // 4], 16)
                        last = dve.bn_stats(stats[:, t, :], x[:, t, :])
                    link(last)
                    for t in range(TILES):
                        last = dve.bn_aggr(mv[:, t, :], stats[:, t, :])
                    link(last)
                    dve.tensor_scalar(var[:, :], mv[:, :, 1], EPS, None, ALU.add).then_inc(s_var, 1)
                    dve.wait_ge(s_sd, n + 1)
                    link(dve.reciprocal(r0[:, :], sd[:, :]))
                    link(dve.tensor_tensor(t0[:, :], r0[:, :], r0[:, :], ALU.mult))
                    link(dve.tensor_tensor(t0[:, :], t0[:, :], var[:, :], ALU.mult))
                    link(dve.tensor_scalar(t0[:, :], t0[:, :], -0.5, 1.5, ALU.mult, ALU.add))
                    link(dve.tensor_tensor(rstd[:, :], r0[:, :], t0[:, :], ALU.mult))
                    for t in range(TILES):
                        last = dve.tensor_scalar(xn[:, t, :], x[:, t, :], mv[:, t, 0:1], rstd[:, t:t + 1],
                                                 ALU.subtract, ALU.mult)
                        if signal:
                            last.then_inc(s_xn, 1)
                    return last

                if twice:
                    link(normalise(0, X, False))
                    link(dve.tensor_tensor(X[:, :, :], X[:, :, :], xn[:, :, :], ALU.add))
                    normalise(1, xn, True)
                else:
                    normalise(0, X, True)
                if affine is not None:
                    dve.wait_ge(s_affine, 16)
                for g in range(4):
                    c, half = g % 2, g // 2
                    cols = slice(half * BLK, half * BLK + BLK)
                    if len(outs) == 2:
                        dve.wait_ge(s_hi, g + 1)
                        dve.tensor_tensor(outs[1][:, c, cols], psT[g][:, :], outs[0][:, c, cols].bitcast(F32),
                                          ALU.subtract).then_inc(s_lo, 1)
                    elif g % 2:
                        dve.wait_ge(s_tr, g + 1)
                        if affine is None:
                            dve.tensor_copy(outs[0][:, c, cols], psT[g][:, :]).then_inc(s_lo, 1)
                        else:
                            w, b = affine
                            dve.tensor_scalar(outs[0][:, c, cols], psT[g][:, :], w[:, c:c + 1], b[:, c:c + 1],
                                              ALU.mult, ALU.add).then_inc(s_lo, 1)

            @block.tensor
            def _(pe):
                for g in range(4):
                    c, half = g % 2, g // 2
                    for j in range(4):
                        t = 4 * half + j
                        if c == 0:
                            pe.wait_ge(s_xn, t + 1)
                        last = pe.transpose(psT[g][:, j * P:(j + 1) * P], xn[:, t, c * P:(c + 1) * P], ident[:, :])
                    last.then_inc(s_tr, 1)

            @block.scalar
            def _(act):
                for n in range(2 if twice else 1):
                    act.wait_ge(s_var, n + 1)
                    act.activation(sd[:, :], var[:, :], ACT.Sqrt).then_inc(s_sd, 1)
                if affine is not None:
                    act.wait_ge(s_affine, 16)
                for g in range(4):
                    c, half = g % 2, g // 2
                    cols = slice(half * BLK, half * BLK + BLK)
                    if len(outs) == 2:
                        act.wait_ge(s_tr, g + 1)
                        act.activation(outs[0][:, c, cols], psT[g][:, :], ACT.Copy).then_inc(s_hi, 1)
                    elif g % 2 == 0:
                        act.wait_ge(s_tr, g + 1)
                        if affine is None:
                            act.activation(outs[0][:, c, cols], psT[g][:, :], ACT.Copy).then_inc(s_hi, 1)
                        else:
                            w, b = affine
                            act.activation(outs[0][:, c, cols], psT[g][:, :], ACT.Identity,
                                           scale=w[:, c:c + 1], bias=b[:, c:c + 1]).then_inc(s_hi, 1)


def load_latents(sp, src, raw, s_raw, b, slot):
    sp.dma_start(raw[slot][:, 0:KT - 1, :],
                 src["ctx"][b, 0:(KT - 1) * P, :].rearrange("(t p) d -> p t d", p=P)).then_inc(s_raw[slot], 16)
    sp.dma_start(raw[slot][0:KLAST, KT - 1, :], src["ctx"][b, (KT - 1) * P:KEYS, :]).then_inc(s_raw[slot], 16)


def make_rope(nc, sems, ctx, raw, s_raw, cosN, sinN, KVd):
    rope_t = ctx.enter_context(nc.sbuf_tensor("rope_t", [P, 2, 2, DC], F32))
    s_rope = sems("rope")
    s_prod = sems("rope_products")
    H = DC // 2

    def piece(pool, b, bk, u):
        k0, k1 = 2 * u, min(2 * u + 2, KT)
        n = k1 - k0
        r, o = raw[bk % 2], KVd[bk % 4]
        if u == 0:
            pool.wait_ge(s_raw[bk % 2], 32 * (1 + (b - bk % 2) // 2) if isinstance(b, int) else 16 * (b - bk % 2) + 32)
        ta, tb = rope_t[:, 0, 0:n, :], rope_t[:, 1, 0:n, :]
        c, s = cosN[:, k0:k1, :], sinN[:, k0:k1, :]
        pool.tensor_tensor(ta, r[:, k0:k1, :], c, ALU.mult).then_inc(s_prod, 1)
        pool.tensor_tensor(tb[:, :, 0:H], r[:, k0:k1, H:DC], s[:, :, 0:H], ALU.mult).then_inc(s_prod, 1)
        pool.tensor_tensor(tb[:, :, H:DC], r[:, k0:k1, 0:H], s[:, :, H:DC], ALU.mult).then_inc(s_prod, 1)
        pool.wait_ge(s_prod, (b * 7 + u) * 3 + 3)
        for k in range(2):
            last = pool.tensor_tensor(o[:, k0:k1, k, :], ta, tb, ALU.add)
        last.then_inc(s_rope, 1)
        pool.wait_ge(s_rope, b * 7 + u + 1)
    return piece, s_rope


def latent_weight_buffers(nc, ctx):
    sb = lambda n, s: ctx.enter_context(nc.sbuf_tensor("lw_" + n, s, F32))
    return {
        "wqrT": sb("wqr", [RR, HEADS, DCQ]),
        "wkrT": sb("wkr", [RR, HEADS, DC]),
        "wkcqT": sb("wkcq", [DCQ // 2, 2, HEADS, DK]),
        "wq": sb("wq", [DK, HEADS, HID]),
        "wkckv": sb("wkv", [DK, HEADS, DC]),
        "woT": sb("wo", [DK, HEADS, HID]),
    }


def latent_weights(nc, sems, Md, V, w, s_w, rope):
    with ExitStack() as ctx:
        sb = lambda n, s, d=F32: ctx.enter_context(nc.sbuf_tensor("lw_" + n, s, d))
        sem = lambda n: sems("lw_" + n)
        CC = DCQ // 2
        wqr, wkr, wkcq, wq, wkv, wo = (w[n] for n in ("wqrT", "wkrT", "wkcqT", "wq", "wkckv", "woT"))
        t1 = sb("t1", [CC, HEADS, 2, DC])
        t2 = sb("t2", [DK, HEADS, DC])
        psA = [ctx.enter_context(nc.psum_tensor(f"lw_A{i}", [P, BLK], F32)) for i in range(4)]
        psB = [ctx.enter_context(nc.psum_tensor(f"lw_B{i}", [P, BLK], F32)) for i in range(4)]
        s_t1, s_t1s, s_t2, s_t2s, s_m, s_ms, s_v, s_vs, s_ms2 = (
            sem(n) for n in ("t1", "t1s", "t2", "t2s", "m", "ms", "v", "vs", "ms2"))

        with nc.Block() as block:
            @block.tensor
            def _(pe):
                pe.wait_ge(s_w["wqrT"], 16)
                pe.wait_ge(s_w["wkrT"], 16)
                for h in range(HEADS):
                    for cc in range(2):
                        last = pe.matmul(psA[h // 4][0:CC, (h % 4) * 128 + cc * 64:(h % 4) * 128 + cc * 64 + 64],
                                         wqr[:, h, cc * CC:(cc + 1) * CC], wkr[:, h, :], start=True, stop=True)
                    if h % 4 == 3:
                        last.then_inc(s_t1, 1)
                pe.wait_ge(s_w["wkcqT"], 16)
                for h in range(HEADS):
                    if h % 4 == 0:
                        pe.wait_ge(s_t1s, h // 4 + 1)
                    for cc in range(2):
                        last = pe.matmul(psB[h // 8][:, (h % 8) * 64:(h % 8) * 64 + 64],
                                         wkcq[:, cc, h, :], t1[:, h, cc, :], start=(cc == 0), stop=(cc == 1))
                    if h % 8 == 7:
                        last.then_inc(s_t2, 1)
                pe.wait_ge(s_w["wq"], 16)
                for h in range(HEADS):
                    if h % 8 == 0:
                        pe.wait_ge(s_t2s, h // 8 + 1)
                    for c in range(HC):
                        last = pe.matmul(psA[h // 4][:, (h % 4) * 128 + c * 64:(h % 4) * 128 + c * 64 + 64],
                                         wq[:, h, c * P:(c + 1) * P], t2[:, h, :], start=True, stop=True)
                    if h % 4 == 3:
                        last.then_inc(s_m, 1)
                pe.wait_ge(s_w["wkckv"], 16)
                pe.wait_ge(s_w["woT"], 16)
                for pj in range(8):
                    h = 4 * (pj // 2) + pj % 2
                    if pj < 4 and pj % 2 == 0:
                        pe.wait_ge(s_t2s, 2)
                    for k in range(2):
                        hh = h + 2 * k
                        last = pe.matmul(psB[pj // 2][64 * k:64 * k + 64, (pj % 2) * HID:(pj % 2 + 1) * HID],
                                         wkv[:, hh, :], wo[:, hh, :], start=True, stop=True)
                    if pj % 2:
                        last.then_inc(s_v, 1)

            @block.vector
            def _(dve):
                for i in range(4):
                    dve.wait_ge(s_t1, i + 1)
                    dve.tensor_copy(t1[:, 4 * i:4 * i + 4, :, :].rearrange("p h c d -> p (h c d)"),
                                    psA[i][0:CC, :]).then_inc(s_t1s, 1)
                for i in range(2):
                    dve.wait_ge(s_t2, i + 1)
                    dve.tensor_copy(t2[:, 8 * i:8 * i + 8, :].rearrange("p h d -> p (h d)"),
                                    psB[i][:, :]).then_inc(s_t2s, 1)
                for i in range(4):
                    dve.wait_ge(s_m, i + 1)
                    for k in range(2):
                        last = dve.tensor_copy(Md[:, :, 4 * i:4 * i + 4, k, :].rearrange("p c h d -> p h c d"),
                                               psA[i][:, :].rearrange("p (h c d) -> p h c d", h=4, c=2))
                    last.then_inc(s_ms, 1)

            @block.scalar
            def _(act):
                for i in range(4):
                    act.wait_ge(s_v, i + 1)
                    act.activation(V[:, 2 * i:2 * i + 2, :].rearrange("p j o -> p (j o)"),
                                   psB[i][:, :], ACT.Copy).then_inc(s_vs, 1)

            @block.gpsimd
            def _(pool):
                for b in range(2):
                    for u in range(7):
                        rope(pool, b, b, u)


def latent_attention(nc, sems, X, xnT, ident, Md, V, src, raw, s_raw, KVd, rope, s_rope):
    with ExitStack() as ctx:
        sb = lambda n, s, d=F32: ctx.enter_context(nc.sbuf_tensor("la_" + n, s, d))
        sem = lambda n: sems("la_" + n)
        ps = lambda n, w: ctx.enter_context(nc.psum_tensor("la_" + n, [P, w], F32))
        KThi = [sb(f"KThi{i}", [P, KPAD], F32R) for i in range(2)]
        KTlo = [sb(f"KTlo{i}", [P, KPAD], F32R) for i in range(2)]
        Q = [[sb(f"Q{i}{j}", [P, HEADS, SEQ], F32R) for j in range(2)] for i in range(2)]
        Pr = [sb(f"Pr{i}", [P, KEYS]) for i in range(2)]
        PT = [sb(f"PT{i}", [P, KT, 2 * P]) for i in range(2)]
        ctx_all = sb("ctx_all", [P, 8, BATCH, SEQ])
        st = [sb(f"st{i}", [P, 16]) for i in range(2)]
        psA, psB = ps("psA", 2 * BLK), ps("psB", 2 * BLK)
        psT = [ps("psT0", BLK), ps("psT1", BLK)]
        psV = ps("psV", BLK)
        psM = ps("psM", BLK)
        (s_scA, s_scB, s_mxA, s_mxB, s_nB, s_eA, s_eB, s_dch, s_nrm, s_pA, s_pB,
         s_tp, s_evA, s_evD, s_pv, s_ctx, s_msc, s_mhi, s_mlo) = (
            sem(n) for n in ("scA", "scB", "mxA", "mxB", "nB", "eA", "eB", "dch",
                             "nrm", "pA", "pB", "tp", "evA", "evD", "pv", "ctx", "msc", "mhi", "mlo"))
        UNITS = BATCH * UPB
        BODY = 4
        TURNS = BATCH // BODY
        UB = BODY * UPB
        R0 = 8
        RPT = 12

        def misc_round(tu):
            b, u = divmod(tu, UPB)
            if u < 4:
                return 6 * b + u, "K", b + 1, u
            if u < 6:
                return 6 * b + u, "Q", 1, 2 * b + u - 4
            return None

        def groups(g):
            return range(4 * g, min(4 * g + 4, KT))

        def rows(kt):
            return KLAST if kt == KT - 1 else P

        def k_round(pe, slot, g):
            for j, kt in enumerate(groups(g)):
                n = rows(kt)
                last = pe.transpose(psM[:, j * P:j * P + n],
                                    KVd[slot][0:n, kt, :, :].rearrange("p a d -> p (a d)"), ident[0:n, 0:n])
            last.then_inc(s_msc, 1)

        def q_round(pe, tile, g):
            for j in range(4):
                for c in range(HC):
                    last = pe.matmul(psM[:, j * P:(j + 1) * P], Md[:, c, 4 * g + j, :, :].rearrange("p a d -> p (a d)"),
                                     xnT[:, c, bass.ts(tile, P)], start=(c == 0), stop=(c == HC - 1))
            last.then_inc(s_msc, 1)

        def scores(pe, U, ut, free):
            tile, bb, u = ut // 16 % 2, ut // 8 % 2, ut % 8
            q = Q[tile][bb][:, 2 * u:2 * u + 2, :].rearrange("p h s -> p (h s)")
            if free:
                pe.wait_ge(s_eA, U)
            for a, b in ((0, BLK), (BLK, KA)):
                pe.matmul(psA[:, a:b], q, KThi[bb][:, a:b], start=True, stop=False)
                last = pe.matmul(psA[:, a:b], q, KTlo[bb][:, a:b], start=False, stop=True)
            last.then_inc(s_scA, 1)
            if free:
                pe.wait_ge(s_eB, U)
            for a, b in ((KA, KA + BLK), (KA + BLK, KPAD)):
                pe.matmul(psB[:, a - KA:b - KA], q, KThi[bb][:, a:b], start=True, stop=False)
                last = pe.matmul(psB[:, a - KA:b - KA], q, KTlo[bb][:, a:b], start=False, stop=True)
            last.then_inc(s_scB, 1)

        def transposes(pe, U, ut, first):
            p = Pr[ut % 2]
            for g in range(4):
                if g == 0:
                    pe.wait_ge(s_pA, U + 1)
                if g == 1:
                    pe.wait_ge(s_pB, U + 1)
                if g < 2 and not first:
                    pe.wait_ge(s_evD, 2 * U - 1 + g)
                if g >= 2:
                    pe.wait_ge(s_evA, 2 * U + 1 + (g - 2))
                for j, kt in enumerate(groups(g)):
                    n = rows(kt)
                    last = pe.transpose(psT[g % 2][0:n, j * P:(j + 1) * P], p[:, kt * P:kt * P + n], ident[:, :])
                last.then_inc(s_tp, 1)

        def values(pe, pair, slot, kslot, part, first):
            if part == 0:
                pe.wait_ge(s_evA, 4 * pair + 4)
                pe.wait_ge(s_evD, 4 * pair + 4)
                if not first:
                    pe.wait_ge(s_ctx, pair)
            for kt in (range(0, 7) if part == 0 else range(7, KT)):
                n = rows(kt)
                for k in range(2):
                    last = pe.matmul(psV[64 * k:64 * k + 64, 0:P], KVd[kslot][0:n, kt, 0, :],
                                     PT[slot][0:n, kt, k * P:(k + 1) * P], start=(kt == 0), stop=(kt == KT - 1))
            if part == 1:
                last.then_inc(s_pv, 1)

        with nc.Block() as block:
            @block.sync
            def _(sp):
                def turn(i, n):
                    for k in range(n):
                        sp.wait_ge(s_rope, (i * BODY + k + 1) * 7)
                        load_latents(sp, src, raw, s_raw, i * BODY + k + 2, k % 2)
                with sp.Fori(0, TURNS - 1) as i:
                    turn(i, BODY)
                turn(TURNS - 1, BODY - 2)

            @block.gpsimd
            def _(pool):
                def turn(i, ropes):
                    for ut in range(UB):
                        U = i * UB + ut
                        pool.wait_ge(s_nrm, U + 1)
                        a = Pr[ut % 2][:, 0:KA]
                        pool.tensor_tensor(a, a, st[ut % 2][:, 8:9].broadcast_to([P, KA]), ALU.mult).then_inc(s_pA, 1)
                        if ut % UPB < 7 and ut // UPB < ropes:
                            rope(pool, i * BODY + ut // UPB + 2, ut // UPB + 2, ut % UPB)
                with pool.Fori(0, TURNS - 1) as i:
                    turn(i, BODY)
                turn(TURNS - 1, BODY - 2)

            @block.tensor
            def _(pe):
                for g in range(4):
                    if g > 0:
                        pe.wait_ge(s_mlo, g)
                    pe.wait_ge(s_rope, min(2 * (g + 1), 7))
                    k_round(pe, 0, g)
                for g in range(4):
                    pe.wait_ge(s_mlo, 4 + g)
                    q_round(pe, 0, g)
                pe.wait_ge(s_mlo, R0)
                scores(pe, 0, 0, False)

                def step(i, ut, first, last):
                    U = i * UB + ut
                    tile = i * 2 + ut // 16
                    r = misc_round(ut % 16)
                    is_end = last and ut >= UB - 16
                    if r is not None:
                        m, kind, off, g = r
                        if not (last and ((kind == "Q" and ut >= UB - 16) or (kind == "K" and ut >= UB - UPB))):
                            M = R0 + tile * RPT + m
                            pe.wait_ge(s_mlo, M)
                            if kind == "K":
                                b = tile * 2 + off
                                if g == 0:
                                    pe.wait_ge(s_rope, (b + 1) * 7)
                                k_round(pe, (ut // UPB + 1) % 4, g)
                            else:
                                q_round(pe, tile + 1, g)
                    if not (last and ut == UB - 1):
                        if ut % UPB == UPB - 1:
                            pe.wait_ge(s_mlo, R0 + tile * RPT + (4 if is_end else 6 if ut % 16 == 7 else 12))
                        scores(pe, U + 1, (ut + 1) % UB, True)
                    if not (first and ut < 2):
                        pair = i * (UB // 2) + ut // 2 - 1
                        pb = (ut // 2 - 1) % (UB // 2)
                        values(pe, pair, pb % 2, pb // 4 % 4, ut % 2, first and ut // 2 == 1)
                    transposes(pe, U, ut, first and ut == 0)

                for ut in range(UB):
                    step(0, ut, True, False)
                with pe.Fori(1, TURNS - 1) as i:
                    for ut in range(UB):
                        step(i, ut, False, False)
                for ut in range(UB):
                    step(TURNS - 1, ut, False, True)
                last_pair = UNITS // 2 - 1
                for part in range(2):
                    values(pe, last_pair, last_pair % 2, (UB // 2 - 1) // 4 % 4, part, False)

            @block.scalar
            def _(act):
                def misc(M, kind, slot, g):
                    act.wait_ge(s_msc, M + 1)
                    if kind == "K":
                        a, b = g * BLK, min(g * BLK + BLK, KEYS)
                        act.activation(KThi[slot][:, a:b], psM[:, 0:b - a], ACT.Copy).then_inc(s_mhi, 1)
                    else:
                        for b in range(2):
                            last = act.activation(Q[slot][b][:, 4 * g:4 * g + 4, :],
                                                  psM[:, :].rearrange("p (h b s) -> p h b s", h=4, b=2)[:, :, b, :],
                                                  ACT.Copy)
                        last.then_inc(s_mhi, 1)

                for g in range(4):
                    misc(g, "K", 0, g)
                for g in range(4):
                    misc(4 + g, "Q", 0, g)

                def exps(U, ut, first):
                    s, p = st[ut % 2], Pr[ut % 2]
                    act.wait_ge(s_mxA, U + 1)
                    if not (first and ut < 2):
                        act.wait_ge(s_tp, 4 * U - 4)
                    act.activation(p[:, 0:KA], psA[:, 0:KA], ACT.Exp, bias=s[:, 0:1],
                                   accum_out=s[:, 3:4]).then_inc(s_eA, 1)
                    act.wait_ge(s_mxB, U + 1)
                    act.activation(s[:, 4:5], s[:, 0:1], ACT.Exp, bias=s[:, 2:3], scale=-1.0)
                    act.activation(p[:, KA:KEYS], psB[:, 0:KB], ACT.Exp, bias=s[:, 2:3],
                                   accum_out=s[:, 5:6]).then_inc(s_eB, 1)

                def evac(U, ut, i, first):
                    slot = PT[ut // 2 % 2]
                    if not (first and ut < 4) and ut % 2 == 0:
                        act.wait_ge(s_pv, i * (UB // 2) + ut // 2 - 1)
                    for g in range(2):
                        act.wait_ge(s_tp, 4 * U + g + 1)
                        act.activation(slot[:, 4 * g:4 * g + 4, (ut % 2) * P:(ut % 2 + 1) * P],
                                       psT[g][:, :].rearrange("p (t q) -> p t q", t=4), ACT.Copy).then_inc(s_evA, 1)

                def turn(i, first, last):
                    for ut in range(UB):
                        U = i * UB + ut
                        tile = i * 2 + ut // 16
                        r = misc_round(ut % 16)
                        exps(U, ut, first)
                        if r is not None:
                            m, kind, off, g = r
                            if not (last and ((kind == "Q" and ut >= UB - 16) or (kind == "K" and ut >= UB - UPB))):
                                slot = (ut // UPB + 1) % 2 if kind == "K" else (ut // 16 + 1) % 2
                                misc(R0 + tile * RPT + m, kind, slot, g)
                        evac(U, ut, i, first)
                turn(0, True, False)
                with act.Fori(1, TURNS - 1) as i:
                    turn(i, False, False)
                turn(TURNS - 1, False, True)

            @block.vector
            def _(dve):
                for t in range(2):
                    dve.memset(KThi[t][:, KEYS:KPAD].bitcast(F32), 0.0)
                    dve.memset(KTlo[t][:, KEYS:KPAD].bitcast(F32), 0.0)

                def misc(M, kind, slot, g):
                    dve.wait_ge(s_mhi, M + 1)
                    if kind == "K":
                        a, b = g * BLK, min(g * BLK + BLK, KEYS)
                        dve.tensor_tensor(KTlo[slot][:, a:b], psM[:, 0:b - a], KThi[slot][:, a:b].bitcast(F32),
                                          ALU.subtract).then_inc(s_mlo, 1)
                    else:
                        for b in range(2):
                            q = Q[slot][b][64:P, 4 * g:4 * g + 4, :]
                            last = dve.tensor_tensor(
                                q, psM[64:P, :].rearrange("p (h b s) -> p h b s", h=4, b=2)[:, :, b, :],
                                q.bitcast(F32), ALU.subtract)
                        last.then_inc(s_mlo, 1)

                for g in range(4):
                    misc(g, "K", 0, g)
                for g in range(4):
                    misc(4 + g, "Q", 0, g)

                def maxima(U, ut):
                    s = st[ut % 2]
                    dve.wait_ge(s_scA, U + 1)
                    dve.tensor_reduce(s[:, 0:1], psA[:, 0:KA], AX.X, ALU.max, negate=True).then_inc(s_mxA, 1)
                    dve.wait_ge(s_scB, U + 1)
                    dve.tensor_reduce(s[:, 1:2], psB[:, 0:KB], AX.X, ALU.max, negate=True).then_inc(s_nB, 1)
                    dve.wait_ge(s_nB, U + 1)
                    dve.tensor_tensor(s[:, 2:3], s[:, 0:1], s[:, 1:2], ALU.min).then_inc(s_mxB, 1)

                def norm(U, ut):
                    s = st[ut % 2]
                    dve.wait_ge(s_eB, U + 1)
                    dve.scalar_tensor_tensor(s[:, 6:7], s[:, 3:4], s[:, 4:5], s[:, 5:6],
                                             ALU.mult, ALU.add).then_inc(s_dch, 1)
                    dve.wait_ge(s_dch, 2 * U + 1)
                    dve.reciprocal(s[:, 7:8], s[:, 6:7]).then_inc(s_dch, 1)
                    dve.wait_ge(s_dch, 2 * U + 2)
                    dve.tensor_tensor(s[:, 8:9], s[:, 7:8], s[:, 4:5], ALU.mult).then_inc(s_nrm, 1)
                    p = Pr[ut % 2][:, KA:KEYS]
                    dve.tensor_scalar(p, p, s[:, 7:8], None, ALU.mult).then_inc(s_pB, 1)

                def evac(U, ut, i, first):
                    slot = PT[ut // 2 % 2]
                    if not (first and ut < 4) and ut % 2 == 0:
                        dve.wait_ge(s_pv, i * (UB // 2) + ut // 2 - 1)
                    dve.wait_ge(s_tp, 4 * U + 3)
                    dve.tensor_copy(slot[:, 8:12, (ut % 2) * P:(ut % 2 + 1) * P],
                                    psT[0][:, :].rearrange("p (t q) -> p t q", t=4)).then_inc(s_evD, 1)
                    dve.wait_ge(s_tp, 4 * U + 4)
                    dve.tensor_copy(slot[0:KLAST, 12, (ut % 2) * P:(ut % 2 + 1) * P],
                                    psT[1][0:KLAST, 0:P]).then_inc(s_evD, 1)

                def ctx_out(pair, b, pj):
                    dve.wait_ge(s_pv, pair + 1)
                    dve.tensor_copy(ctx_all[:, 2 * pj:2 * pj + 2, bass.ds(b, 1), :].rearrange("p j b s -> p j (b s)"),
                                    psV[:, 0:P].rearrange("p (j s) -> p j s", j=2)).then_inc(s_ctx, 1)

                maxima(0, 0)

                def turn(i, first, last):
                    for ut in range(UB):
                        U = i * UB + ut
                        tile = i * 2 + ut // 16
                        r = misc_round(ut % 16)
                        norm(U, ut)
                        if r is not None:
                            m, kind, off, g = r
                            if not (last and ((kind == "Q" and ut >= UB - 16) or (kind == "K" and ut >= UB - UPB))):
                                slot = (ut // UPB + 1) % 2 if kind == "K" else (ut // 16 + 1) % 2
                                misc(R0 + tile * RPT + m, kind, slot, g)
                        if not (last and ut == UB - 1):
                            maxima(U + 1, ut + 1)
                        if ut % 2 == 1 and not (first and ut == 1):
                            lp = (ut // 2 - 1) % (UB // 2)
                            ctx_out(i * (UB // 2) + ut // 2 - 1, i * BODY + ut // UPB if ut // 2 % 4 else
                                    i * BODY + ut // UPB - 1, lp % 4)
                        evac(U, ut, i, first)
                turn(0, True, False)
                with dve.Fori(1, TURNS - 1) as i:
                    turn(i, False, False)
                turn(TURNS - 1, False, True)
                ctx_out(UNITS // 2 - 1, BATCH - 1, 3)

        s_o, s_x = sem("o"), sem("x")
        psO = [psA, psB]
        with nc.Block() as block:
            @block.tensor
            def _(pe):
                for t in range(TILES):
                    if t >= 2:
                        pe.wait_ge(s_x, t - 1)
                    for pj in range(8):
                        last = pe.matmul(psO[t % 2][:, 0:HID],
                                         ctx_all[:, pj, 2 * t:2 * t + 2, :].rearrange("p b s -> p (b s)"),
                                         V[:, pj, :], start=(pj == 0), stop=(pj == 7))
                    last.then_inc(s_o, 1)

            @block.vector
            def _(dve):
                for t in range(TILES):
                    dve.wait_ge(s_o, t + 1)
                    dve.tensor_tensor(X[:, t, :], X[:, t, :], psO[t % 2][:, 0:HID], ALU.add).then_inc(s_x, 1)
def head_attention(nc, sems, name, X, qin, ident, wq, s_w, mask_value, keys, values, out_w):
    shared = values is None
    with ExitStack() as ctx:
        sb = lambda n, s, d=F32: ctx.enter_context(nc.sbuf_tensor(f"{name}_{n}", s, d))
        sem = lambda n: sems(f"{name}_{n}")
        ps = lambda n: ctx.enter_context(nc.psum_tensor(f"{name}_{n}", [P, BLK], F32))
        HPC = HEADS // HC
        PAIRS = HEADS // 2
        scale = 1.0 / float(DH) ** 0.5
        wk, kin, wv = keys
        kdim = kin.shape[0]
        qT = sb("qT", [P, HC, TOK])
        kT = sb("kT", [P, HC, TOK])
        kblk = sb("kblk", [P, HC, BATCH, HPC, SEQ])
        headmask = sb("headmask", [P, HPC])
        identb = sb("identb", [P, P], BF16)
        causal = sb("causal", [P, HPC, SEQ], BF16)
        D = [sb(f"D{i}", [P, HEADS, SEQ]) for i in range(2)]
        E = [sb(f"E{i}", [P, HEADS, SEQ]) for i in range(2)]
        mx, sm, rs = (sb(n, [P, HEADS]) for n in ("mx", "sm", "rs"))
        if shared:
            v = sb("v", [P, TILES, HID])
            pbar = sb("pbar", [P, 2, SEQ])
            pbT = sb("pbT", [P, P])
            blockmask = sb("blockmask", [P, P])
        else:
            vblk = sb("vblk", [P, BATCH, PAIRS, 2, DH])
            AT = sb("AT", [P, PAIRS, P])
            Os = sb("Os", [P, HID])
        scratch = sb("scratch", [P, 1])
        oT = sb("oT", [P, HC, P])
        psP = [ps("psP0"), ps("psP1")]
        psS = [[ps(f"psS{i}{c}") for c in range(HC)] for i in range(2)]
        psT = [ps("psT0"), ps("psT1")]
        s_pool, s_c2, s_z, s_p, s_pe, s_kb, s_kbp, s_s, s_dch, s_D, s_E, s_rs, s_En, s_free = (
            sem(n) for n in ("pool", "c2", "z", "p", "pe", "kb", "kbp", "s", "dch", "D", "E", "rs", "En", "free"))
        s_a, s_ae, s_b, s_be, s_o, s_oe, s_f, s_fe = (sem(n) for n in ("a", "ae", "b", "be", "o", "oe", "f", "fe"))
        s_D2 = sem("D2")
        NV = TILES if shared else BATCH // 2

        def steps(T):
            return [(k, T - k) for k in range(5) if 0 <= T - k < TILES]

        with nc.Block() as block:
            @block.gpsimd
            def _(pool):
                link = chain(pool, s_pool)
                link(pool.memset(headmask[:, :], 1.0))
                link(pool.memset(causal[:, :, :], 0.0))
                if shared:
                    link(pool.memset(blockmask[:, :], 0.0))
                    for k in range(2):
                        link(pool.memset(blockmask[64 * k:64 * k + 64, 64 * k:64 * k + 64], 1.0))
                else:
                    pool.memset(vblk[:, :, :, :, :], 0.0).then_inc(s_z, 1)
                link(pool.affine_select(out=headmask[:, :], in_=headmask[:, :], compare_op=ALU.is_ge, fill=0.0,
                                        base=0, pattern=[[-DH, HPC]], channel_multiplier=1))
                link(pool.affine_select(out=headmask[:, :], in_=headmask[:, :], compare_op=ALU.is_ge, fill=0.0,
                                        base=DH - 1, pattern=[[DH, HPC]], channel_multiplier=-1))
                for k in range(2):
                    link(pool.affine_select(out=causal[64 * k:64 * k + 64], in_=causal[64 * k:64 * k + 64],
                                            compare_op=ALU.is_ge, fill=mask_value, base=0,
                                            pattern=[[0, HPC], [-1, SEQ]], channel_multiplier=1))
                pool.memset(scratch[:, :], 0.0).then_inc(s_c2, 1)
                for blk in range(2):
                    pool.wait_ge(s_pe, 4 + 2 * (blk + 1))
                    for b in range(8 * blk + 1, 8 * blk + 8, 2):
                        for c in range(HC):
                            last = pool.tensor_tensor(
                                kblk[:, c, b, :, :],
                                kT[:, c, b * SEQ:(b + 1) * SEQ].unsqueeze(1).broadcast_to([P, HPC, SEQ]),
                                headmask[:, :].unsqueeze(2).broadcast_to([P, HPC, SEQ]), ALU.mult)
                        last.then_inc(s_kbp, 1)
                for T in range(TILES):
                    pool.wait_ge(s_rs, T + 1)
                    e = E[T % 2]
                    pool.tensor_tensor(e[:, :, :], e[:, :, :], rs[:, :].unsqueeze(2).broadcast_to([P, HEADS, SEQ]),
                                       ALU.mult).then_inc(s_En, 1)

            @block.tensor
            def _(pe):
                n = 0

                def bank():
                    if n >= 2:
                        pe.wait_ge(s_pe, n - 1)
                    return psP[n % 2]
                for s in s_w:
                    pe.wait_ge(s, 16)
                for w, rhs, kk in ((wq, qin, P), (wk, kin, kdim)):
                    for blk in range(2):
                        for oc in range(HC):
                            o = bank()
                            ics = range(HC) if kk == P else range(1)
                            for ic in ics:
                                m = rhs[:, ic, blk * BLK:(blk + 1) * BLK] if kk == P else rhs[:, blk * BLK:(blk + 1) * BLK]
                                l = w[:, ic, oc * P:(oc + 1) * P] if kk == P else w[:, oc * P:(oc + 1) * P]
                                last = pe.matmul(o[:, :], l, m, start=(ic == 0), stop=(ic == ics[-1]))
                            last.then_inc(s_p, 1)
                            n += 1
                for g in range(NV):
                    o = bank()
                    if shared:
                        for ic in range(HC):
                            last = pe.matmul(o[:, 0:HID], qin[:, ic, g * P:(g + 1) * P], wv[:, ic, :],
                                             start=(ic == 0), stop=(ic == HC - 1))
                    else:
                        for k in range(4):
                            bb, half = k // 2, k % 2
                            b = 2 * g + bb
                            last = pe.matmul(o[64 * half:64 * half + 64, bb * HID:(bb + 1) * HID],
                                             kin[:, b * SEQ:(b + 1) * SEQ], wv[:, :], start=True, stop=True)
                    last.then_inc(s_p, 1)
                    n += 1
                pe.wait_ge(s_pe, n)
                pe.wait_ge(s_c2, 1)
                pe.wait_ge(s_z, 1 if shared else 2)

                def tail(k, T):
                    if k == 1 and shared:
                        pe.wait_ge(s_a, T + 1)
                        if T:
                            pe.wait_ge(s_ae, T)
                        pe.transpose(psT[0][:, 0:P], pbar[:, :, :].rearrange("p a k -> p (a k)"),
                                     ident[:, :]).then_inc(s_b, 1)
                    elif k == 1:
                        pe.wait_ge(s_En, T + 1)
                        for g in range(2):
                            if T:
                                pe.wait_ge(s_ae, 2 * T - 1 + g)
                            for j in range(4):
                                last = pe.transpose(psT[g][:, j * P:(j + 1) * P],
                                                    E[T % 2][:, 8 * g + 2 * j:8 * g + 2 * j + 2, :].rearrange(
                                                        "p h k -> p (h k)"), ident[:, :])
                            last.then_inc(s_b, 1)
                    elif k == 2 and shared:
                        pe.wait_ge(s_ae, T + 1)
                        if T:
                            pe.wait_ge(s_oe, T)
                        for c in range(HC):
                            last = pe.matmul(psT[1][:, c * P:(c + 1) * P], v[:, T, c * P:(c + 1) * P], pbT[:, :],
                                             start=True, stop=True)
                        last.then_inc(s_o, 1)
                    elif k == 2:
                        pe.wait_ge(s_ae, 2 * T + 2)
                        if T:
                            pe.wait_ge(s_o, T)
                        if T >= 2:
                            pe.wait_ge(s_fe, T - 1)
                        for p in range(PAIRS):
                            for bb in range(2):
                                last = pe.matmul(psP[0][64 * bb:64 * bb + 64, 32 * p:32 * p + 32],
                                                 AT[:, p, 64 * bb:64 * bb + 64],
                                                 vblk[:, 2 * T + bb, p, :, :].rearrange("p a d -> p (a d)"),
                                                 start=True, stop=True)
                        last.then_inc(s_be, 1)
                    elif k == 3 and not shared:
                        pe.wait_ge(s_o, T + 1)
                        if T:
                            pe.wait_ge(s_oe, T)
                        for c in range(HC):
                            last = pe.transpose(psP[1][:, c * P:(c + 1) * P], Os[:, c * P:(c + 1) * P], ident[:, :])
                        last.then_inc(s_D2, 1)
                        pe.wait_ge(s_oe, T + 1)
                        pe.wait_ge(s_o, min(T + 2, TILES))
                        if T:
                            pe.wait_ge(s_fe, T)
                        for c in range(HC):
                            last = pe.matmul(psP[0][:, HID:2 * HID], oT[:, c, :], out_w[:, c, :],
                                             start=(c == 0), stop=(c == HC - 1))
                        last.then_inc(s_f, 1)
                    elif k == 3:
                        pe.wait_ge(s_oe, T + 1)
                        if T:
                            pe.wait_ge(s_fe, T)
                        for c in range(HC):
                            last = pe.matmul(psP[0][:, 0:HID], oT[:, c, :], out_w[:, c, :],
                                             start=(c == 0), stop=(c == HC - 1))
                        last.then_inc(s_f, 1)

                for step in range(TILES + 4):
                    for k, T in steps(step):
                        if k == 0:
                            pe.wait_ge(s_kb, T + 1)
                            pe.wait_ge(s_kbp, T + 1)
                            if T >= 2:
                                pe.wait_ge(s_D, T - 1)
                            for c in range(HC):
                                for bb in range(2):
                                    pe.matmul(psS[T % 2][c][64 * bb:64 * bb + 64, :], identb[:, 64 * bb:64 * bb + 64],
                                              causal[:, :, :].rearrange("p h k -> p (h k)"), start=True, stop=False)
                                for bb in range(2):
                                    b = 2 * T + bb
                                    last = pe.matmul(psS[T % 2][c][64 * bb:64 * bb + 64, :],
                                                     qT[:, c, b * SEQ:(b + 1) * SEQ],
                                                     kblk[:, c, b, :, :].rearrange("p h k -> p (h k)"),
                                                     start=False, stop=True)
                            last.then_inc(s_s, 1)
                        else:
                            tail(k, T)

            @block.scalar
            def _(act):
                n = 0
                for dst in (qT, kT):
                    for blk in range(2):
                        for oc in range(HC):
                            act.wait_ge(s_p, n + 1)
                            act.activation(dst[:, oc, blk * BLK:(blk + 1) * BLK], psP[n % 2][:, :],
                                           ACT.Copy).then_inc(s_pe, 1)
                            n += 1
                if not shared:
                    act.wait_ge(s_z, 2)
                for g in range(NV):
                    act.wait_ge(s_p, n + 1)
                    if shared:
                        act.activation(v[:, g, :], psP[n % 2][:, 0:HID], ACT.Copy).then_inc(s_pe, 1)
                    else:
                        for half in range(2):
                            src_ = psP[n % 2][64 * half:64 * half + 64, :].rearrange(
                                "p (b j a d) -> p b j a d", b=2, j=PAIRS, a=2)
                            for bb in range(2):
                                last = act.activation(vblk[64 * half:64 * half + 64, 2 * g + bb, :, half, :],
                                                      src_[:, bb, :, half, :], ACT.Copy)
                        last.then_inc(s_pe, 1)
                    n += 1

                for step in range(TILES + 4):
                    for k, T in steps(step):
                        if k == 0:
                            act.wait_ge(s_D, T + 1)
                            if T >= 2:
                                if shared:
                                    act.wait_ge(s_a, T - 1)
                                else:
                                    act.wait_ge(s_b, 2 * T - 2)
                            act.activation(E[T % 2][:, :, :], D[T % 2][:, :, :], ACT.Exp, scale=scale).then_inc(s_E, 1)
                        elif k == 1 and not shared:
                            if T:
                                act.wait_ge(s_be, T)
                            for g in range(2):
                                act.wait_ge(s_b, 2 * T + g + 1)
                                act.activation(AT[:, 4 * g:4 * g + 4, :].rearrange("p j q -> p (j q)"), psT[g][:, :],
                                               ACT.Copy).then_inc(s_ae, 1)
                        elif k == 2 and shared:
                            act.wait_ge(s_o, T + 1)
                            if T:
                                act.wait_ge(s_f, T)
                            act.activation(oT[:, :, :].rearrange("p c t -> p (c t)"), psT[1][:, 0:HID],
                                           ACT.Copy).then_inc(s_oe, 1)
                        elif k == 2:
                            act.wait_ge(s_be, T + 1)
                            if T:
                                act.wait_ge(s_D2, T)
                            act.activation(Os[:, :], psP[0][:, 0:HID], ACT.Copy).then_inc(s_o, 1)

            @block.vector
            def _(dve):
                link = chain(dve, s_dch)
                dve.tensor_copy(identb[:, :], ident[:, :]).then_inc(s_z, 1)
                dve.wait_ge(s_c2, 1)
                for blk in range(2):
                    dve.wait_ge(s_pe, 4 + 2 * (blk + 1))
                    for b in range(8 * blk, 8 * blk + 8, 2):
                        for c in range(HC):
                            last = dve.tensor_tensor(
                                kblk[:, c, b, :, :],
                                kT[:, c, b * SEQ:(b + 1) * SEQ].unsqueeze(1).broadcast_to([P, HPC, SEQ]),
                                headmask[:, :].unsqueeze(2).broadcast_to([P, HPC, SEQ]), ALU.mult)
                        last.then_inc(s_kb, 1)

                for step in range(TILES + 4):
                    for k, T in steps(step):
                        if k == 0:
                            s3 = [psS[T % 2][c][:, :].rearrange("p (h k) -> p h k", h=HPC) for c in range(HC)]
                            dve.wait_ge(s_s, T + 1)
                            for c in range(HC):
                                last = dve.tensor_reduce(mx[:, c * HPC:(c + 1) * HPC], s3[c], AX.X, ALU.max)
                            link(last)
                            if T >= 2:
                                dve.wait_ge(s_E, T - 1)
                            for c in range(HC):
                                last = dve.tensor_tensor(D[T % 2][:, c * HPC:(c + 1) * HPC, :], s3[c],
                                                         mx[:, c * HPC:(c + 1) * HPC].unsqueeze(2).broadcast_to(
                                                             [P, HPC, SEQ]), ALU.subtract)
                            last.then_inc(s_D, 1)
                        if k == 1:
                            if shared:
                                dve.wait_ge(s_En, T + 1)
                                if T:
                                    dve.wait_ge(s_b, T)
                                for a in range(2):
                                    last = dve.tensor_reduce(pbar[:, a, :], E[T % 2][:, :, :].rearrange("p h k -> p k h"),
                                                             AX.X, ALU.add) if a == 0 else \
                                        dve.tensor_copy(pbar[:, 1, :], pbar[:, 0, :])
                                    if a == 0:
                                        link(last)
                                last.then_inc(s_a, 1)
                                dve.wait_ge(s_b, T + 1)
                                if T:
                                    dve.wait_ge(s_o, T)
                                dve.tensor_tensor(pbT[:, :], psT[0][:, 0:P], blockmask[:, :], ALU.mult).then_inc(s_ae, 1)
                        if k == 3:
                            if not shared:
                                dve.wait_ge(s_D2, T + 1)
                                if T:
                                    dve.wait_ge(s_f, T)
                                dve.tensor_copy(oT[:, :, :].rearrange("p c t -> p (c t)"),
                                                psP[1][:, 0:HID]).then_inc(s_oe, 1)
                            dve.wait_ge(s_f, T + 1)
                            o = psP[0][:, 0:HID] if shared else psP[0][:, HID:2 * HID]
                            dve.tensor_tensor(X[:, T, :], X[:, T, :], o, ALU.add).then_inc(s_fe, 1)
                        if k == 0:
                            dve.wait_ge(s_E, T + 1)
                            link(dve.tensor_reduce(sm[:, :], E[T % 2][:, :, :], AX.X, ALU.add))
                            if T:
                                dve.wait_ge(s_En, T)
                            dve.reciprocal(rs[:, :], sm[:, :]).then_inc(s_rs, 1)


def experts(nc, sems, name, X, xhi, xlo, ident, stream, router, E, K, NT, gated, out=None, s_out=None):
    with ExitStack() as ctx:
        sb = lambda n, s, d=F32: ctx.enter_context(nc.sbuf_tensor(f"{name}_{n}", s, d))
        sem = lambda n: sems(f"{name}_{n}")
        ps = lambda n: ctx.enter_context(nc.psum_tensor(f"{name}_{n}", [P, BLK], F32))
        EW = router.shape[-1]
        SW = 6 * P
        WW = SW + P
        Wraw = [sb(f"Wraw{i}", [P, WW]) for i in range(2)]
        Whi = [sb(f"Whi{i}", [P, WW], F32R) for i in range(2)]
        Wlo = [sb(f"Wlo{i}", [P, SW], F32R) for i in range(2)]
        rw = sb("rw", [P, HC, EW])
        rhi, rlo = sb("rhi", [P, HC, EW], F32R), sb("rlo", [P, HC, EW], F32R)
        L = sb("L", [P, TILES, EW])
        m8 = sb("m8", [P, TILES, 8])
        gt, eq, cum, rst, ex = (sb(n, [P, TILES, E]) for n in ("gt", "eq", "cum", "rst", "ex"))
        need, ssum, rsum, sg = (sb(n, [P, TILES]) for n in ("need", "ssum", "rsum", "sg"))
        cmb = [sb(f"cmb{i}", [P, TILES, P]) for i in range(2 if gated else 1)]
        cT = [sb(f"cT{i}", [P, TOK], F32R) for i in range(2 if gated else 1)]
        a = [sb(f"a{i}", [P, BLK]) for i in range(2)]
        t = sb("t", [P, BLK])
        h = [sb(f"h{i}", [P, BLK]) for i in range(2)]
        hhi = [sb(f"hhi{i}", [P, BLK], F32R) for i in range(2)]
        hlo = [sb(f"hlo{i}", [P, BLK], F32R) for i in range(2)]
        yT = sb("yT", [P, HC, TOK])
        acc = [[ps(f"acc{o}{b}") for b in range(2)] for o in range(HC)]
        psG = [ps("psG0"), ps("psG1")]
        psU, psC = ps("psU"), ps("psC")
        s_wr = [sem(f"wr{i}") for i in range(2)]
        (s_r, s_rs, s_l, s_le, s_dch, s_z, s_e, s_c, s_ct, s_cte, s_whi, s_wlo, s_g, s_u, s_cc, s_a, s_t, s_h, s_hhi,
         s_hlo, s_d, s_y, s_ye, s_yv, s_tr, s_x) = (
            sem(n) for n in ("r", "rs", "l", "le", "dch", "z", "e", "c", "ct", "cte", "whi", "wlo", "g", "u", "cc",
                             "a", "t", "h", "hhi", "hlo", "d", "y", "ye", "yv", "tr", "x"))
        NC = len(cT)
        LAST = NT - 1

        def tiles(eng, body):
            for j in range(3):
                body(j, j % 2)
            with eng.Fori(1, (NT - 3) // 2) as i:
                body(2 * i + 1, 1)
                body(2 * i + 2, 0)
            body(LAST - 1, 1)
            body(LAST, 0)

        with nc.Block() as block:
            @block.sync
            def _(sp):
                sp.dma_start(rw[:], router).then_inc(s_r, 16)

                def load(j, slot):
                    if not isinstance(j, int) or j >= 2:
                        sp.wait_ge(s_wlo, j - 1)
                    sp.dma_start(Wraw[slot][:, :], stream[j]).then_inc(s_wr[slot], 16)
                tiles(sp, load)
                if out is not None:
                    view = out.rearrange("(t p) h -> p t h", p=P)
                    for T in range(TILES):
                        sp.wait_ge(s_x, T + 1)
                        sp.dma_start(view[:, T, :], X[:, T, :]).then_inc(s_out, 16)
                    sp.wait_ge(s_out, 16 * TILES)

            @block.gpsimd
            def _(pool):
                pool.memset(rst[:, :, :], 1.0).then_inc(s_z, 1)
                for c in cmb:
                    pool.memset(c[:, :, :], 0.0).then_inc(s_z, 1)
                pool.wait_ge(s_z, 1 + NC)
                pool.memset(rst[:, :, 0:1], 0.0).then_inc(s_z, 1)
                if not gated:
                    pool.memset(cmb[0][:, :, E:E + 1], 1.0).then_inc(s_z, 1)

                def split_lo(j, slot):
                    pool.wait_ge(s_whi, j + 1)
                    pool.tensor_tensor(Wlo[slot][:, :], Wraw[slot][:, 0:SW], Whi[slot][:, 0:SW].bitcast(F32),
                                       ALU.subtract).then_inc(s_wlo, 1)

                def tile(j, slot):
                    for blk in range(2):
                        r = 2 * j + blk
                        pool.wait_ge(s_hhi, r + 1)
                        pool.tensor_tensor(hlo[blk][:, :], h[blk][:, :], hhi[blk][:, :].bitcast(F32),
                                           ALU.subtract).then_inc(s_hlo, 1)
                        if blk == 0 and not (isinstance(j, int) and j == LAST):
                            split_lo(j + 1, 1 - slot)
                split_lo(0, 0)
                tiles(pool, tile)

            @block.tensor
            def _(pe):
                pe.wait_ge(s_rs, 1)
                for T in range(TILES):
                    o = psG[T // 4][:, (T % 4) * EW:(T % 4 + 1) * EW]
                    n = 0
                    for c in range(HC):
                        for x, w in ((xhi, rhi), (xhi, rlo), (xlo, rhi)):
                            last = pe.matmul(o, x[:, c, T * P:(T + 1) * P], w[:, c, :], start=(n == 0), stop=(n == 5))
                            n += 1
                    if T % 4 == 3:
                        last.then_inc(s_l, 1)
                pe.wait_ge(s_c, 1)
                banks = [psU, psC, psG[0], psG[1]]
                for k in range(NC):
                    for half in range(2):
                        for q in range(4):
                            last = pe.transpose(banks[2 * k + half][:, q * P:(q + 1) * P], cmb[k][:, 4 * half + q, :],
                                                ident[:, :])
                        last.then_inc(s_ct, 1)
                pe.wait_ge(s_cte, 2 * NC)

                def product3(o, whi, wlo, cols, xh, xl, start, stop, n0, n1):
                    n = n0
                    for (w, x) in ((whi, xh), (whi, xl), (wlo, xh)):
                        last = pe.matmul(o, w[:, cols], x, start=start and n == 0, stop=stop and n == n1)
                        n += 1
                    return last

                def down(r_done, slot, blk, first, final):
                    pe.wait_ge(s_hlo, r_done)
                    for oc in range(HC):
                        cols = slice(4 * P + oc * P, 5 * P + oc * P)
                        last = product3(acc[oc][blk][:, :], Whi[slot], Wlo[slot], cols, hhi[blk][:, :], hlo[blk][:, :],
                                        first, final, 0, 2)
                    last.then_inc(s_d, 1)

                def tile(j, slot):
                    const = isinstance(j, int)
                    for blk in range(2):
                        r = 2 * j + blk
                        tok = slice(blk * BLK, blk * BLK + BLK)
                        if blk == 0:
                            pe.wait_ge(s_wlo, j + 1)
                        if not (const and r < 2):
                            pe.wait_ge(s_a, r - 1)
                        for k, (o, s) in enumerate(((psG[blk], s_g), (psU, s_u))):
                            if k == 1 and not (const and r == 0):
                                pe.wait_ge(s_t, r)
                            for c in range(HC):
                                cols = slice((2 * k + c) * P, (2 * k + c + 1) * P)
                                last = product3(o[:, :], Whi[slot], Wlo[slot], cols, xhi[:, c, tok], xlo[:, c, tok],
                                                True, True, 3 * c, 5)
                            last.then_inc(s, 1)
                        if not (const and r == 0):
                            pe.wait_ge(s_h, r)
                        which = cT[1] if gated and const and j == LAST else cT[0]
                        pe.matmul(psC[:, :], Whi[slot][:, SW:WW], which[:, tok], start=True, stop=True).then_inc(s_cc, 1)
                        if not (const and r == 0):
                            down(r, slot if blk else 1 - slot, 1 - blk, const and r <= 2, const and r - 1 >= 2 * LAST)
                tiles(pe, tile)
                down(2 * NT, 0, 1, False, True)

                banks = [psG[0], psG[1], psU, psC]
                for T in range(TILES):
                    if T == 0:
                        pe.wait_ge(s_h, 2 * NT)
                    if T % 4 == 0:
                        pe.wait_ge(s_ye, T // 4 + 1)
                        pe.wait_ge(s_yv, T // 4 + 1)
                    if T >= 4:
                        pe.wait_ge(s_x, T - 3)
                    for c in range(HC):
                        last = pe.transpose(banks[T % 4][:, c * P:(c + 1) * P], yT[:, c, T * P:(T + 1) * P], ident[:, :])
                    last.then_inc(s_tr, 1)

            @block.scalar
            def _(act):
                for k in range(2):
                    act.wait_ge(s_l, k + 1)
                    act.activation(L[:, 4 * k:4 * k + 4, :].rearrange("p t e -> p (t e)"), psG[k][:, 0:4 * EW],
                                   ACT.Copy).then_inc(s_le, 1)
                act.wait_ge(s_e, 1)
                act.activation(ex[:, :, :], ex[:, :, :], ACT.Exp).then_inc(s_e, 1)
                if gated:
                    act.activation(sg[:, :], L[:, :, E], ACT.Exp, scale=-1.0).then_inc(s_e, 1)
                banks = [psU, psC, psG[0], psG[1]]
                for n in range(2 * NC):
                    act.wait_ge(s_ct, n + 1)
                    act.activation(cT[n // 2][:, (n % 2) * BLK:(n % 2 + 1) * BLK], banks[n][:, :],
                                   ACT.Copy).then_inc(s_cte, 1)

                def split_hi(j, slot):
                    if isinstance(j, int):
                        act.wait_ge(s_wr[slot], 16 * (j // 2 + 1))
                    else:
                        act.wait_ge(s_wr[slot], 8 * (j - slot) + 16)
                    if not isinstance(j, int) or j >= 2:
                        act.wait_ge(s_d, 2 * j - 2)
                    act.activation(Whi[slot][:, :], Wraw[slot][:, :], ACT.Copy).then_inc(s_whi, 1)

                def tile(j, slot):
                    for blk in range(2):
                        r = 2 * j + blk
                        act.wait_ge(s_g, r + 1)
                        if not (isinstance(j, int) and r < 2):
                            act.wait_ge(s_t, r - 1)
                        act.activation(a[blk][:, :], psG[blk][:, :], ACT.Silu).then_inc(s_a, 1)
                        act.wait_ge(s_h, r + 1)
                        if not (isinstance(j, int) and r < 2):
                            act.wait_ge(s_d, r - 1)
                        act.activation(hhi[blk][:, :], h[blk][:, :], ACT.Copy).then_inc(s_hhi, 1)
                        if blk == 0 and not (isinstance(j, int) and j == LAST):
                            split_hi(j + 1, 1 - slot)
                split_hi(0, 0)
                tiles(act, tile)
                act.wait_ge(s_d, 2 * NT)
                for blk in range(2):
                    act.activation(yT[:, 0, blk * BLK:(blk + 1) * BLK], acc[0][blk][:, :], ACT.Copy).then_inc(s_ye, 1)

            @block.vector
            def _(dve):
                link = chain(dve, s_dch)
                dve.wait_ge(s_r, 16)
                link(dve.tensor_copy(rhi[:, :, :], rw[:, :, :]))
                dve.tensor_tensor(rlo[:, :, :], rw[:, :, :], rhi[:, :, :].bitcast(F32), ALU.subtract).then_inc(s_rs, 1)
                dve.wait_ge(s_le, 2)
                dve.wait_ge(s_z, 2 + NC + (0 if gated else 1))
                for T in range(TILES):
                    last = dve.max(m8[:, T, :], L[:, T, 0:E])
                link(last)
                wide = lambda col: col.broadcast_to([P, TILES, E])
                logits, kth = L[:, :, 0:E], m8[:, :, K - 1:K]
                dve.tensor_tensor(ex[:, :, :], logits, wide(m8[:, :, 0:1]), ALU.subtract).then_inc(s_e, 1)
                dve.tensor_tensor(gt[:, :, :], logits, wide(kth), ALU.is_gt)
                link(dve.tensor_tensor(eq[:, :, :], logits, wide(kth), ALU.is_equal))
                dve.tensor_reduce(need[:, :], gt[:, :, :], AX.X, ALU.add)
                flat = lambda x: x[:, :, :].rearrange("p t e -> p (t e)")
                link(dve.tensor_tensor_scan(flat(cum), flat(rst), flat(eq), 0.0, ALU.mult, ALU.add))
                link(dve.tensor_scalar(need[:, :], need[:, :], -1.0, float(K), ALU.mult, ALU.add))
                link(dve.tensor_tensor(cum[:, :, :], cum[:, :, :], need[:, :].unsqueeze(2).broadcast_to([P, TILES, E]),
                                       ALU.is_le))
                link(dve.tensor_tensor(eq[:, :, :], eq[:, :, :], cum[:, :, :], ALU.mult))
                link(dve.tensor_tensor(gt[:, :, :], gt[:, :, :], eq[:, :, :], ALU.add))
                dve.wait_ge(s_e, 3 if gated else 2)
                link(dve.tensor_tensor(ex[:, :, :], ex[:, :, :], gt[:, :, :], ALU.mult))
                link(dve.tensor_reduce(ssum[:, :], ex[:, :, :], AX.X, ALU.add))
                link(dve.reciprocal(rsum[:, :], ssum[:, :]))
                link(dve.tensor_tensor(ex[:, :, :], ex[:, :, :], rsum[:, :].unsqueeze(2).broadcast_to([P, TILES, E]),
                                       ALU.mult))
                lo0 = E if gated else E + 1
                link(dve.tensor_copy(cmb[0][:, :, 0:E].bitcast(F32R), ex[:, :, :]))
                last = dve.tensor_tensor(cmb[0][:, :, lo0:lo0 + E], ex[:, :, :], cmb[0][:, :, 0:E], ALU.subtract)
                if gated:
                    link(dve.tensor_scalar(sg[:, :], sg[:, :], 1.0, None, ALU.add))
                    link(dve.reciprocal(sg[:, :], sg[:, :]))
                    link(dve.tensor_copy(cmb[1][:, :, 0].bitcast(F32R), sg[:, :]))
                    last = dve.tensor_tensor(cmb[1][:, :, 1], sg[:, :], cmb[1][:, :, 0], ALU.subtract)
                last.then_inc(s_c, 1)

                def tile(j, slot):
                    for blk in range(2):
                        r = 2 * j + blk
                        dve.wait_ge(s_a, r + 1)
                        dve.wait_ge(s_u, r + 1)
                        dve.tensor_tensor(t[:, :], a[blk][:, :], psU[:, :], ALU.mult).then_inc(s_t, 1)
                        dve.wait_ge(s_cc, r + 1)
                        dve.wait_ge(s_t, r + 1)
                        if not (isinstance(j, int) and r < 2):
                            dve.wait_ge(s_hlo, r - 1)
                        dve.tensor_tensor(h[blk][:, :], t[:, :], psC[:, :], ALU.mult).then_inc(s_h, 1)
                tiles(dve, tile)
                dve.wait_ge(s_d, 2 * NT)
                for blk in range(2):
                    dve.tensor_copy(yT[:, 1, blk * BLK:(blk + 1) * BLK], acc[1][blk][:, :]).then_inc(s_yv, 1)
                banks = [psG[0], psG[1], psU, psC]
                for T in range(TILES):
                    dve.wait_ge(s_tr, T + 1)
                    dve.tensor_tensor(X[:, T, :], X[:, T, :], banks[T % 4][:, 0:HID], ALU.add).then_inc(s_x, 1)


def time_mix(nc, sems, X, xT, w, cols, s_w):
    with ExitStack() as ctx:
        sb = lambda n, s, d=F32: ctx.enter_context(nc.sbuf_tensor("tm_" + n, s, d))
        sem = lambda n: sems("tm_" + n)
        full = [P, HC, TOK]
        sx, dx = sb("sx", full), sb("dx", full)
        mixed = [sb("xk", full), sb("xv", full), sb("xr", full)]
        k, v, r = sb("k", full), sb("v", full), sb("r", full)
        decay = sb("decay", [P, HC])
        dec = sb("dec", full)
        norm = sb("norm", [P, HC, TOK])
        num, den = sb("num", [P, HC, TOK + 1]), sb("den", [P, HC, TOK + 1])
        normp = sb("normp", full)
        cn, ep, ec, ed, ek = (sb(n, full) for n in ("cn", "ep", "ec", "ed", "ek"))
        rwkv = sb("rwkv", full)
        bank = [ctx.enter_context(nc.psum_tensor(f"tm_ps{i}", [P, BLK], F32)) for i in range(8)]
        s_dch, s_pch, s_mix, s_pr, s_ev, s_dy, s_np, s_arg, s_exp, s_ekv, s_p2, s_rw, s_o, s_x, s_z, s_den = (
            sem(n) for n in ("dch", "pch", "mix", "pr", "ev", "dy", "np", "arg", "exp", "ekv", "p2", "rw", "o", "x", "z",
                             "den"))
        starts = lambda x, c: x[:, c, :].rearrange("p (b t) -> p b t", t=SEQ)[:, :, 0:1]
        rest = lambda x, c: x[:, c, :].rearrange("p (b t) -> p b t", t=SEQ)[:, :, 1:SEQ]
        before = lambda x, c: x[:, c, :].rearrange("p (b t) -> p b t", t=SEQ)[:, :, 0:SEQ - 1]

        with nc.Block() as block:
            @block.tensor
            def _(pe):
                for g in range(12):
                    m, blk, oc = g // 4, g // 2 % 2, g % 2
                    if g % 4 == 0:
                        pe.wait_ge(s_w[m], 16)
                        pe.wait_ge(s_mix, 2 * m + 2)
                    if g >= 8:
                        pe.wait_ge(s_ev, g - 7)
                    for ic in range(HC):
                        last = pe.matmul(bank[g % 8][:, :], w[m][:, ic, oc * P:(oc + 1) * P],
                                         mixed[m][:, ic, blk * BLK:(blk + 1) * BLK], start=(ic == 0), stop=(ic == HC - 1))
                    last.then_inc(s_pr, 1)
                pe.wait_ge(s_w[3], 16)
                pe.wait_ge(s_rw, 2)
                pe.wait_ge(s_ev, 12)
                for T in range(TILES):
                    for c in range(HC):
                        last = pe.matmul(bank[T][:, 0:HID], rwkv[:, c, T * P:(T + 1) * P], w[3][:, c, :],
                                         start=(c == 0), stop=(c == HC - 1))
                    last.then_inc(s_o, 1)

            @block.scalar
            def _(act):
                act.activation(decay[:, :], cols["time_decay"][:, :], ACT.Exp).then_inc(s_dy, 1)
                for g in range(12):
                    m, blk, oc = g // 4, g // 2 % 2, g % 2
                    act.wait_ge(s_pr, g + 1)
                    act.activation((k, v, r)[m][:, oc, blk * BLK:(blk + 1) * BLK], bank[g % 8][:, :],
                                   ACT.Copy if m < 2 else ACT.Sigmoid).then_inc(s_ev, 1)
                for c in range(HC):
                    for n, x in enumerate((ed, ek, ep, ec)):
                        act.wait_ge(s_arg, 4 * c + n + 1)
                        act.activation(x[:, c, :], x[:, c, :], ACT.Exp).then_inc(s_exp, 1)

            @block.gpsimd
            def _(pool):
                for x in (num, den):
                    pool.memset(x[:, :, 0:1], 0.0).then_inc(s_z, 1)
                for c in range(HC):
                    pool.memset(starts(normp, c), NEG).then_inc(s_z, 1)
                for c in range(HC):
                    pool.wait_ge(s_exp, 4 * c + 2)
                    pool.tensor_tensor(dx[:, c, :], ek[:, c, :], v[:, c, :], ALU.mult).then_inc(s_ekv, 1)
                    pool.wait_ge(s_exp, 4 * c + 4)
                    pool.tensor_tensor(sx[:, c, :], ec[:, c, :], v[:, c, :], ALU.mult).then_inc(s_p2, 1)
                    pool.wait_ge(s_den, c + 1)
                    pool.tensor_tensor(normp[:, c, :], ep[:, c, :], den[:, c, 0:TOK], ALU.mult).then_inc(s_p2, 1)

            @block.vector
            def _(dve):
                link = chain(dve, s_dch)
                for c in range(HC):
                    dve.memset(starts(sx, c), 0.0)
                    dve.tensor_copy(rest(sx, c), before(xT, c))
                link(dve.memset(cn[:, :, 0:1], 0.0))
                link(dve.tensor_tensor(dx[:, :, :], xT[:, :, :], sx[:, :, :], ALU.subtract))
                for m, mix in enumerate(("mix_k", "mix_v", "mix_r")):
                    for c in range(HC):
                        dve.scalar_tensor_tensor(mixed[m][:, c, :], dx[:, c, :], cols[mix][:, c:c + 1], sx[:, c, :],
                                                 ALU.mult, ALU.add).then_inc(s_mix, 1)
                dve.wait_ge(s_dy, 1)
                dve.wait_ge(s_z, 4)
                link(dve.tensor_scalar(decay[:, :], decay[:, :], -1.0, None, ALU.mult))
                for c in range(HC):
                    link(dve.tensor_scalar(dec[:, c, :], xT[:, c, :], 0.0, decay[:, c:c + 1], ALU.mult, ALU.add))
                    link(dve.memset(starts(dec, c), NEG))
                cw = cols["current_token_weight"]
                dve.wait_ge(s_ev, 8)
                for c in range(HC):
                    link(dve.tensor_tensor_scan(norm[:, c, :], dec[:, c, :], k[:, c, :], NEG, ALU.add, ALU.max))
                    link(dve.tensor_copy(rest(normp, c), before(norm, c)))
                    dve.scalar_tensor_tensor(ed[:, c, :], normp[:, c, :], decay[:, c:c + 1], norm[:, c, :],
                                             ALU.add, ALU.subtract).then_inc(s_arg, 1)
                    dve.tensor_tensor(ek[:, c, :], k[:, c, :], norm[:, c, :], ALU.subtract).then_inc(s_arg, 1)
                    link(dve.scalar_tensor_tensor(cn[:, c, :], k[:, c, :], cw[:, c:c + 1], normp[:, c, :],
                                                  ALU.add, ALU.max))
                    dve.tensor_tensor(ep[:, c, :], normp[:, c, :], cn[:, c, :], ALU.subtract).then_inc(s_arg, 1)
                    dve.scalar_tensor_tensor(ec[:, c, :], k[:, c, :], cw[:, c:c + 1], cn[:, c, :],
                                             ALU.add, ALU.subtract).then_inc(s_arg, 1)
                for c in range(HC):
                    dve.wait_ge(s_exp, 4 * c + 2)
                    dve.tensor_tensor_scan(den[:, c, 1:TOK + 1], ed[:, c, :], ek[:, c, :], 0.0,
                                           ALU.mult, ALU.add).then_inc(s_den, 1)
                    dve.wait_ge(s_ekv, c + 1)
                    link(dve.tensor_tensor_scan(num[:, c, 1:TOK + 1], ed[:, c, :], dx[:, c, :], 0.0,
                                                ALU.mult, ALU.add))
                    dve.wait_ge(s_exp, 4 * c + 4)
                    link(dve.tensor_tensor(cn[:, c, :], ep[:, c, :], num[:, c, 0:TOK], ALU.mult))
                    dve.wait_ge(s_p2, 2 * c + 1)
                    link(dve.tensor_tensor(cn[:, c, :], cn[:, c, :], sx[:, c, :], ALU.add))
                    dve.wait_ge(s_p2, 2 * c + 2)
                    link(dve.tensor_tensor(dec[:, c, :], normp[:, c, :], ec[:, c, :], ALU.add))
                    link(dve.reciprocal(dec[:, c, :], dec[:, c, :]))
                    link(dve.tensor_tensor(cn[:, c, :], cn[:, c, :], dec[:, c, :], ALU.mult))
                    dve.wait_ge(s_ev, 12)
                    dve.tensor_tensor(rwkv[:, c, :], cn[:, c, :], r[:, c, :], ALU.mult).then_inc(s_rw, 1)
                for T in range(TILES):
                    dve.wait_ge(s_o, T + 1)
                    dve.tensor_tensor(X[:, T, :], X[:, T, :], bank[T][:, 0:HID], ALU.add).then_inc(s_x, 1)


def perceiver(nc, src, out):
    with ExitStack() as top:
        sb = lambda n, s, d=F32: top.enter_context(nc.sbuf_tensor(n, s, d))
        sem = lambda n: nc.alloc_semaphore(n)
        sems = Semaphores(nc)
        X = sb("X", [P, TILES, HID])
        ident = sb("ident", [P, P])
        s_x = [sem(f"x_in{k}") for k in range(2)]
        s_const, s_out = sem("const"), sem("out")
        x_view = src["x"].rearrange("(t p) h -> p t h", p=P)

        with ExitStack() as ctx:
            s1 = lambda n, s, d=F32: ctx.enter_context(nc.sbuf_tensor(n, s, d))
            xnT = s1("xnT", [P, HC, TOK])
            Md = s1("Md", [P, HC, HEADS, 2, DC])
            V = s1("V", [P, 8, HID])
            cosN, sinN = s1("cosN", [P, KT, DC]), s1("sinN", [P, KT, DC])
            raw = [s1(f"raw{i}", [P, KT, DC]) for i in range(2)]
            KVd = [s1(f"KVd{i}", [P, KT, 2, DC]) for i in range(4)]
            s_raw = [sems(f"raw{i}") for i in range(2)]
            s_tab = sems("rope_tables")
            rope, s_rope = make_rope(nc, sems, ctx, raw, s_raw, cosN, sinN, KVd)
            with ExitStack() as wctx:
                w = latent_weight_buffers(nc, wctx)
                s_w = {n: sems("w_" + n) for n in w}
                with nc.Block() as block:
                    @block.gpsimd
                    def _(pool):
                        pool.memset(ident[:, :], 0.0).then_inc(s_const, 1)
                        pool.wait_ge(s_const, 1)
                        pool.affine_select(out=ident[:, :], in_=ident[:, :], compare_op=ALU.not_equal, fill=1.0,
                                           base=0, pattern=[[-1, P]], channel_multiplier=1)
                        for r in raw:
                            pool.memset(r[:, KT - 1, :], 0.0)

                    @block.sync
                    def _(sp):
                        for k in range(2):
                            sp.dma_start(X[:, 4 * k:4 * k + 4, :], x_view[:, 4 * k:4 * k + 4, :]).then_inc(s_x[k], 16)

                def loads(sp):
                    for n in ("wqrT", "wkrT"):
                        sp.dma_start(w[n][:], src[n]).then_inc(s_w[n], 16)
                    sp.dma_start(cosN[:], src["cosN"]).then_inc(s_tab, 16)
                    sp.dma_start(sinN[:], src["sinN"]).then_inc(s_tab, 16)
                    for b in range(2):
                        load_latents(sp, src, raw, s_raw, b, b)
                    for n in ("wkcqT", "wq", "wkckv", "woT"):
                        sp.dma_start(w[n][:], src[n]).then_inc(s_w[n], 16)
                    sp.wait_ge(s_tab, 32)
                layernorm(nc, sems, "ln0", X, ident, (xnT,), loads=loads, x_load=s_x)
                latent_weights(nc, sems, Md, V, w, s_w, rope)
            latent_attention(nc, sems, X, xnT, ident, Md, V, src, raw, s_raw, KVd, rope, s_rope)
            sems.recycle()

        with ExitStack() as ctx:
            s2 = lambda n, s, d=F32: ctx.enter_context(nc.sbuf_tensor(n, s, d))
            xnT = s2("a0_xnT", [P, HC, TOK])
            w = {n: s2(n, [P, HC, HID]) for n in ("a0_wq", "a0_wk", "a0_wv", "a0_wo")}
            s_w = {n: sems("w_" + n) for n in w}

            def loads(sp):
                for n in w:
                    sp.dma_start(w[n][:], src[n]).then_inc(s_w[n], 16)
            layernorm(nc, sems, "ln1", X, ident, (xnT,), loads=loads)
            head_attention(nc, sems, "a0", X, xnT, ident, w["a0_wq"], list(s_w.values()), -1.0e9,
                           (w["a0_wk"], xnT, w["a0_wv"]), None, w["a0_wo"])
        with ExitStack() as ctx:
            s3 = lambda n, s, d=F32: ctx.enter_context(nc.sbuf_tensor(n, s, d))
            xhi, xlo = s3("f0_xhi", [P, HC, TOK], F32R), s3("f0_xlo", [P, HC, TOK], F32R)
            layernorm(nc, sems, "ln2", X, ident, (xhi, xlo))
            experts(nc, sems, "f0", X, xhi, xlo, ident, src["f0_stream"], src["f0_router"], 16, 4, 25, False)
            sems.recycle()

        with ExitStack() as ctx:
            s4 = lambda n, s, d=F32: ctx.enter_context(nc.sbuf_tensor(n, s, d))
            xnT = s4("x1_xnT", [P, HC, TOK])
            w = {n: s4(n, [P, HC, HID]) for n in ("x1_wq", "x1_wo")}
            w.update({n: s4(n, [DC, HID]) for n in ("x1_wk", "x1_wv")})
            w["x1_lat"] = s4("x1_lat", [DC, TOK])
            s_w = {n: sems("w_" + n) for n in w}

            def loads(sp):
                for n in w:
                    sp.dma_start(w[n][:], src[n]).then_inc(s_w[n], 16)
            layernorm(nc, sems, "ln3", X, ident, (xnT,), loads=loads)
            head_attention(nc, sems, "x1", X, xnT, ident, w["x1_wq"], list(s_w.values()), NEG,
                           (w["x1_wk"], w["x1_lat"], w["x1_wv"]), "latent", w["x1_wo"])

        with ExitStack() as ctx:
            s5 = lambda n, s, d=F32: ctx.enter_context(nc.sbuf_tensor(n, s, d))
            xT = s5("tm_xT", [P, HC, TOK])
            w = [s5(f"tm_w{n}", [P, HC, HID]) for n in "kvro"]
            cols = s5("tm_cols", [P, 7, HC])
            names = ("ln_w", "ln_b", "mix_k", "mix_v", "mix_r", "time_decay", "current_token_weight")
            col = {n: cols[:, i, :] for i, n in enumerate(names)}
            s_w = [sems(f"tm_w{n}_in") for n in "kvro"]
            s_cols = sems("tm_cols_in")

            def loads(sp):
                sp.dma_start(cols[:], src["tm_cols"]).then_inc(s_cols, 16)
                for n, t, s in zip("kvro", w, s_w):
                    sp.dma_start(t[:], src["tm_w" + n]).then_inc(s, 16)
                sp.wait_ge(s_cols, 16)
            layernorm(nc, sems, "ln4", X, ident, (xT,), affine=(col["ln_w"], col["ln_b"]), s_affine=s_cols, twice=True,
                      loads=loads)
            time_mix(nc, sems, X, xT, w, col, s_w)

        with ExitStack() as ctx:
            s6 = lambda n, s, d=F32: ctx.enter_context(nc.sbuf_tensor(n, s, d))
            xhi, xlo = s6("f1_xhi", [P, HC, TOK], F32R), s6("f1_xlo", [P, HC, TOK], F32R)
            layernorm(nc, sems, "ln5", X, ident, (xhi, xlo))
            experts(nc, sems, "f1", X, xhi, xlo, ident, src["f1_stream"], src["f1_router"], 64, 8, 33, True, out, s_out)


def rope_tables():
    import numpy as np
    f = np.float32
    inv = (f(1.0) / np.power(f(10000.0), (np.arange(0, DC, 2, dtype=f) / f(DC)).astype(f)).astype(f)).astype(f)
    angle = (np.arange(KEYS, dtype=f)[:, None] * inv[None, :]).astype(f).astype(np.float64)
    sin = np.repeat(np.sin(angle), 2, axis=-1)
    cos = np.repeat(np.cos(angle), 2, axis=-1)
    sin[:, :DC // 2] *= -1
    tiles = []
    for t in (cos, sin):
        full = np.zeros((KT * P, DC), f)
        full[:KEYS] = t
        tiles.append(np.ascontiguousarray(full.reshape(KT, P, DC).transpose(1, 0, 2)))
    return tiles


def kernel(**inputs):
    import numpy as np
    import concourse.bacc as bacc
    from concourse.bass_utils import run_bass_kernel_spmd

    a = {k: np.asarray(v) for k, v in inputs.items()}
    arrays = layouts(a)
    nc = bacc.Bacc("TRN2", target_bir_lowering=False, num_devices=1)
    arrays = {k: np.ascontiguousarray(v) for k, v in arrays.items()}
    src = {k: nc.dram_tensor("in_" + k, v.shape, mybir.dt.from_np(v.dtype), kind="ExternalInput").ap()
           for k, v in arrays.items()}
    out = nc.dram_tensor("out", (TOK, HID), F32, kind="ExternalOutput").ap()
    perceiver(nc, src, out)
    r = run_bass_kernel_spmd(nc, [{"in_" + k: v for k, v in arrays.items()}], core_ids=[0])
    return r.results[0]["out"].reshape(BATCH, SEQ, HID)


def layouts(a):
    import numpy as np
    cosN, sinN = rope_tables()
    d = {"x": a["x"].reshape(TOK, HID), "ctx": a["ctx_512"], "cosN": cosN, "sinN": sinN}
    d["wqrT"] = a["L0_xattn_W_qr"].transpose(2, 0, 1)
    d["wkrT"] = a["L0_xattn_W_kr"].transpose(2, 0, 1)
    d["wkcqT"] = a["L0_xattn_w_kc_q"].reshape(HEADS, DK, 2, DCQ // 2).transpose(3, 2, 0, 1)
    d["wq"] = a["L0_xattn_Wq"].reshape(HEADS, DK, HID).transpose(1, 0, 2)
    d["wkckv"] = a["L0_xattn_w_kc_kv"].transpose(1, 0, 2)
    d["woT"] = a["L0_xattn_Wo"].reshape(HID, HEADS, DK).transpose(2, 1, 0)
    by_chunk = lambda w: w.reshape(HC, P, -1).transpose(1, 0, 2)
    for n, k in (("a0_wq", "W_q"), ("a0_wk", "W_k"), ("a0_wv", "W_v"), ("a0_wo", "W_o")):
        d[n] = by_chunk(a["L0_attn_" + k])
    d["x1_wq"] = by_chunk(a["L1_xattn_Wq"].T)
    d["x1_wo"] = by_chunk(a["L1_xattn_Wout"].T)
    d["x1_wk"], d["x1_wv"] = a["L1_xattn_Wkv_expand"][:HID].T, a["L1_xattn_Wkv_expand"][HID:].T
    d["x1_lat"] = a["ctx_512"][:, :SEQ].transpose(2, 0, 1).reshape(DC, TOK)
    for n, k in (("k", "Wk"), ("v", "Wv"), ("r", "Wr"), ("o", "Wo")):
        d["tm_w" + n] = by_chunk(a["L1_attn_" + k].T)
    names = ("ln_w", "ln_b", "mix_k", "mix_v", "mix_r", "time_decay", "current_token_weight")
    d["tm_cols"] = np.stack([a["L1_attn_" + n].reshape(HC, P).T for n in names], axis=1)

    def stream(gate, up, down, sel, NT):
        f = np.float32
        s = np.zeros((NT, P, 7 * P), f)
        H = gate.shape[1]
        pad = lambda m, ax: np.pad(m, [(0, NT * P - H if i == ax else 0) for i in range(2)])
        for at, m in ((0, gate), (2 * P, up)):
            s[:, :, at:at + 2 * P] = pad(m, 1).reshape(HC, P, NT, P).transpose(2, 1, 0, 3).reshape(NT, P, 2 * P)
        s[:, :, 4 * P:6 * P] = pad(down, 0).reshape(NT, P, HID)
        s[:, :, 6 * P:] = sel.reshape(P, NT, P).transpose(1, 0, 2)
        return s

    E, I, NT = 16, 176, 25
    flat = lambda w: w.transpose(1, 0, 2).reshape(HID, -1)
    owner = np.minimum(np.arange(NT * P) // I, E)
    sel = np.zeros((P, NT * P), np.float32)
    for half in range(2):
        sel[owner + (E + 1) * half, np.arange(NT * P)] = 1.0
    d["f0_stream"] = stream(np.concatenate([flat(a["L0_ffn_w_gate"]), a["L0_ffn_sw_gate"]], 1),
                            np.concatenate([flat(a["L0_ffn_w_up"]), a["L0_ffn_sw_up"]], 1),
                            np.concatenate([a["L0_ffn_w_down"].reshape(E * I, HID), a["L0_ffn_sw_down"]], 0), sel, NT)
    d["f0_router"] = by_chunk(a["L0_ffn_gate_w"].T)

    E, I, NT = 64, 64, 33
    sel = np.zeros((P, NT * P), np.float32)
    n = np.arange(E * I)
    for half in range(2):
        sel[n // I + E * half, n] = 1.0
        sel[half, E * I:E * I + I] = 1.0
    gu = a["L1_ffn_gu_w"]
    to_cols = lambda w: w.transpose(2, 0, 1).reshape(HID, -1)
    d["f1_stream"] = stream(np.concatenate([to_cols(gu[:, :I]), a["L1_ffn_sh_gate_w"].T], 1),
                            np.concatenate([to_cols(gu[:, I:]), a["L1_ffn_sh_up_w"].T], 1),
                            np.concatenate([a["L1_ffn_dp_w"].transpose(0, 2, 1).reshape(E * I, HID),
                                            a["L1_ffn_sh_down_w"].T], 0), sel, NT)
    router = np.concatenate([a["L1_ffn_gate_w"].T, a["L1_ffn_sh_gate1_w"].T, np.zeros((HID, 1), np.float32)], 1)
    d["f1_router"] = by_chunk(router)
    return d
```

```python
from contextlib import ExitStack

import concourse.bass as bass
from concourse import mybir

F32 = mybir.dt.float32
F32R = mybir.dt.float32r
BF16 = mybir.dt.bfloat16
ALU = mybir.AluOpType
ACT = mybir.ActivationFunctionType
AX = mybir.AxisListType

P = 128
BATCH, SEQ, HID = 16, 64, 256
TOK = BATCH * SEQ
TILES = TOK // P
HC = HID // P
BLK = 512
EPS = 1e-5
NEG = -1.0e30

HEADS = 16
KEYS, DC, DCQ, RR, DK = 1601, 64, 192, 64, 128
KT = -(-KEYS // P)
KLAST = KEYS - (KT - 1) * P
KPAD = KEYS + KEYS % 2
KA = 2 * BLK
KB = KEYS - KA
PPB = HEADS // 4
QP = 2 * P
DH = HID // HEADS


class Semaphores:

    def __init__(self, nc):
        self.nc, self.held = nc, []

    def __call__(self, name):
        self.held.append(self.nc.alloc_semaphore(name))
        return self.held[-1]

    def recycle(self):
        self.nc.clear_and_free_semaphores(self.held)
        self.nc.all_engine_barrier()
        self.held = []


def chain(eng, sem):
    n = [0]

    def link(ins):
        n[0] += 1
        ins.then_inc(sem, 1)
        eng.wait_ge(sem, n[0])
    return link


def layernorm(nc, sems, name, X, ident, outs, affine=None, s_affine=None, twice=False, loads=None, x_load=None):
    with ExitStack() as ctx:
        sb = lambda n, s, d=F32: ctx.enter_context(nc.sbuf_tensor(f"{name}_{n}", s, d))
        sem = lambda n: sems(f"{name}_{n}")
        xn = sb("xn", [P, TILES, HID])
        stats = sb("stats", [P, TILES, 6])
        mv = sb("mv", [P, TILES, 2])
        var, sd, r0, t0, rstd = (sb(n, [P, TILES]) for n in ("var", "sd", "r0", "t0", "rstd"))
        psT = [ctx.enter_context(nc.psum_tensor(f"{name}_psT{i}", [P, BLK], F32)) for i in range(4)]
        s_dve, s_var, s_sd, s_xn, s_tr, s_hi, s_lo = (
            sem(n) for n in ("dve", "var", "sd", "xn", "tr", "hi", "lo"))
        with nc.Block() as block:
            @block.sync
            def _(sp):
                if loads is not None:
                    loads(sp)

            @block.vector
            def _(dve):
                link = chain(dve, s_dve)

                def normalise(n, x, signal):
                    for t in range(TILES):
                        if x_load is not None and t % 4 == 0:
                            dve.wait_ge(x_load[t // 4], 16)
                        last = dve.bn_stats(stats[:, t, :], x[:, t, :])
                    link(last)
                    for t in range(TILES):
                        last = dve.bn_aggr(mv[:, t, :], stats[:, t, :])
                    link(last)
                    dve.tensor_scalar(var[:, :], mv[:, :, 1], EPS, None, ALU.add).then_inc(s_var, 1)
                    dve.wait_ge(s_sd, n + 1)
                    link(dve.reciprocal(r0[:, :], sd[:, :]))
                    link(dve.tensor_tensor(t0[:, :], r0[:, :], r0[:, :], ALU.mult))
                    link(dve.tensor_tensor(t0[:, :], t0[:, :], var[:, :], ALU.mult))
                    link(dve.tensor_scalar(t0[:, :], t0[:, :], -0.5, 1.5, ALU.mult, ALU.add))
                    link(dve.tensor_tensor(rstd[:, :], r0[:, :], t0[:, :], ALU.mult))
                    for t in range(TILES):
                        last = dve.tensor_scalar(xn[:, t, :], x[:, t, :], mv[:, t, 0:1], rstd[:, t:t + 1],
                                                 ALU.subtract, ALU.mult)
                        if signal:
                            last.then_inc(s_xn, 1)
                    return last

                if twice:
                    link(normalise(0, X, False))
                    link(dve.tensor_tensor(X[:, :, :], X[:, :, :], xn[:, :, :], ALU.add))
                    normalise(1, xn, True)
                else:
                    normalise(0, X, True)
                if affine is not None:
                    dve.wait_ge(s_affine, 16)
                for g in range(4):
                    c, half = g % 2, g // 2
                    cols = slice(half * BLK, half * BLK + BLK)
                    if len(outs) == 2:
                        dve.wait_ge(s_hi, g + 1)
                        dve.tensor_tensor(outs[1][:, c, cols], psT[g][:, :], outs[0][:, c, cols].bitcast(F32),
                                          ALU.subtract).then_inc(s_lo, 1)
                    elif g % 2:
                        dve.wait_ge(s_tr, g + 1)
                        if affine is None:
                            dve.tensor_copy(outs[0][:, c, cols], psT[g][:, :]).then_inc(s_lo, 1)
                        else:
                            w, b = affine
                            dve.tensor_scalar(outs[0][:, c, cols], psT[g][:, :], w[:, c:c + 1], b[:, c:c + 1],
                                              ALU.mult, ALU.add).then_inc(s_lo, 1)

            @block.tensor
            def _(pe):
                for g in range(4):
                    c, half = g % 2, g // 2
                    for j in range(4):
                        t = 4 * half + j
                        if c == 0:
                            pe.wait_ge(s_xn, t + 1)
                        last = pe.transpose(psT[g][:, j * P:(j + 1) * P], xn[:, t, c * P:(c + 1) * P], ident[:, :])
                    last.then_inc(s_tr, 1)

            @block.scalar
            def _(act):
                for n in range(2 if twice else 1):
                    act.wait_ge(s_var, n + 1)
                    act.activation(sd[:, :], var[:, :], ACT.Sqrt).then_inc(s_sd, 1)
                if affine is not None:
                    act.wait_ge(s_affine, 16)
                for g in range(4):
                    c, half = g % 2, g // 2
                    cols = slice(half * BLK, half * BLK + BLK)
                    if len(outs) == 2:
                        act.wait_ge(s_tr, g + 1)
                        act.activation(outs[0][:, c, cols], psT[g][:, :], ACT.Copy).then_inc(s_hi, 1)
                    elif g % 2 == 0:
                        act.wait_ge(s_tr, g + 1)
                        if affine is None:
                            act.activation(outs[0][:, c, cols], psT[g][:, :], ACT.Copy).then_inc(s_hi, 1)
                        else:
                            w, b = affine
                            act.activation(outs[0][:, c, cols], psT[g][:, :], ACT.Identity,
                                           scale=w[:, c:c + 1], bias=b[:, c:c + 1]).then_inc(s_hi, 1)


def load_latents(sp, src, raw, s_raw, b):
    sp.dma_start(raw[:, 0:KT - 1, :],
                 src["ctx"][b, 0:(KT - 1) * P, :].rearrange("(t p) d -> p t d", p=P)).then_inc(s_raw, 16)
    sp.dma_start(raw[0:KLAST, KT - 1, :], src["ctx"][b, (KT - 1) * P:KEYS, :]).then_inc(s_raw, 16)


def make_rope(nc, sems, ctx, raw, s_raw, cosN, sinN, KV):
    rope_t = ctx.enter_context(nc.sbuf_tensor("rope_t", [P, 2, 2, DC], F32))
    s_rope = sems("rope")
    s_prod = sems("rope_products")
    H = DC // 2

    def piece(pool, b, bk, u):
        k0, k1 = 2 * u, min(2 * u + 2, KT)
        n = k1 - k0
        if u == 0:
            pool.wait_ge(s_raw, 32 * b + 32)
        ta, tb = rope_t[:, 0, 0:n, :], rope_t[:, 1, 0:n, :]
        c, s = cosN[:, k0:k1, :], sinN[:, k0:k1, :]
        pool.tensor_tensor(ta, raw[:, k0:k1, :], c, ALU.mult).then_inc(s_prod, 1)
        pool.tensor_tensor(tb[:, :, 0:H], raw[:, k0:k1, H:DC], s[:, :, 0:H], ALU.mult).then_inc(s_prod, 1)
        pool.tensor_tensor(tb[:, :, H:DC], raw[:, k0:k1, 0:H], s[:, :, H:DC], ALU.mult).then_inc(s_prod, 1)
        pool.wait_ge(s_prod, (b * 7 + u) * 3 + 3)
        pool.tensor_tensor(KV[bk % 4][:, k0:k1, :], ta, tb, ALU.add).then_inc(s_rope, 1)
        pool.wait_ge(s_rope, b * 7 + u + 1)
    return piece, s_rope


def latent_weight_buffers(nc, ctx):
    sb = lambda n, s: ctx.enter_context(nc.sbuf_tensor("lw_" + n, s, F32))
    return {
        "wqrT": sb("wqr", [RR, HEADS, DCQ]),
        "wkrT": sb("wkr", [RR, HEADS, DC]),
        "wkcqT": sb("wkcq", [DCQ // 2, 2, HEADS, DK]),
        "wq": sb("wq", [DK, HEADS, HID]),
        "wkckv": sb("wkv", [DK, HEADS, DC]),
        "woT": sb("wo", [DK, HEADS, HID]),
    }


def latent_weights(nc, sems, ident, M, V, w, s_w, src, raw, s_raw, rope, s_rope):
    with ExitStack() as ctx:
        sb = lambda n, s, d=F32: ctx.enter_context(nc.sbuf_tensor("lw_" + n, s, d))
        sem = lambda n: sems("lw_" + n)
        CC = DCQ // 2
        PAIRS = HEADS // 2
        wqr, wkr, wkcq, wq, wkv, wo = (w[n] for n in ("wqrT", "wkrT", "wkcqT", "wq", "wkckv", "woT"))
        t1 = sb("t1", [CC, HEADS, 2, DC])
        t2T = sb("t2T", [P, PAIRS, DK])
        t2 = sb("t2", [DK, HEADS, DC])
        mT = sb("mT", [P, PAIRS, HID])
        psA = [ctx.enter_context(nc.psum_tensor(f"lw_A{i}", [P, BLK], F32)) for i in range(4)]
        psB = [ctx.enter_context(nc.psum_tensor(f"lw_B{i}", [P, BLK], F32)) for i in range(4)]
        s_t1, s_t1s, s_t2T, s_t2Ts, s_t2, s_t2s, s_mT, s_mTs, s_m, s_ms, s_v, s_vs = (
            sem(n) for n in ("t1", "t1s", "t2T", "t2Ts", "t2", "t2s", "mT", "mTs", "m", "ms", "v", "vs"))

        with nc.Block() as block:
            @block.tensor
            def _(pe):
                pe.wait_ge(s_w["wqrT"], 16)
                pe.wait_ge(s_w["wkrT"], 16)
                for h in range(HEADS):
                    for cc in range(2):
                        last = pe.matmul(psA[h // 4][0:CC, (h % 4) * 128 + cc * 64:(h % 4) * 128 + cc * 64 + 64],
                                         wqr[:, h, cc * CC:(cc + 1) * CC], wkr[:, h, :], start=True, stop=True)
                    if h % 4 == 3:
                        last.then_inc(s_t1, 1)
                pe.wait_ge(s_w["wkcqT"], 16)
                for j in range(PAIRS):
                    if j % 2 == 0:
                        pe.wait_ge(s_t1s, j // 2 + 1)
                    for cc in range(2):
                        for k in range(2):
                            last = pe.matmul(psB[j // 4][64 * k:64 * k + 64, (j % 4) * P:(j % 4 + 1) * P],
                                             t1[:, 2 * j + k, cc, :], wkcq[:, cc, 2 * j + k, :],
                                             start=(cc == 0), stop=(cc == 1))
                    if j % 4 == 3:
                        last.then_inc(s_t2T, 1)
                for i in range(2):
                    pe.wait_ge(s_t2Ts, i + 1)
                    for j in range(4):
                        last = pe.transpose(psB[2 + i][:, j * P:(j + 1) * P], t2T[:, 4 * i + j, :], ident[:, :])
                    last.then_inc(s_t2, 1)
                pe.wait_ge(s_w["wq"], 16)
                for j in range(PAIRS):
                    if j % 4 == 0:
                        pe.wait_ge(s_t2s, j // 4 + 1)
                    for k in range(2):
                        last = pe.matmul(psA[j // 2][64 * k:64 * k + 64, (j % 2) * HID:(j % 2 + 1) * HID],
                                         t2[:, 2 * j + k, :], wq[:, 2 * j + k, :], start=True, stop=True)
                    if j % 2:
                        last.then_inc(s_mT, 1)
                pe.wait_ge(s_w["wkckv"], 16)
                pe.wait_ge(s_w["woT"], 16)
                for pj in range(8):
                    h = 8 * (pj // 4) + pj % 4
                    if pj == 0:
                        pe.wait_ge(s_t2s, 2)
                    for k in range(2):
                        hh = h + 4 * k
                        last = pe.matmul(psB[pj // 2][64 * k:64 * k + 64, (pj % 2) * HID:(pj % 2 + 1) * HID],
                                         wkv[:, hh, :], wo[:, hh, :], start=True, stop=True)
                    if pj % 2:
                        last.then_inc(s_v, 1)
                for i in range(4):
                    pe.wait_ge(s_mTs, i + 1)
                    for c in range(HC):
                        for j in range(2):
                            last = pe.transpose(psA[i][:, (2 * c + j) * P:(2 * c + j + 1) * P],
                                                mT[:, 2 * i + j, c * P:(c + 1) * P], ident[:, :])
                    last.then_inc(s_m, 1)

            @block.vector
            def _(dve):
                for i in range(4):
                    dve.wait_ge(s_t1, i + 1)
                    dve.tensor_copy(t1[:, 4 * i:4 * i + 4, :, :].rearrange("p h c d -> p (h c d)"),
                                    psA[i][0:CC, :]).then_inc(s_t1s, 1)
                for i in range(2):
                    dve.wait_ge(s_t2T, i + 1)
                    dve.tensor_copy(t2T[:, 4 * i:4 * i + 4, :].rearrange("p j q -> p (j q)"),
                                    psB[i][:, :]).then_inc(s_t2Ts, 1)
                for i in range(2):
                    dve.wait_ge(s_t2, i + 1)
                    dve.tensor_copy(t2[:, 8 * i:8 * i + 8, :].rearrange("p h d -> p (h d)"),
                                    psB[2 + i][:, :]).then_inc(s_t2s, 1)
                for i in range(4):
                    dve.wait_ge(s_mT, i + 1)
                    dve.tensor_copy(mT[:, 2 * i:2 * i + 2, :].rearrange("p j h -> p (j h)"),
                                    psA[i][:, :]).then_inc(s_mTs, 1)
                for i in range(4):
                    dve.wait_ge(s_m, i + 1)
                    dve.tensor_copy(M[:, :, 4 * i:4 * i + 4, :].rearrange("p c h d -> p c (h d)"),
                                    psA[i][:, :].rearrange("p (c x) -> p c x", c=2)).then_inc(s_ms, 1)

            @block.scalar
            def _(act):
                for i in range(4):
                    act.wait_ge(s_v, i + 1)
                    act.activation(V[:, 2 * i:2 * i + 2, :].rearrange("p j o -> p (j o)"),
                                   psB[i][:, :], ACT.Copy).then_inc(s_vs, 1)

            @block.sync
            def _(sp):
                sp.wait_ge(s_rope, 7)
                load_latents(sp, src, raw, s_raw, 1)

            @block.gpsimd
            def _(pool):
                for b in range(2):
                    for u in range(7):
                        rope(pool, b, b, u)


def latent_attention(nc, sems, X, xnT, ident, M, V, src, raw, s_raw, KV, rope, s_rope):
    with ExitStack() as ctx:
        sb = lambda n, s, d=F32: ctx.enter_context(nc.sbuf_tensor("la_" + n, s, d))
        sem = lambda n: sems("la_" + n)
        ps = lambda n, w: ctx.enter_context(nc.psum_tensor("la_" + n, [P, w], F32))
        KThi = [sb(f"KThi{i}", [P, KPAD], F32R) for i in range(2)]
        KTlo = [sb(f"KTlo{i}", [P, KPAD], F32R) for i in range(2)]
        Q = [[sb(f"Q{i}{j}", [P, HEADS, SEQ], F32R) for j in range(2)] for i in range(2)]
        Qm = [sb(f"Qm{i}", [P, QP], F32R) for i in range(2)]
        mt = [sb(f"mt{i}", [P, P]) for i in range(2)]
        nm = sb("nm", [P, 2, 2])
        PT = [sb(f"PT{i}", [P, KT + 1, QP]) for i in range(4)]
        part = sb("part", [P, 4, QP])
        sums = [sb(f"sums{i}", [P, QP]) for i in range(2)]
        ones = sb("ones", [P, SEQ])
        rsum = sb("rsum", [P, QP])
        ctx_all = sb("ctx_all", [P, 8, BATCH, SEQ])
        psS = ps("psS", 2 * BLK)
        psT = [ps(f"psT{i}", BLK) for i in range(3)]
        psV = [ps(f"psV{i}", BLK) for i in range(2)]
        psM = ps("psM", BLK)
        (s_sA, s_sB, s_mxA, s_mxB, s_m, s_mT, s_mrow, s_tp, s_ex, s_add, s_part, s_sum, s_sm,
         s_pv, s_rs, s_ctx, s_msc, s_mhi, s_mlo) = (
            sem(n) for n in ("sA", "sB", "mxA", "mxB", "m", "mT", "mrow", "tp", "ex", "add", "part", "sum",
                             "sm", "pv", "rs", "ctx", "msc", "mhi", "mlo"))
        PAIRS = BATCH * PPB
        BODY = 4
        TURNS = BATCH // BODY
        PB = BODY * PPB
        G = 7
        R0 = 6
        RPT = 8
        ROUNDS = (("K", 0), ("K", 1), ("Q", 0), ("Q", 1), ("K", 0), ("K", 1), ("Q", 2), ("Q", 3))

        BANKS0 = [psM, psV[0], psV[1], psT[0], psT[1], psT[2]]

        def place(kt):
            return kt if kt < 4 else 4 if kt == KT - 1 else kt + 2
        PARTIAL = 5

        def misc_of(i, pt, last):
            kind, g = ROUNDS[pt % 8]
            if last and pt >= PB - (8 if kind == "Q" else PPB):
                return None
            slot = (pt // PPB + 1) % 4 if kind == "K" else (pt // 8 + 1) % 2
            return R0 + i * 2 * RPT + pt, kind, slot, g

        def rows(kt):
            return KLAST if kt == KT - 1 else P

        def tiles(g):
            return range(2 * g, min(2 * g + 2, KT))

        def k_round(pe, slot, g, bank=psM):
            for j, kt in enumerate(range(8 * g, min(8 * g + 8, KT), 2)):
                n = rows(kt)
                last = pe.transpose(bank[:, j * P:j * P + n], KV[slot][0:n, kt:kt + 2, :].rearrange("p t d -> p (t d)"),
                                    ident[0:n, 0:n])
            last.then_inc(s_msc, 1)

        def k_views(g, half, bank=psM):
            n, c0, h = (4, 2)[g], 8 * P * g, slice(64 * half, 64 * half + 64)
            views = [(lambda t, rows_: t[rows_, c0:c0 + 2 * P * n].rearrange("p (n q) -> p n q", q=2 * P)
                      [:, :, half * P:half * P + P],
                      bank[h, 0:n * P].rearrange("p (n q) -> p n q", q=P))]
            if g == 1 and half == 0:
                views.append((lambda t, rows_: t[rows_, (KT - 1) * P:KEYS], bank[h, 2 * P:2 * P + KLAST]))
            return views

        def q_round(pe, tile, g, bank=psM):
            for j in range(2):
                for c in range(HC):
                    last = pe.matmul(bank[:, j * P:(j + 1) * P],
                                     M[:, c, 4 * g + 2 * j:4 * g + 2 * j + 2, :].rearrange("p h d -> p (h d)"),
                                     xnT[:, c, bass.ts(tile, P)], start=(c == 0), stop=(c == HC - 1))
            last.then_inc(s_msc, 1)

        def q_views(slot, g, half, b, bank=psM):
            return (lambda rows_: Q[slot][b][rows_, 4 * g:4 * g + 4, :].rearrange("p (j a) s -> p j a s", a=2)
                    [:, :, half, :],
                    bank[64 * half:64 * half + 64, 0:2 * P].rearrange("p (j b s) -> p j b s", j=2, b=2)[:, :, b, :])

        def queries(pt, h0, n):
            q = Q[pt // 8 % 2][pt // PPB % 2]
            h = 4 * (pt % PPB) + h0
            return q[:, h:h + n, :].rearrange("p h s -> p (h s)")

        def scores(pe, n, pt, k, chunk):
            U = n * 2 + k
            first = isinstance(U, int) and U == 0
            keys = KThi[pt // PPB % 2]
            if chunk == 0:
                if not first:
                    pe.wait_ge(s_mxB, U)
                for a in range(0, KA, BLK):
                    last = pe.matmul(psS[:, a:a + BLK], queries(pt, 2 * k, 2), keys[:, a:a + BLK],
                                     start=True, stop=True)
                last.then_inc(s_sA, 1)
            else:
                pe.wait_ge(s_mxA, U + 1)
                for a in range(KA, KPAD, BLK):
                    b = min(a + BLK, KPAD)
                    last = pe.matmul(psS[:, a - KA:b - KA], queries(pt, 2 * k, 2), keys[:, a:b],
                                     start=True, stop=True)
                last.then_inc(s_sB, 1)

        def shift_rows(pe, n):
            pe.wait_ge(s_m, 2 * n + 2)
            if not (isinstance(n, int) and n == 0):
                pe.wait_ge(s_ex, G * n - 2)
            for k in range(2):
                last = pe.transpose(psT[1][:, k * P:(k + 1) * P], mt[k][:, :], ident[:, :])
            last.then_inc(s_mT, 1)

        def exponents(pe, n, pt, g):
            first = isinstance(n, int) and n == 0
            bb = pt // PPB % 2
            if g == 0:
                pe.wait_ge(s_mrow, n + 1)
                if not first:
                    pe.wait_ge(s_ex, G * n)
            if g >= 3:
                pe.wait_ge(s_ex, G * n + g - 2)
            for j, kt in enumerate(tiles(g)):
                m = rows(kt)
                o = psT[g % 3][0:m, j * QP:(j + 1) * QP]
                pe.matmul(o, KThi[bb][:, kt * P:kt * P + m], queries(pt, 0, 4), start=True, stop=False)
                last = pe.matmul(o, KTlo[bb][:, kt * P:kt * P + m], Qm[pt % 2][:, :], start=False, stop=True)
            last.then_inc(s_tp, 1)

        def values(pe, quad, pt, kslot, kts):
            if 0 in kts:
                pe.wait_ge(s_ex, G * (2 * quad + 2))
                if not (isinstance(quad, int) and quad < 2):
                    pe.wait_ge(s_ctx, 2 * quad - 2)
            for kt in kts:
                n = rows(kt)
                for k in range(2):
                    last = pe.matmul(psV[pt // 2 % 2][64 * k:64 * k + 64, 0:QP], KV[kslot][0:n, kt, :],
                                     PT[(pt + k) % 4][0:n, place(kt), :], start=(kt == 0), stop=(kt == KT - 1))
            if KT - 1 in kts:
                last.then_inc(s_pv, 1)

        def sum_spread(pe, quad, bank):
            pe.wait_ge(s_sum, 2 * quad + 2)
            for k in range(2):
                last = pe.matmul(bank[64 * k:64 * k + 64, QP:2 * QP], ones[:, :], sums[k][:, :], start=True, stop=True)
            last.then_inc(s_sm, 1)

        def misc_pe(pe, i, pt, last):
            r = misc_of(i, pt, last)
            if r is None:
                return
            number, kind, slot, g = r
            pe.wait_ge(s_mlo, number)
            if kind == "K":
                if g == 0:
                    pe.wait_ge(s_rope, (i * BODY + pt // PPB + 2) * 7)
                k_round(pe, slot, g)
            else:
                q_round(pe, i * 2 + pt // 8 + 1, g)

        def values_part(pe, i, pt, where):
            n = i * PB + pt
            if isinstance(n, int) and n < 2:
                return
            half, q = pt % 2, (pt - 2) // 2
            quad = i * (PB // 2) + q
            kts = ((range(0, 3), range(3, 5), range(5, 6), range(6, 7)),
                   (range(7, 9), range(9, 11), range(11, 12), range(12, 13)))[half][where]
            values(pe, quad, (2 * q) % PB, q // 2 % 4, kts)
            if half == 1 and where == 3:
                sum_spread(pe, quad, psV[q % 2])

        with nc.Block() as block:
            @block.sync
            def _(sp):
                def turn(i, n):
                    for k in range(n):
                        sp.wait_ge(s_rope, (i * BODY + k + 2) * 7)
                        load_latents(sp, src, raw, s_raw, i * BODY + k + 2)
                with sp.Fori(0, TURNS - 1) as i:
                    turn(i, BODY)
                turn(TURNS - 1, BODY - 2)

            @block.gpsimd
            def _(pool):
                def partial(n, pt):
                    p = PT[pt % 4]
                    pool.wait_ge(s_ex, G * n + 6)
                    if not (isinstance(n, int) and n == 0):
                        pool.wait_ge(s_part, n)
                    pool.tensor_tensor(part[:, :, :], p[:, 6:10, :], p[:, 10:14, :], ALU.add).then_inc(s_add, 1)
                    pool.wait_ge(s_add, 2 * n + 1)
                    pool.tensor_tensor(part[:, 0:2, :], part[:, 0:2, :], part[:, 2:4, :], ALU.add).then_inc(s_add, 1)
                    pool.wait_ge(s_add, 2 * n + 2)
                    pool.tensor_tensor(p[:, PARTIAL, :], part[:, 0, :], part[:, 1, :], ALU.add).then_inc(s_part, 1)

                def turn(i, ropes):
                    for pt in range(PB):
                        n = i * PB + pt
                        if not (isinstance(n, int) and n == 0):
                            partial(n - 1, pt - 1)
                        if pt // PPB < ropes:
                            for u in range(2 * (pt % PPB), min(2 * (pt % PPB) + 2, 7)):
                                rope(pool, i * BODY + pt // PPB + 2, pt // PPB + 2, u)
                turn(0, BODY)
                with pool.Fori(1, TURNS - 1) as i:
                    turn(i, BODY)
                turn(TURNS - 1, BODY - 2)
                partial(PAIRS - 1, PB - 1)

            @block.tensor
            def _(pe):
                for g in range(2):
                    pe.wait_ge(s_rope, (4, 7)[g])
                    k_round(pe, 0, g, BANKS0[g])
                for g in range(4):
                    q_round(pe, 0, g, BANKS0[2 + g])
                pe.wait_ge(s_mlo, 3)
                for k in range(2):
                    scores(pe, 0, 0, k, 0)
                    scores(pe, 0, 0, k, 1)
                pe.wait_ge(s_mlo, R0)
                scores(pe, 1, 1, 0, 0)
                shift_rows(pe, 0)

                def step(i, pt, last):
                    n = i * PB + pt
                    nxt = (pt + 1) % PB
                    more = not (last and pt == PB - 1)
                    exponents(pe, n, pt, 0)
                    exponents(pe, n, pt, 1)
                    exponents(pe, n, pt, 2)
                    if more:
                        scores(pe, n + 1, nxt, 0, 1)
                    values_part(pe, i, pt, 0)
                    exponents(pe, n, pt, 3)
                    if more:
                        scores(pe, n + 1, nxt, 1, 0)
                    misc_pe(pe, i, pt, last)
                    exponents(pe, n, pt, 4)
                    values_part(pe, i, pt, 1)
                    if more:
                        scores(pe, n + 1, nxt, 1, 1)
                    values_part(pe, i, pt, 2)
                    exponents(pe, n, pt, 5)
                    exponents(pe, n, pt, 6)
                    if not (last and pt >= PB - 2):
                        if pt % PPB == PPB - 2:
                            pe.wait_ge(s_mlo, R0 + (i * 2 + pt // 8) * RPT + (2 if pt % 8 < PPB else 6))
                        scores(pe, n + 2, (pt + 2) % PB, 0, 0)
                    if more:
                        shift_rows(pe, n + 1)
                    values_part(pe, i, pt, 3)

                for pt in range(PB):
                    step(0, pt, False)
                with pe.Fori(1, TURNS - 1) as i:
                    for pt in range(PB):
                        step(i, pt, False)
                for pt in range(PB):
                    step(TURNS - 1, pt, True)
                for pt in range(PB, PB + 2):
                    for where in range(4):
                        values_part(pe, TURNS - 1, pt, where)

            @block.scalar
            def _(act):
                def misc(number, kind, slot, g, source=psM):
                    act.wait_ge(s_msc, number + 1)
                    if kind == "K":
                        for half in range(2):
                            for view, bank in k_views(g, half, source):
                                for k in range(2):
                                    last = act.activation(view(KThi[slot % 2], slice(64 * k, 64 * k + 64)), bank,
                                                          ACT.Copy)
                        last.then_inc(s_mhi, 1)
                    else:
                        for b in range(2):
                            for half in range(2):
                                view, bank = q_views(slot, g, half, b, source)
                                for k in range(2):
                                    last = act.activation(view(slice(64 * k, 64 * k + 64)), bank, ACT.Copy)
                        last.then_inc(s_mhi, 1)

                def misc_act(i, pt, last):
                    r = misc_of(i, pt, last)
                    if r is not None:
                        misc(*r)

                def high_queries(pt):
                    act.activation(Qm[pt % 2][0:64, :], queries(pt, 0, 4)[0:64, :], ACT.Copy)

                def shift_row(n, pt):
                    act.wait_ge(s_mT, n + 1)
                    act.activation(Qm[pt % 2][64:65, :], psT[1][64:65, 0:QP], ACT.Copy).then_inc(s_mrow, 1)

                def exps(n, pt, quad, g):
                    kts = tiles(g)
                    m = rows(kts[-1])
                    if g == 0 and not (isinstance(n, int) and n < 4):
                        act.wait_ge(s_pv, quad - 1)
                        act.wait_ge(s_sum, n - 3)
                    act.wait_ge(s_tp, G * n + g + 1)
                    act.activation(PT[pt % 4][0:m, place(kts[0]):place(kts[0]) + len(kts), :].rearrange("p t q -> p (t q)"),
                                   psT[g % 3][0:m, 0:QP * len(kts)], ACT.Exp).then_inc(s_ex, 1)

                for g in range(2):
                    misc(g, "K", 0, g, BANKS0[g])
                for g in range(4):
                    misc(2 + g, "Q", 0, g, BANKS0[2 + g])
                act.wait_ge(s_mhi, R0)
                high_queries(0)
                act.wait_ge(s_mlo, R0)
                shift_row(0, 0)

                def turn(i, last):
                    for pt in range(PB):
                        n = i * PB + pt
                        for g in range(G):
                            exps(n, pt, i * (PB // 2) + pt // 2, g)
                        if not (last and pt == PB - 1):
                            p = (pt + 1) % 8
                            if p < 4 and not (isinstance(n, int) and n < 7):
                                act.wait_ge(s_mhi, R0 + (i * 2 + (pt + 1) // 8 - 1) * RPT + (3, 4, 7, 8)[p])
                            high_queries((pt + 1) % PB)
                            shift_row(n + 1, (pt + 1) % PB)
                        misc_act(i, pt, last)
                turn(0, False)
                with act.Fori(1, TURNS - 1) as i:
                    turn(i, False)
                turn(TURNS - 1, True)

            @block.vector
            def _(dve):
                dve.memset(ones[:, :], 1.0)
                for t in range(2):
                    dve.memset(KThi[t][:, KEYS:KPAD].bitcast(F32), 0.0)
                    dve.memset(Qm[t][64:P, :].bitcast(F32), 0.0)
                    dve.memset(mt[t][:, :], 0.0)
                for t in range(4):
                    dve.memset(PT[t][64:P, place(KT - 1), :], 0.0)

                def misc(number, kind, slot, g, source=psM):
                    dve.wait_ge(s_mhi, number + 1)
                    if kind == "K":
                        for half in range(2):
                            for view, bank in k_views(g, half, source):
                                last = dve.tensor_tensor(view(KTlo[slot % 2], slice(0, 64)), bank,
                                                         view(KThi[slot % 2], slice(64 * half, 64 * half + 64)).bitcast(F32),
                                                         ALU.subtract)
                        last.then_inc(s_mlo, 1)
                    else:
                        for b in range(2):
                            for half in range(2):
                                view, bank = q_views(slot, g, half, b, source)
                                last = dve.tensor_tensor(view(slice(64, P)), bank,
                                                         view(slice(64 * half, 64 * half + 64)).bitcast(F32), ALU.subtract)
                        last.then_inc(s_mlo, 1)

                def misc_dve(i, pt, last):
                    r = misc_of(i, pt, last)
                    if r is not None:
                        misc(*r)

                for g in range(2):
                    misc(g, "K", 0, g, BANKS0[g])
                misc(2, "Q", 0, 0, BANKS0[2])

                def maximum_a(n, k):
                    dve.wait_ge(s_sA, n * 2 + k + 1)
                    dve.tensor_reduce(nm[:, k, 0:1], psS[:, 0:KA], AX.X, ALU.max, negate=True).then_inc(s_mxA, 1)

                def maximum_b(n, k):
                    U = n * 2 + k
                    dve.wait_ge(s_sB, U + 1)
                    dve.tensor_reduce(nm[:, k, 1:2], psS[:, 0:KB], AX.X, ALU.max, negate=True).then_inc(s_mxB, 1)
                    dve.wait_ge(s_mxB, U + 1)
                    if not (isinstance(n, int) and n == 0):
                        dve.wait_ge(s_mT, n)
                    dve.tensor_tensor(mt[k][:, 64:65], nm[:, k, 0:1], nm[:, k, 1:2], ALU.min).then_inc(s_m, 1)

                def sum_tiles(n, pt, quad):
                    dve.wait_ge(s_part, n + 1)
                    dve.wait_ge(s_ex, G * n + G)
                    if not (isinstance(n, int) and n < 2):
                        dve.wait_ge(s_sm, quad)
                    dve.tensor_reduce(sums[pt % 2][:, :], PT[pt % 4][:, 0:6, :].rearrange("p t q -> p q t"),
                                      AX.X, ALU.add).then_inc(s_sum, 1)

                def quotient(quad, b, qq, half):
                    q, h = slice(half * P, half * P + P), 4 * qq + 2 * half
                    if half == 0:
                        dve.wait_ge(s_pv, quad + 1)
                        dve.wait_ge(s_sm, quad + 1)
                    dve.reciprocal(rsum[:, q], psV[qq][:, QP + half * P:QP + half * P + P]).then_inc(s_rs, 1)
                    dve.wait_ge(s_rs, 2 * quad + half + 1)
                    dve.tensor_tensor(ctx_all[:, h:h + 2, bass.ds(b, 1), :].rearrange("p j b s -> p j (b s)"),
                                      psV[qq][:, q].rearrange("p (j s) -> p j s", j=2),
                                      rsum[:, q].rearrange("p (j s) -> p j s", j=2), ALU.mult).then_inc(s_ctx, 1)

                maximum_a(0, 0)
                misc(3, "Q", 0, 1, BANKS0[3])
                maximum_b(0, 0)
                dve.memset(KTlo[0][64:P, :].bitcast(F32), 1.0)
                maximum_a(0, 1)
                misc(4, "Q", 0, 2, BANKS0[4])
                dve.memset(KTlo[1][64:P, :].bitcast(F32), 1.0)
                maximum_b(0, 1)
                misc(5, "Q", 0, 3, BANKS0[5])
                maximum_a(1, 0)

                def turn(i, last, steps):
                    for pt in steps:
                        n = i * PB + pt
                        const = isinstance(n, int)
                        more = pt < PB - (1 if last else 0)
                        if more:
                            maximum_b(n + 1, 0)
                        if not (const and n < 4):
                            q = (pt - 4) // 2
                            quotient(i * (PB // 2) + q, i * BODY + q // 2, q % 2, pt % 2)
                        if more:
                            maximum_a(n + 1, 1)
                        if more:
                            maximum_b(n + 1, 1)
                        if pt < PB - (2 if last else 0):
                            maximum_a(n + 2, 0)
                        if not (const and n == 0) and pt < PB + 1:
                            sum_tiles(n - 1, pt - 1, i * (PB // 2) + (pt - 1) // 2)
                        if pt < PB:
                            misc_dve(i, pt, last)
                turn(0, False, range(PB))
                with dve.Fori(1, TURNS - 1) as i:
                    turn(i, False, range(PB))
                turn(TURNS - 1, True, range(PB + 4))

        s_o, s_x = sem("o"), sem("x")
        psO = [psS, psM]
        with nc.Block() as block:
            @block.tensor
            def _(pe):
                for t in range(TILES):
                    if t >= 2:
                        pe.wait_ge(s_x, t - 1)
                    for pj in range(8):
                        last = pe.matmul(psO[t % 2][:, 0:HID],
                                         ctx_all[:, pj, 2 * t:2 * t + 2, :].rearrange("p b s -> p (b s)"),
                                         V[:, pj, :], start=(pj == 0), stop=(pj == 7))
                    last.then_inc(s_o, 1)

            @block.vector
            def _(dve):
                for t in range(TILES):
                    dve.wait_ge(s_o, t + 1)
                    dve.tensor_tensor(X[:, t, :], X[:, t, :], psO[t % 2][:, 0:HID], ALU.add).then_inc(s_x, 1)
def head_attention(nc, sems, name, X, qin, ident, wq, s_w, mask_value, keys, values, out_w):
    shared = values is None
    with ExitStack() as ctx:
        sb = lambda n, s, d=F32: ctx.enter_context(nc.sbuf_tensor(f"{name}_{n}", s, d))
        sem = lambda n: sems(f"{name}_{n}")
        ps = lambda n: ctx.enter_context(nc.psum_tensor(f"{name}_{n}", [P, BLK], F32))
        HPC = HEADS // HC
        PAIRS = HEADS // 2
        scale = 1.0 / float(DH) ** 0.5
        wk, kin, wv = keys
        kdim = kin.shape[0]
        qT = sb("qT", [P, HC, TOK])
        kT = sb("kT", [P, HC, TOK])
        kblk = sb("kblk", [P, HC, BATCH, HPC, SEQ])
        headmask = sb("headmask", [P, HPC])
        identb = sb("identb", [P, P], BF16)
        causal = sb("causal", [P, HPC, SEQ], BF16)
        D = [sb(f"D{i}", [P, HEADS, SEQ]) for i in range(2)]
        E = [sb(f"E{i}", [P, HEADS, SEQ]) for i in range(2)]
        mx, sm, rs = (sb(n, [P, HEADS]) for n in ("mx", "sm", "rs"))
        if shared:
            v = sb("v", [P, TILES, HID])
            pbar = sb("pbar", [P, 2, SEQ])
            pbT = sb("pbT", [P, P])
            blockmask = sb("blockmask", [P, P])
        else:
            vblk = sb("vblk", [P, BATCH, PAIRS, 2, DH])
            AT = sb("AT", [P, PAIRS, P])
            Os = sb("Os", [P, HID])
        scratch = sb("scratch", [P, 1])
        oT = sb("oT", [P, HC, P])
        psP = [ps("psP0"), ps("psP1")]
        psS = [[ps(f"psS{i}{c}") for c in range(HC)] for i in range(2)]
        psT = [ps("psT0"), ps("psT1")]
        s_pool, s_c2, s_z, s_p, s_pe, s_kb, s_kbp, s_s, s_dch, s_D, s_E, s_rs, s_En, s_free = (
            sem(n) for n in ("pool", "c2", "z", "p", "pe", "kb", "kbp", "s", "dch", "D", "E", "rs", "En", "free"))
        s_a, s_ae, s_b, s_be, s_o, s_oe, s_f, s_fe = (sem(n) for n in ("a", "ae", "b", "be", "o", "oe", "f", "fe"))
        s_D2 = sem("D2")
        NV = TILES if shared else BATCH // 2

        def steps(T):
            return [(k, T - k) for k in range(5) if 0 <= T - k < TILES]

        with nc.Block() as block:
            @block.gpsimd
            def _(pool):
                link = chain(pool, s_pool)
                link(pool.memset(headmask[:, :], 1.0))
                link(pool.memset(causal[:, :, :], 0.0))
                if shared:
                    link(pool.memset(blockmask[:, :], 0.0))
                    for k in range(2):
                        link(pool.memset(blockmask[64 * k:64 * k + 64, 64 * k:64 * k + 64], 1.0))
                else:
                    pool.memset(vblk[:, :, :, :, :], 0.0).then_inc(s_z, 1)
                link(pool.affine_select(out=headmask[:, :], in_=headmask[:, :], compare_op=ALU.is_ge, fill=0.0,
                                        base=0, pattern=[[-DH, HPC]], channel_multiplier=1))
                link(pool.affine_select(out=headmask[:, :], in_=headmask[:, :], compare_op=ALU.is_ge, fill=0.0,
                                        base=DH - 1, pattern=[[DH, HPC]], channel_multiplier=-1))
                for k in range(2):
                    link(pool.affine_select(out=causal[64 * k:64 * k + 64], in_=causal[64 * k:64 * k + 64],
                                            compare_op=ALU.is_ge, fill=mask_value, base=0,
                                            pattern=[[0, HPC], [-1, SEQ]], channel_multiplier=1))
                pool.memset(scratch[:, :], 0.0).then_inc(s_c2, 1)
                for blk in range(2):
                    pool.wait_ge(s_pe, (0 if shared else 4) + 2 * (blk + 1))
                    for b in range(8 * blk + 1, 8 * blk + 8, 2):
                        for c in range(HC):
                            last = pool.tensor_tensor(
                                kblk[:, c, b, :, :],
                                kT[:, c, b * SEQ:(b + 1) * SEQ].unsqueeze(1).broadcast_to([P, HPC, SEQ]),
                                headmask[:, :].unsqueeze(2).broadcast_to([P, HPC, SEQ]), ALU.mult)
                        last.then_inc(s_kbp, 1)
                for T in range(TILES):
                    pool.wait_ge(s_rs, T + 1)
                    e = E[T % 2]
                    pool.tensor_tensor(e[:, :, :], e[:, :, :], rs[:, :].unsqueeze(2).broadcast_to([P, HEADS, SEQ]),
                                       ALU.mult).then_inc(s_En, 1)

            @block.tensor
            def _(pe):
                n = 0

                def bank():
                    if n >= 2:
                        pe.wait_ge(s_pe, n - 1)
                    return psP[n % 2]
                for s in s_w:
                    pe.wait_ge(s, 16)
                for w, rhs, kk in ((wk, kin, kdim), (wq, qin, P)) if shared else ((wq, qin, P), (wk, kin, kdim)):
                    for blk in range(2):
                        for oc in range(HC):
                            o = bank()
                            ics = range(HC) if kk == P else range(1)
                            for ic in ics:
                                m = rhs[:, ic, blk * BLK:(blk + 1) * BLK] if kk == P else rhs[:, blk * BLK:(blk + 1) * BLK]
                                l = w[:, ic, oc * P:(oc + 1) * P] if kk == P else w[:, oc * P:(oc + 1) * P]
                                last = pe.matmul(o[:, :], l, m, start=(ic == 0), stop=(ic == ics[-1]))
                            last.then_inc(s_p, 1)
                            n += 1
                for g in range(0 if shared else NV):
                    o = bank()
                    for k in range(4):
                        bb, half = k // 2, k % 2
                        b = 2 * g + bb
                        last = pe.matmul(o[64 * half:64 * half + 64, bb * HID:(bb + 1) * HID],
                                         kin[:, b * SEQ:(b + 1) * SEQ], wv[:, :], start=True, stop=True)
                    last.then_inc(s_p, 1)
                    n += 1
                pe.wait_ge(s_pe, n)
                pe.wait_ge(s_c2, 1)
                pe.wait_ge(s_z, 1 if shared else 2)

                def values(g):
                    pe.wait_ge(s_pe, n + g)
                    for ic in range(HC):
                        last = pe.matmul(psP[1][:, 0:HID], qin[:, ic, g * P:(g + 1) * P], wv[:, ic, :],
                                         start=(ic == 0), stop=(ic == HC - 1))
                    last.then_inc(s_p, 1)

                def tail(k, T):
                    if k == 1 and shared:
                        pe.wait_ge(s_a, T + 1)
                        if T:
                            pe.wait_ge(s_ae, T)
                        pe.transpose(psT[0][:, 0:P], pbar[:, :, :].rearrange("p a k -> p (a k)"),
                                     ident[:, :]).then_inc(s_b, 1)
                    elif k == 1:
                        pe.wait_ge(s_En, T + 1)
                        for g in range(2):
                            if T:
                                pe.wait_ge(s_ae, 2 * T - 1 + g)
                            for j in range(4):
                                last = pe.transpose(psT[g][:, j * P:(j + 1) * P],
                                                    E[T % 2][:, 8 * g + 2 * j:8 * g + 2 * j + 2, :].rearrange(
                                                        "p h k -> p (h k)"), ident[:, :])
                            last.then_inc(s_b, 1)
                    elif k == 2 and shared:
                        pe.wait_ge(s_pe, n + T + 1)
                        pe.wait_ge(s_ae, T + 1)
                        if T:
                            pe.wait_ge(s_oe, T)
                        for c in range(HC):
                            last = pe.matmul(psT[1][:, c * P:(c + 1) * P], v[:, T, c * P:(c + 1) * P], pbT[:, :],
                                             start=True, stop=True)
                        last.then_inc(s_o, 1)
                    elif k == 2:
                        pe.wait_ge(s_ae, 2 * T + 2)
                        if T:
                            pe.wait_ge(s_o, T)
                        for p in range(PAIRS):
                            for bb in range(2):
                                last = pe.matmul(psP[0][64 * bb:64 * bb + 64, 32 * p:32 * p + 32],
                                                 AT[:, p, 64 * bb:64 * bb + 64],
                                                 vblk[:, 2 * T + bb, p, :, :].rearrange("p a d -> p (a d)"),
                                                 start=True, stop=True)
                        last.then_inc(s_be, 1)
                    elif k == 3 and not shared:
                        pe.wait_ge(s_o, T + 1)
                        if T:
                            pe.wait_ge(s_oe, T)
                        if T >= 2:
                            pe.wait_ge(s_fe, T - 1)
                        for c in range(HC):
                            last = pe.transpose(psP[1][:, c * P:(c + 1) * P], Os[:, c * P:(c + 1) * P], ident[:, :])
                        last.then_inc(s_D2, 1)
                    elif k == 4 and not shared:
                        pe.wait_ge(s_oe, T + 1)
                        if T:
                            pe.wait_ge(s_fe, T)
                        for c in range(HC):
                            last = pe.matmul(psP[1][:, HID:2 * HID], oT[:, c, :], out_w[:, c, :],
                                             start=(c == 0), stop=(c == HC - 1))
                        last.then_inc(s_f, 1)
                    elif k == 3 and shared:
                        pe.wait_ge(s_oe, T + 1)
                        if T:
                            pe.wait_ge(s_fe, T)
                        for c in range(HC):
                            last = pe.matmul(psP[0][:, 0:HID], oT[:, c, :], out_w[:, c, :],
                                             start=(c == 0), stop=(c == HC - 1))
                        last.then_inc(s_f, 1)

                def scores(T):
                    pe.wait_ge(s_kb, T + 1)
                    pe.wait_ge(s_kbp, T + 1)
                    if T >= 2:
                        pe.wait_ge(s_D, T - 1)
                    for c in range(HC):
                        for bb in range(2):
                            pe.matmul(psS[T % 2][c][64 * bb:64 * bb + 64, :], identb[:, 64 * bb:64 * bb + 64],
                                      causal[:, :, :].rearrange("p h k -> p (h k)"), start=True, stop=False)
                        for bb in range(2):
                            b = 2 * T + bb
                            last = pe.matmul(psS[T % 2][c][64 * bb:64 * bb + 64, :],
                                             qT[:, c, b * SEQ:(b + 1) * SEQ],
                                             kblk[:, c, b, :, :].rearrange("p h k -> p (h k)"),
                                             start=False, stop=True)
                    last.then_inc(s_s, 1)

                scores(0)
                for step in range(TILES + 4):
                    for k, T in steps(step):
                        if k >= 3:
                            tail(k, T)
                    if step + 1 < TILES:
                        scores(step + 1)
                    if shared and step < TILES:
                        values(step)
                    for k, T in reversed(steps(step)):
                        if k in (1, 2):
                            tail(k, T)

            @block.scalar
            def _(act):
                n = 0
                for dst in (kT, qT) if shared else (qT, kT):
                    for blk in range(2):
                        for oc in range(HC):
                            act.wait_ge(s_p, n + 1)
                            act.activation(dst[:, oc, blk * BLK:(blk + 1) * BLK], psP[n % 2][:, :],
                                           ACT.Copy).then_inc(s_pe, 1)
                            n += 1
                if not shared:
                    act.wait_ge(s_z, 2)
                for g in range(0 if shared else NV):
                    act.wait_ge(s_p, n + 1)
                    for half in range(2):
                        src_ = psP[n % 2][64 * half:64 * half + 64, :].rearrange(
                            "p (b j a d) -> p b j a d", b=2, j=PAIRS, a=2)
                        for bb in range(2):
                            last = act.activation(vblk[64 * half:64 * half + 64, 2 * g + bb, :, half, :],
                                                  src_[:, bb, :, half, :], ACT.Copy)
                    last.then_inc(s_pe, 1)
                    n += 1

                for step in range(TILES + 4):
                    for k, T in steps(step):
                        if k == 0:
                            act.wait_ge(s_D, T + 1)
                            if T >= 2:
                                if shared:
                                    act.wait_ge(s_a, T - 1)
                                else:
                                    act.wait_ge(s_b, 2 * T - 2)
                            act.activation(E[T % 2][:, :, :], D[T % 2][:, :, :], ACT.Exp, scale=scale).then_inc(s_E, 1)
                            if shared:
                                act.wait_ge(s_p, n + T + 1)
                                act.activation(v[:, T, :], psP[1][:, 0:HID], ACT.Copy).then_inc(s_pe, 1)
                        elif k == 1 and not shared:
                            if T:
                                act.wait_ge(s_be, T)
                            for g in range(2):
                                act.wait_ge(s_b, 2 * T + g + 1)
                                act.activation(AT[:, 4 * g:4 * g + 4, :].rearrange("p j q -> p (j q)"), psT[g][:, :],
                                               ACT.Copy).then_inc(s_ae, 1)
                        elif k == 2 and shared:
                            act.wait_ge(s_o, T + 1)
                            if T:
                                act.wait_ge(s_f, T)
                            act.activation(oT[:, :, :].rearrange("p c t -> p (c t)"), psT[1][:, 0:HID],
                                           ACT.Copy).then_inc(s_oe, 1)
                        elif k == 2:
                            act.wait_ge(s_be, T + 1)
                            if T:
                                act.wait_ge(s_D2, T)
                            act.activation(Os[:, :], psP[0][:, 0:HID], ACT.Copy).then_inc(s_o, 1)

            @block.vector
            def _(dve):
                link = chain(dve, s_dch)
                dve.tensor_copy(identb[:, :], ident[:, :]).then_inc(s_z, 1)
                dve.wait_ge(s_c2, 1)
                for blk in range(2):
                    dve.wait_ge(s_pe, (0 if shared else 4) + 2 * (blk + 1))
                    for b in range(8 * blk, 8 * blk + 8, 2):
                        for c in range(HC):
                            last = dve.tensor_tensor(
                                kblk[:, c, b, :, :],
                                kT[:, c, b * SEQ:(b + 1) * SEQ].unsqueeze(1).broadcast_to([P, HPC, SEQ]),
                                headmask[:, :].unsqueeze(2).broadcast_to([P, HPC, SEQ]), ALU.mult)
                        last.then_inc(s_kb, 1)

                for step in range(TILES + 4):
                    for k, T in steps(step):
                        if k == 0:
                            s3 = [psS[T % 2][c][:, :].rearrange("p (h k) -> p h k", h=HPC) for c in range(HC)]
                            dve.wait_ge(s_s, T + 1)
                            for c in range(HC):
                                last = dve.tensor_reduce(mx[:, c * HPC:(c + 1) * HPC], s3[c], AX.X, ALU.max)
                            link(last)
                            if T >= 2:
                                dve.wait_ge(s_E, T - 1)
                            for c in range(HC):
                                last = dve.tensor_tensor(D[T % 2][:, c * HPC:(c + 1) * HPC, :], s3[c],
                                                         mx[:, c * HPC:(c + 1) * HPC].unsqueeze(2).broadcast_to(
                                                             [P, HPC, SEQ]), ALU.subtract)
                            last.then_inc(s_D, 1)
                        if k == 3 and not shared:
                            dve.wait_ge(s_D2, T + 1)
                            if T:
                                dve.wait_ge(s_f, T)
                            dve.tensor_copy(oT[:, :, :].rearrange("p c t -> p (c t)"),
                                            psP[1][:, 0:HID]).then_inc(s_oe, 1)
                        if k == (3 if shared else 4):
                            dve.wait_ge(s_f, T + 1)
                            o = psP[0][:, 0:HID] if shared else psP[1][:, HID:2 * HID]
                            dve.tensor_tensor(X[:, T, :], X[:, T, :], o, ALU.add).then_inc(s_fe, 1)
                    for k, T in steps(step):
                        if k == 1 and shared:
                            dve.wait_ge(s_En, T + 1)
                            if T:
                                dve.wait_ge(s_b, T)
                            for a in range(2):
                                last = dve.tensor_reduce(pbar[:, a, :], E[T % 2][:, :, :].rearrange("p h k -> p k h"),
                                                         AX.X, ALU.add) if a == 0 else \
                                    dve.tensor_copy(pbar[:, 1, :], pbar[:, 0, :])
                                if a == 0:
                                    link(last)
                            last.then_inc(s_a, 1)
                    for k, T in steps(step):
                        if k == 0:
                            dve.wait_ge(s_E, T + 1)
                            link(dve.tensor_reduce(sm[:, :], E[T % 2][:, :, :], AX.X, ALU.add))
                            if T:
                                dve.wait_ge(s_En, T)
                            dve.reciprocal(rs[:, :], sm[:, :]).then_inc(s_rs, 1)
                    for k, T in steps(step):
                        if k == 1 and shared:
                            dve.wait_ge(s_b, T + 1)
                            if T:
                                dve.wait_ge(s_o, T)
                            dve.tensor_tensor(pbT[:, :], psT[0][:, 0:P], blockmask[:, :], ALU.mult).then_inc(s_ae, 1)
def experts(nc, sems, name, X, xhi, xlo, ident, stream, router, E, K, NT, gated, out=None, s_out=None):
    with ExitStack() as ctx:
        sb = lambda n, s, d=F32: ctx.enter_context(nc.sbuf_tensor(f"{name}_{n}", s, d))
        sem = lambda n: sems(f"{name}_{n}")
        ps = lambda n: ctx.enter_context(nc.psum_tensor(f"{name}_{n}", [P, BLK], F32))
        EW = router.shape[-1]
        SW = 6 * P
        WW = SW + P
        Wraw = [sb(f"Wraw{i}", [P, WW]) for i in range(2)]
        Whi = [sb(f"Whi{i}", [P, WW], F32R) for i in range(2)]
        Wlo = [sb(f"Wlo{i}", [P, SW], F32R) for i in range(2)]
        rw = sb("rw", [P, HC, EW])
        rhi, rlo = sb("rhi", [P, HC, EW], F32R), sb("rlo", [P, HC, EW], F32R)
        L = sb("L", [P, TILES, EW])
        LT = sb("LT", [P, TOK])
        m8 = sb("m8", [P, TILES, 8])
        gt, eq, cum, rst, ex = (sb(n, [P, TILES, E]) for n in ("gt", "eq", "cum", "rst", "ex"))
        need, ssum, rsum, sg = (sb(n, [P, TILES]) for n in ("need", "ssum", "rsum", "sg"))
        cmb = [sb(f"cmb{i}", [P, TILES, P]) for i in range(2 if gated else 1)]
        cT = [sb(f"cT{i}", [P, TOK], F32R) for i in range(2 if gated else 1)]
        a = [sb(f"a{i}", [P, BLK]) for i in range(2)]
        t = sb("t", [P, BLK])
        h = [sb(f"h{i}", [P, BLK]) for i in range(2)]
        hhi = [sb(f"hhi{i}", [P, BLK], F32R) for i in range(2)]
        hlo = [sb(f"hlo{i}", [P, BLK], F32R) for i in range(2)]
        yT = sb("yT", [P, HC, TOK])
        acc = [[ps(f"acc{o}{b}") for b in range(2)] for o in range(HC)]
        psG = [ps("psG0"), ps("psG1")]
        psU, psC = ps("psU"), ps("psC")
        s_wr = [sem(f"wr{i}") for i in range(2)]
        (s_r, s_rs, s_l, s_le, s_dch, s_z, s_e, s_c, s_ct, s_cte, s_whi, s_wlo, s_g, s_u, s_cc, s_a, s_t, s_h, s_hhi,
         s_hlo, s_d, s_y, s_ye, s_yv, s_tr, s_x) = (
            sem(n) for n in ("r", "rs", "l", "le", "dch", "z", "e", "c", "ct", "cte", "whi", "wlo", "g", "u", "cc",
                             "a", "t", "h", "hhi", "hlo", "d", "y", "ye", "yv", "tr", "x"))
        s_lt, s_lte = sem("lt"), sem("lte")
        NC = len(cT)
        LAST = NT - 1

        def tiles(eng, body):
            for j in range(3):
                body(j, j % 2)
            with eng.Fori(1, (NT - 3) // 2) as i:
                body(2 * i + 1, 1)
                body(2 * i + 2, 0)
            body(LAST - 1, 1)
            body(LAST, 0)

        with nc.Block() as block:
            @block.sync
            def _(sp):
                sp.dma_start(rw[:], router).then_inc(s_r, 16)

                def load(j, slot):
                    if not isinstance(j, int) or j >= 2:
                        sp.wait_ge(s_wlo, j - 1)
                    sp.dma_start(Wraw[slot][:, :], stream[j]).then_inc(s_wr[slot], 16)
                tiles(sp, load)
                if out is not None:
                    view = out.rearrange("(t p) h -> p t h", p=P)
                    for T in range(TILES):
                        sp.wait_ge(s_x, T + 1)
                        sp.dma_start(view[:, T, :], X[:, T, :]).then_inc(s_out, 16)
                    sp.wait_ge(s_out, 16 * TILES)

            @block.gpsimd
            def _(pool):
                pool.memset(LT[:, :], 0.0).then_inc(s_z, 1)
                pool.memset(rst[:, :, :], 1.0).then_inc(s_z, 1)
                for c in cmb:
                    pool.memset(c[:, :, :], 0.0).then_inc(s_z, 1)
                pool.wait_ge(s_z, 2 + NC)
                pool.memset(rst[:, :, 0:1], 0.0).then_inc(s_z, 1)
                if not gated:
                    pool.memset(cmb[0][:, :, E:E + 1], 1.0).then_inc(s_z, 1)

                def split_lo(j, slot):
                    pool.wait_ge(s_whi, j + 1)
                    pool.tensor_tensor(Wlo[slot][:, :], Wraw[slot][:, 0:SW], Whi[slot][:, 0:SW].bitcast(F32),
                                       ALU.subtract).then_inc(s_wlo, 1)

                def tile(j, slot):
                    for blk in range(2):
                        r = 2 * j + blk
                        pool.wait_ge(s_hhi, r + 1)
                        pool.tensor_tensor(hlo[blk][:, :], h[blk][:, :], hhi[blk][:, :].bitcast(F32),
                                           ALU.subtract).then_inc(s_hlo, 1)
                        if blk == 0 and not (isinstance(j, int) and j == LAST):
                            split_lo(j + 1, 1 - slot)
                split_lo(0, 0)
                tiles(pool, tile)

            @block.tensor
            def _(pe):
                pe.wait_ge(s_rs, 1)
                for blk in range(2):
                    tok = slice(blk * BLK, blk * BLK + BLK)
                    n = 0
                    for c in range(HC):
                        for x, w in ((xhi, rhi), (xhi, rlo), (xlo, rhi)):
                            last = pe.matmul(acc[0][blk][0:EW, :], w[:, c, :], x[:, c, tok], start=(n == 0), stop=(n == 5))
                            n += 1
                    last.then_inc(s_lt, 1)
                for blk in range(2):
                    pe.wait_ge(s_lte, blk + 1)
                    for q in range(4):
                        last = pe.transpose(acc[1][blk][:, q * P:(q + 1) * P], LT[:, blk * BLK + q * P:blk * BLK + q * P + P],
                                            ident[:, :])
                    last.then_inc(s_l, 1)

                def product3(o, whi, wlo, cols, xh, xl, start, stop, n0, n1):
                    n = n0
                    for (w, x) in ((whi, xh), (whi, xl), (wlo, xh)):
                        last = pe.matmul(o, w[:, cols], x, start=start and n == 0, stop=stop and n == n1)
                        n += 1
                    return last

                def gate_or_up(o, slot, k, tok, signal):
                    for c in range(HC):
                        cols = slice((2 * k + c) * P, (2 * k + c + 1) * P)
                        last = product3(o[:, :], Whi[slot], Wlo[slot], cols, xhi[:, c, tok], xlo[:, c, tok],
                                        True, True, 3 * c, 5)
                    last.then_inc(signal, 1)

                pe.wait_ge(s_wlo, 1)
                gate_or_up(psG[0], 0, 0, slice(0, BLK), s_g)
                gate_or_up(psU, 0, 1, slice(0, BLK), s_u)
                gate_or_up(psG[1], 0, 0, slice(BLK, TOK), s_g)
                pe.wait_ge(s_c, 1)
                pe.wait_ge(s_le, 2)
                banks = [acc[0][0], acc[0][1], acc[1][0], acc[1][1]]
                for k in range(NC):
                    for half in range(2):
                        for q in range(4):
                            last = pe.transpose(banks[2 * k + half][:, q * P:(q + 1) * P], cmb[k][:, 4 * half + q, :],
                                                ident[:, :])
                        last.then_inc(s_ct, 1)
                pe.wait_ge(s_cte, 2 * NC)

                def down(r_done, slot, blk, first, final):
                    pe.wait_ge(s_hlo, r_done)
                    for oc in range(HC):
                        cols = slice(4 * P + oc * P, 5 * P + oc * P)
                        last = product3(acc[oc][blk][:, :], Whi[slot], Wlo[slot], cols, hhi[blk][:, :], hlo[blk][:, :],
                                        first, final, 0, 2)
                    last.then_inc(s_d, 1)

                def tile(j, slot):
                    const = isinstance(j, int)
                    for blk in range(2):
                        r = 2 * j + blk
                        tok = slice(blk * BLK, blk * BLK + BLK)
                        if not (const and r < 2):
                            if blk == 0:
                                pe.wait_ge(s_wlo, j + 1)
                            pe.wait_ge(s_a, r - 1)
                            gate_or_up(psG[blk], slot, 0, tok, s_g)
                        if not (const and r == 0):
                            pe.wait_ge(s_t, r)
                            gate_or_up(psU, slot, 1, tok, s_u)
                        if not (const and r == 0):
                            pe.wait_ge(s_h, r)
                        which = cT[1] if gated and const and j == LAST else cT[0]
                        pe.matmul(psC[:, :], Whi[slot][:, SW:WW], which[:, tok], start=True, stop=True).then_inc(s_cc, 1)
                        if not (const and r == 0):
                            down(r, slot if blk else 1 - slot, 1 - blk, const and r <= 2, const and r - 1 >= 2 * LAST)
                tiles(pe, tile)
                down(2 * NT, 0, 1, False, True)

                banks = [psG[0], psG[1], psU, psC]
                for T in range(TILES):
                    if T == 0:
                        pe.wait_ge(s_h, 2 * NT)
                    if T % 4 == 0:
                        pe.wait_ge(s_ye, T // 4 + 1)
                        pe.wait_ge(s_yv, T // 4 + 1)
                    if T >= 4:
                        pe.wait_ge(s_x, T - 3)
                    for c in range(HC):
                        last = pe.transpose(banks[T % 4][:, c * P:(c + 1) * P], yT[:, c, T * P:(T + 1) * P], ident[:, :])
                    last.then_inc(s_tr, 1)

            @block.scalar
            def _(act):
                def split_hi(j, slot):
                    if isinstance(j, int):
                        act.wait_ge(s_wr[slot], 16 * (j // 2 + 1))
                    else:
                        act.wait_ge(s_wr[slot], 8 * (j - slot) + 16)
                    if not isinstance(j, int) or j >= 2:
                        act.wait_ge(s_d, 2 * j - 2)
                    act.activation(Whi[slot][:, :], Wraw[slot][:, :], ACT.Copy).then_inc(s_whi, 1)

                act.wait_ge(s_z, 1)
                for blk in range(2):
                    act.wait_ge(s_lt, blk + 1)
                    act.activation(LT[0:EW, blk * BLK:(blk + 1) * BLK], acc[0][blk][0:EW, :], ACT.Copy).then_inc(s_lte, 1)
                for blk in range(2):
                    act.wait_ge(s_l, blk + 1)
                    act.activation(L[:, 4 * blk:4 * blk + 4, :],
                                   acc[1][blk][:, :].rearrange("p (t e) -> p t e", t=4)[:, :, 0:EW],
                                   ACT.Copy).then_inc(s_le, 1)
                split_hi(0, 0)
                act.wait_ge(s_e, 1)
                act.activation(ex[:, :, :], ex[:, :, :], ACT.Exp).then_inc(s_e, 1)
                if gated:
                    act.activation(sg[:, :], L[:, :, E], ACT.Exp, scale=-1.0).then_inc(s_e, 1)
                banks = [acc[0][0], acc[0][1], acc[1][0], acc[1][1]]
                for n in range(2 * NC):
                    act.wait_ge(s_ct, n + 1)
                    act.activation(cT[n // 2][:, (n % 2) * BLK:(n % 2 + 1) * BLK], banks[n][:, :],
                                   ACT.Copy).then_inc(s_cte, 1)

                def tile(j, slot):
                    for blk in range(2):
                        r = 2 * j + blk
                        act.wait_ge(s_g, r + 1)
                        if not (isinstance(j, int) and r < 2):
                            act.wait_ge(s_t, r - 1)
                        act.activation(a[blk][:, :], psG[blk][:, :], ACT.Silu).then_inc(s_a, 1)
                        act.wait_ge(s_h, r + 1)
                        if not (isinstance(j, int) and r < 2):
                            act.wait_ge(s_d, r - 1)
                        act.activation(hhi[blk][:, :], h[blk][:, :], ACT.Copy).then_inc(s_hhi, 1)
                        if blk == 0 and not (isinstance(j, int) and j == LAST):
                            split_hi(j + 1, 1 - slot)
                tiles(act, tile)
                act.wait_ge(s_d, 2 * NT)
                for blk in range(2):
                    act.activation(yT[:, 0, blk * BLK:(blk + 1) * BLK], acc[0][blk][:, :], ACT.Copy).then_inc(s_ye, 1)

            @block.vector
            def _(dve):
                link = chain(dve, s_dch)
                dve.wait_ge(s_r, 16)
                link(dve.tensor_copy(rhi[:, :, :], rw[:, :, :]))
                dve.tensor_tensor(rlo[:, :, :], rw[:, :, :], rhi[:, :, :].bitcast(F32), ALU.subtract).then_inc(s_rs, 1)
                dve.wait_ge(s_le, 2)
                dve.wait_ge(s_z, 3 + NC + (0 if gated else 1))
                for T in range(TILES):
                    last = dve.max(m8[:, T, :], L[:, T, 0:E])
                link(last)
                wide = lambda col: col.broadcast_to([P, TILES, E])
                logits, kth = L[:, :, 0:E], m8[:, :, K - 1:K]
                dve.tensor_tensor(ex[:, :, :], logits, wide(m8[:, :, 0:1]), ALU.subtract).then_inc(s_e, 1)
                dve.tensor_tensor(gt[:, :, :], logits, wide(kth), ALU.is_gt)
                link(dve.tensor_tensor(eq[:, :, :], logits, wide(kth), ALU.is_equal))
                dve.tensor_reduce(need[:, :], gt[:, :, :], AX.X, ALU.add)
                flat = lambda x: x[:, :, :].rearrange("p t e -> p (t e)")
                link(dve.tensor_tensor_scan(flat(cum), flat(rst), flat(eq), 0.0, ALU.mult, ALU.add))
                link(dve.tensor_scalar(need[:, :], need[:, :], -1.0, float(K), ALU.mult, ALU.add))
                link(dve.tensor_tensor(cum[:, :, :], cum[:, :, :], need[:, :].unsqueeze(2).broadcast_to([P, TILES, E]),
                                       ALU.is_le))
                link(dve.tensor_tensor(eq[:, :, :], eq[:, :, :], cum[:, :, :], ALU.mult))
                link(dve.tensor_tensor(gt[:, :, :], gt[:, :, :], eq[:, :, :], ALU.add))
                dve.wait_ge(s_e, 3 if gated else 2)
                link(dve.tensor_tensor(ex[:, :, :], ex[:, :, :], gt[:, :, :], ALU.mult))
                link(dve.tensor_reduce(ssum[:, :], ex[:, :, :], AX.X, ALU.add))
                link(dve.reciprocal(rsum[:, :], ssum[:, :]))
                link(dve.tensor_tensor(ex[:, :, :], ex[:, :, :], rsum[:, :].unsqueeze(2).broadcast_to([P, TILES, E]),
                                       ALU.mult))
                lo0 = E if gated else E + 1
                link(dve.tensor_copy(cmb[0][:, :, 0:E].bitcast(F32R), ex[:, :, :]))
                last = dve.tensor_tensor(cmb[0][:, :, lo0:lo0 + E], ex[:, :, :], cmb[0][:, :, 0:E], ALU.subtract)
                if gated:
                    link(dve.tensor_scalar(sg[:, :], sg[:, :], 1.0, None, ALU.add))
                    link(dve.reciprocal(sg[:, :], sg[:, :]))
                    link(dve.tensor_copy(cmb[1][:, :, 0].bitcast(F32R), sg[:, :]))
                    last = dve.tensor_tensor(cmb[1][:, :, 1], sg[:, :], cmb[1][:, :, 0], ALU.subtract)
                last.then_inc(s_c, 1)

                def tile(j, slot):
                    for blk in range(2):
                        r = 2 * j + blk
                        dve.wait_ge(s_a, r + 1)
                        dve.wait_ge(s_u, r + 1)
                        dve.tensor_tensor(t[:, :], a[blk][:, :], psU[:, :], ALU.mult).then_inc(s_t, 1)
                        dve.wait_ge(s_cc, r + 1)
                        dve.wait_ge(s_t, r + 1)
                        if not (isinstance(j, int) and r < 2):
                            dve.wait_ge(s_hlo, r - 1)
                        dve.tensor_tensor(h[blk][:, :], t[:, :], psC[:, :], ALU.mult).then_inc(s_h, 1)
                tiles(dve, tile)
                dve.wait_ge(s_d, 2 * NT)
                for blk in range(2):
                    dve.tensor_copy(yT[:, 1, blk * BLK:(blk + 1) * BLK], acc[1][blk][:, :]).then_inc(s_yv, 1)
                banks = [psG[0], psG[1], psU, psC]
                for T in range(TILES):
                    dve.wait_ge(s_tr, T + 1)
                    dve.tensor_tensor(X[:, T, :], X[:, T, :], banks[T % 4][:, 0:HID], ALU.add).then_inc(s_x, 1)


def time_mix(nc, sems, X, xT, w, cols, s_w):
    with ExitStack() as ctx:
        sb = lambda n, s, d=F32: ctx.enter_context(nc.sbuf_tensor("tm_" + n, s, d))
        sem = lambda n: sems("tm_" + n)
        full = [P, HC, TOK]
        sx, dx = sb("sx", full), sb("dx", full)
        mixed = [sb("xk", full), sb("xv", full), sb("xr", full)]
        k, v, r = sb("k", full), sb("v", full), sb("r", full)
        decay = sb("decay", [P, HC])
        dec = sb("dec", full)
        norm = sb("norm", [P, HC, TOK])
        num, den = sb("num", [P, HC, TOK + 1]), sb("den", [P, HC, TOK + 1])
        normp = sb("normp", full)
        cn, ep, ec, ed, ek = (sb(n, full) for n in ("cn", "ep", "ec", "ed", "ek"))
        rwkv = sb("rwkv", full)
        bank = [ctx.enter_context(nc.psum_tensor(f"tm_ps{i}", [P, BLK], F32)) for i in range(8)]
        s_dch, s_pch, s_mix, s_pr, s_ev, s_dy, s_np, s_arg, s_exp, s_ekv, s_p2, s_rw, s_o, s_x, s_z, s_den = (
            sem(n) for n in ("dch", "pch", "mix", "pr", "ev", "dy", "np", "arg", "exp", "ekv", "p2", "rw", "o", "x", "z",
                             "den"))
        starts = lambda x, c: x[:, c, :].rearrange("p (b t) -> p b t", t=SEQ)[:, :, 0:1]
        rest = lambda x, c: x[:, c, :].rearrange("p (b t) -> p b t", t=SEQ)[:, :, 1:SEQ]
        before = lambda x, c: x[:, c, :].rearrange("p (b t) -> p b t", t=SEQ)[:, :, 0:SEQ - 1]

        with nc.Block() as block:
            @block.tensor
            def _(pe):
                for g in range(12):
                    m, oc, blk = g // 4, g // 2 % 2, g % 2
                    if g % 4 == 0:
                        pe.wait_ge(s_w[m], 16)
                        pe.wait_ge(s_mix, 2 * m + 2)
                    if g >= 8:
                        pe.wait_ge(s_ev, g - 7)
                    for ic in range(HC):
                        last = pe.matmul(bank[g % 8][:, :], w[m][:, ic, oc * P:(oc + 1) * P],
                                         mixed[m][:, ic, blk * BLK:(blk + 1) * BLK], start=(ic == 0), stop=(ic == HC - 1))
                    last.then_inc(s_pr, 1)
                pe.wait_ge(s_w[3], 16)
                pe.wait_ge(s_ev, 12)
                for c in range(HC):
                    for T in range(TILES):
                        if T % 4 == 0:
                            pe.wait_ge(s_rw, 2 * c + T // 4 + 1)
                        last = pe.matmul(bank[T][:, 0:HID], rwkv[:, c, T * P:(T + 1) * P], w[3][:, c, :],
                                         start=(c == 0), stop=(c == HC - 1))
                        if c == HC - 1:
                            last.then_inc(s_o, 1)

            @block.scalar
            def _(act):
                act.activation(decay[:, :], cols["time_decay"][:, :], ACT.Exp).then_inc(s_dy, 1)
                def projected(groups):
                    for g in groups:
                        m, oc, blk = g // 4, g // 2 % 2, g % 2
                        act.wait_ge(s_pr, g + 1)
                        act.activation((k, v, r)[m][:, oc, blk * BLK:(blk + 1) * BLK], bank[g % 8][:, :],
                                       ACT.Copy if m < 2 else ACT.Sigmoid).then_inc(s_ev, 1)
                projected(range(8))
                for c in range(HC):
                    for n, x in enumerate((ed, ek, ep, ec)):
                        act.wait_ge(s_arg, 4 * c + n + 1)
                        act.activation(x[:, c, :], x[:, c, :], ACT.Exp).then_inc(s_exp, 1)
                projected(range(8, 12))

            @block.gpsimd
            def _(pool):
                for x in (num, den):
                    pool.memset(x[:, :, 0:1], 0.0).then_inc(s_z, 1)
                for c in range(HC):
                    pool.memset(starts(normp, c), NEG).then_inc(s_z, 1)
                pool.wait_ge(s_ev, 8)
                for c in range(HC):
                    pool.wait_ge(s_exp, 4 * c + 2)
                    pool.tensor_tensor(dx[:, c, :], ek[:, c, :], v[:, c, :], ALU.mult).then_inc(s_ekv, 1)
                    pool.wait_ge(s_exp, 4 * c + 4)
                    pool.tensor_tensor(sx[:, c, :], ec[:, c, :], v[:, c, :], ALU.mult).then_inc(s_p2, 1)
                    pool.wait_ge(s_den, c + 1)
                    pool.tensor_tensor(normp[:, c, :], ep[:, c, :], den[:, c, 0:TOK], ALU.mult).then_inc(s_p2, 1)

            @block.vector
            def _(dve):
                link = chain(dve, s_dch)
                for c in range(HC):
                    dve.memset(starts(sx, c), 0.0)
                    dve.tensor_copy(rest(sx, c), before(xT, c))
                link(dve.memset(cn[:, :, 0:1], 0.0))
                link(dve.tensor_tensor(dx[:, :, :], xT[:, :, :], sx[:, :, :], ALU.subtract))
                for m, mix in enumerate(("mix_k", "mix_v", "mix_r")):
                    for c in range(HC):
                        dve.scalar_tensor_tensor(mixed[m][:, c, :], dx[:, c, :], cols[mix][:, c:c + 1], sx[:, c, :],
                                                 ALU.mult, ALU.add).then_inc(s_mix, 1)
                dve.wait_ge(s_dy, 1)
                dve.wait_ge(s_z, 4)
                link(dve.tensor_scalar(decay[:, :], decay[:, :], -1.0, None, ALU.mult))
                for c in range(HC):
                    link(dve.tensor_scalar(dec[:, c, :], xT[:, c, :], 0.0, decay[:, c:c + 1], ALU.mult, ALU.add))
                    link(dve.memset(starts(dec, c), NEG))
                cw = cols["current_token_weight"]
                for c in range(HC):
                    dve.wait_ge(s_ev, 2 * c + 2)
                    link(dve.tensor_tensor_scan(norm[:, c, :], dec[:, c, :], k[:, c, :], NEG, ALU.add, ALU.max))
                    link(dve.tensor_copy(rest(normp, c), before(norm, c)))
                    dve.scalar_tensor_tensor(ed[:, c, :], normp[:, c, :], decay[:, c:c + 1], norm[:, c, :],
                                             ALU.add, ALU.subtract).then_inc(s_arg, 1)
                    dve.tensor_tensor(ek[:, c, :], k[:, c, :], norm[:, c, :], ALU.subtract).then_inc(s_arg, 1)
                    link(dve.scalar_tensor_tensor(cn[:, c, :], k[:, c, :], cw[:, c:c + 1], normp[:, c, :],
                                                  ALU.add, ALU.max))
                    dve.tensor_tensor(ep[:, c, :], normp[:, c, :], cn[:, c, :], ALU.subtract).then_inc(s_arg, 1)
                    dve.scalar_tensor_tensor(ec[:, c, :], k[:, c, :], cw[:, c:c + 1], cn[:, c, :],
                                             ALU.add, ALU.subtract).then_inc(s_arg, 1)
                for c in range(HC):
                    dve.wait_ge(s_exp, 4 * c + 2)
                    dve.tensor_tensor_scan(den[:, c, 1:TOK + 1], ed[:, c, :], ek[:, c, :], 0.0,
                                           ALU.mult, ALU.add).then_inc(s_den, 1)
                    dve.wait_ge(s_ekv, c + 1)
                    link(dve.tensor_tensor_scan(num[:, c, 1:TOK + 1], ed[:, c, :], dx[:, c, :], 0.0,
                                                ALU.mult, ALU.add))
                    dve.wait_ge(s_exp, 4 * c + 4)
                    link(dve.tensor_tensor(cn[:, c, :], ep[:, c, :], num[:, c, 0:TOK], ALU.mult))
                    dve.wait_ge(s_p2, 2 * c + 1)
                    link(dve.tensor_tensor(cn[:, c, :], cn[:, c, :], sx[:, c, :], ALU.add))
                    dve.wait_ge(s_p2, 2 * c + 2)
                    link(dve.tensor_tensor(dec[:, c, :], normp[:, c, :], ec[:, c, :], ALU.add))
                    for blk in range(2):
                        tok = slice(blk * BLK, blk * BLK + BLK)
                        link(dve.reciprocal(dec[:, c, tok], dec[:, c, tok]))
                        link(dve.tensor_tensor(cn[:, c, tok], cn[:, c, tok], dec[:, c, tok], ALU.mult))
                        dve.wait_ge(s_ev, 12)
                        dve.tensor_tensor(rwkv[:, c, tok], cn[:, c, tok], r[:, c, tok], ALU.mult).then_inc(s_rw, 1)
                for T in range(TILES):
                    dve.wait_ge(s_o, T + 1)
                    dve.tensor_tensor(X[:, T, :], X[:, T, :], bank[T][:, 0:HID], ALU.add).then_inc(s_x, 1)


def perceiver(nc, src, out):
    with ExitStack() as top:
        sb = lambda n, s, d=F32: top.enter_context(nc.sbuf_tensor(n, s, d))
        sem = lambda n: nc.alloc_semaphore(n)
        sems = Semaphores(nc)
        X = sb("X", [P, TILES, HID])
        ident = sb("ident", [P, P])
        s_x = [sem(f"x_in{k}") for k in range(2)]
        s_const, s_out = sem("const"), sem("out")
        x_view = src["x"].rearrange("(t p) h -> p t h", p=P)

        with ExitStack() as ctx:
            s1 = lambda n, s, d=F32: ctx.enter_context(nc.sbuf_tensor(n, s, d))
            xnT = s1("xnT", [P, HC, TOK])
            M = s1("M", [P, HC, HEADS, DC])
            V = s1("V", [P, 8, HID])
            cosN, sinN = s1("cosN", [P, KT, DC]), s1("sinN", [P, KT, DC])
            raw = s1("raw", [P, KT, DC])
            KV = [s1(f"KV{i}", [P, KT + 1, DC]) for i in range(4)]
            s_raw = sems("raw")
            s_tab = sems("rope_tables")
            rope, s_rope = make_rope(nc, sems, ctx, raw, s_raw, cosN, sinN, KV)
            with ExitStack() as wctx:
                w = latent_weight_buffers(nc, wctx)
                s_w = {n: sems("w_" + n) for n in w}
                with nc.Block() as block:
                    @block.gpsimd
                    def _(pool):
                        pool.memset(ident[:, :], 0.0).then_inc(s_const, 1)
                        pool.wait_ge(s_const, 1)
                        pool.affine_select(out=ident[:, :], in_=ident[:, :], compare_op=ALU.not_equal, fill=1.0,
                                           base=0, pattern=[[-1, P]], channel_multiplier=1)
                        pool.memset(raw[:, KT - 1, :], 0.0)
                        for t in KV:
                            pool.memset(t[:, KT, :], 0.0)

                    @block.sync
                    def _(sp):
                        for k in range(2):
                            sp.dma_start(X[:, 4 * k:4 * k + 4, :], x_view[:, 4 * k:4 * k + 4, :]).then_inc(s_x[k], 16)

                def loads(sp):
                    for n in ("wqrT", "wkrT"):
                        sp.dma_start(w[n][:], src[n]).then_inc(s_w[n], 16)
                    sp.dma_start(cosN[:], src["cosN"]).then_inc(s_tab, 16)
                    sp.dma_start(sinN[:], src["sinN"]).then_inc(s_tab, 16)
                    load_latents(sp, src, raw, s_raw, 0)
                    for n in ("wkcqT", "wq", "wkckv", "woT"):
                        sp.dma_start(w[n][:], src[n]).then_inc(s_w[n], 16)
                    sp.wait_ge(s_tab, 32)
                layernorm(nc, sems, "ln0", X, ident, (xnT,), loads=loads, x_load=s_x)
                latent_weights(nc, sems, ident, M, V, w, s_w, src, raw, s_raw, rope, s_rope)
            latent_attention(nc, sems, X, xnT, ident, M, V, src, raw, s_raw, KV, rope, s_rope)
            sems.recycle()

        with ExitStack() as ctx:
            s2 = lambda n, s, d=F32: ctx.enter_context(nc.sbuf_tensor(n, s, d))
            xnT = s2("a0_xnT", [P, HC, TOK])
            w = {n: s2(n, [P, HC, HID]) for n in ("a0_wq", "a0_wk", "a0_wv", "a0_wo")}
            s_w = {n: sems("w_" + n) for n in w}

            def loads(sp):
                for n in w:
                    sp.dma_start(w[n][:], src[n]).then_inc(s_w[n], 16)
            layernorm(nc, sems, "ln1", X, ident, (xnT,), loads=loads)
            head_attention(nc, sems, "a0", X, xnT, ident, w["a0_wq"], list(s_w.values()), -1.0e9,
                           (w["a0_wk"], xnT, w["a0_wv"]), None, w["a0_wo"])
        with ExitStack() as ctx:
            s3 = lambda n, s, d=F32: ctx.enter_context(nc.sbuf_tensor(n, s, d))
            xhi, xlo = s3("f0_xhi", [P, HC, TOK], F32R), s3("f0_xlo", [P, HC, TOK], F32R)
            layernorm(nc, sems, "ln2", X, ident, (xhi, xlo))
            experts(nc, sems, "f0", X, xhi, xlo, ident, src["f0_stream"], src["f0_router"], 16, 4, 25, False)
            sems.recycle()

        with ExitStack() as ctx:
            s4 = lambda n, s, d=F32: ctx.enter_context(nc.sbuf_tensor(n, s, d))
            xnT = s4("x1_xnT", [P, HC, TOK])
            w = {n: s4(n, [P, HC, HID]) for n in ("x1_wq", "x1_wo")}
            w.update({n: s4(n, [DC, HID]) for n in ("x1_wk", "x1_wv")})
            w["x1_lat"] = s4("x1_lat", [DC, TOK])
            s_w = {n: sems("w_" + n) for n in w}

            def loads(sp):
                for n in w:
                    sp.dma_start(w[n][:], src[n]).then_inc(s_w[n], 16)
            layernorm(nc, sems, "ln3", X, ident, (xnT,), loads=loads)
            head_attention(nc, sems, "x1", X, xnT, ident, w["x1_wq"], list(s_w.values()), NEG,
                           (w["x1_wk"], w["x1_lat"], w["x1_wv"]), "latent", w["x1_wo"])

        with ExitStack() as ctx:
            s5 = lambda n, s, d=F32: ctx.enter_context(nc.sbuf_tensor(n, s, d))
            xT = s5("tm_xT", [P, HC, TOK])
            w = [s5(f"tm_w{n}", [P, HC, HID]) for n in "kvro"]
            cols = s5("tm_cols", [P, 7, HC])
            names = ("ln_w", "ln_b", "mix_k", "mix_v", "mix_r", "time_decay", "current_token_weight")
            col = {n: cols[:, i, :] for i, n in enumerate(names)}
            s_w = [sems(f"tm_w{n}_in") for n in "kvro"]
            s_cols = sems("tm_cols_in")

            def loads(sp):
                sp.dma_start(cols[:], src["tm_cols"]).then_inc(s_cols, 16)
                for n, t, s in zip("kvro", w, s_w):
                    sp.dma_start(t[:], src["tm_w" + n]).then_inc(s, 16)
                sp.wait_ge(s_cols, 16)
            layernorm(nc, sems, "ln4", X, ident, (xT,), affine=(col["ln_w"], col["ln_b"]), s_affine=s_cols, twice=True,
                      loads=loads)
            time_mix(nc, sems, X, xT, w, col, s_w)

        with ExitStack() as ctx:
            s6 = lambda n, s, d=F32: ctx.enter_context(nc.sbuf_tensor(n, s, d))
            xhi, xlo = s6("f1_xhi", [P, HC, TOK], F32R), s6("f1_xlo", [P, HC, TOK], F32R)
            layernorm(nc, sems, "ln5", X, ident, (xhi, xlo))
            experts(nc, sems, "f1", X, xhi, xlo, ident, src["f1_stream"], src["f1_router"], 64, 8, 33, True, out, s_out)


def rope_tables():
    import numpy as np
    f = np.float32
    inv = (f(1.0) / np.power(f(10000.0), (np.arange(0, DC, 2, dtype=f) / f(DC)).astype(f)).astype(f)).astype(f)
    angle = (np.arange(KEYS, dtype=f)[:, None] * inv[None, :]).astype(f).astype(np.float64)
    sin = np.repeat(np.sin(angle), 2, axis=-1)
    cos = np.repeat(np.cos(angle), 2, axis=-1)
    sin[:, :DC // 2] *= -1
    tiles = []
    for t in (cos, sin):
        full = np.zeros((KT * P, DC), f)
        full[:KEYS] = t
        tiles.append(np.ascontiguousarray(full.reshape(KT, P, DC).transpose(1, 0, 2)))
    return tiles


def kernel(**inputs):
    import numpy as np
    import concourse.bacc as bacc
    from concourse.bass_utils import run_bass_kernel_spmd

    a = {k: np.asarray(v) for k, v in inputs.items()}
    arrays = layouts(a)
    nc = bacc.Bacc("TRN2", target_bir_lowering=False, num_devices=1)
    arrays = {k: np.ascontiguousarray(v) for k, v in arrays.items()}
    src = {k: nc.dram_tensor("in_" + k, v.shape, mybir.dt.from_np(v.dtype), kind="ExternalInput").ap()
           for k, v in arrays.items()}
    out = nc.dram_tensor("out", (TOK, HID), F32, kind="ExternalOutput").ap()
    perceiver(nc, src, out)
    r = run_bass_kernel_spmd(nc, [{"in_" + k: v for k, v in arrays.items()}], core_ids=[0])
    return r.results[0]["out"].reshape(BATCH, SEQ, HID)


def layouts(a):
    import numpy as np
    cosN, sinN = rope_tables()
    d = {"x": a["x"].reshape(TOK, HID), "ctx": a["ctx_512"], "cosN": cosN, "sinN": sinN}
    d["wqrT"] = a["L0_xattn_W_qr"].transpose(2, 0, 1)
    d["wkrT"] = a["L0_xattn_W_kr"].transpose(2, 0, 1)
    d["wkcqT"] = a["L0_xattn_w_kc_q"].reshape(HEADS, DK, 2, DCQ // 2).transpose(3, 2, 0, 1)
    d["wq"] = a["L0_xattn_Wq"].reshape(HEADS, DK, HID).transpose(1, 0, 2)
    d["wkckv"] = a["L0_xattn_w_kc_kv"].transpose(1, 0, 2)
    d["woT"] = a["L0_xattn_Wo"].reshape(HID, HEADS, DK).transpose(2, 1, 0)
    by_chunk = lambda w: w.reshape(HC, P, -1).transpose(1, 0, 2)
    for n, k in (("a0_wq", "W_q"), ("a0_wk", "W_k"), ("a0_wv", "W_v"), ("a0_wo", "W_o")):
        d[n] = by_chunk(a["L0_attn_" + k])
    d["x1_wq"] = by_chunk(a["L1_xattn_Wq"].T)
    d["x1_wo"] = by_chunk(a["L1_xattn_Wout"].T)
    d["x1_wk"], d["x1_wv"] = a["L1_xattn_Wkv_expand"][:HID].T, a["L1_xattn_Wkv_expand"][HID:].T
    d["x1_lat"] = a["ctx_512"][:, :SEQ].transpose(2, 0, 1).reshape(DC, TOK)
    for n, k in (("k", "Wk"), ("v", "Wv"), ("r", "Wr"), ("o", "Wo")):
        d["tm_w" + n] = by_chunk(a["L1_attn_" + k].T)
    names = ("ln_w", "ln_b", "mix_k", "mix_v", "mix_r", "time_decay", "current_token_weight")
    d["tm_cols"] = np.stack([a["L1_attn_" + n].reshape(HC, P).T for n in names], axis=1)

    def stream(gate, up, down, sel, NT):
        f = np.float32
        s = np.zeros((NT, P, 7 * P), f)
        H = gate.shape[1]
        pad = lambda m, ax: np.pad(m, [(0, NT * P - H if i == ax else 0) for i in range(2)])
        for at, m in ((0, gate), (2 * P, up)):
            s[:, :, at:at + 2 * P] = pad(m, 1).reshape(HC, P, NT, P).transpose(2, 1, 0, 3).reshape(NT, P, 2 * P)
        s[:, :, 4 * P:6 * P] = pad(down, 0).reshape(NT, P, HID)
        s[:, :, 6 * P:] = sel.reshape(P, NT, P).transpose(1, 0, 2)
        return s

    E, I, NT = 16, 176, 25
    flat = lambda w: w.transpose(1, 0, 2).reshape(HID, -1)
    owner = np.minimum(np.arange(NT * P) // I, E)
    sel = np.zeros((P, NT * P), np.float32)
    for half in range(2):
        sel[owner + (E + 1) * half, np.arange(NT * P)] = 1.0
    d["f0_stream"] = stream(np.concatenate([flat(a["L0_ffn_w_gate"]), a["L0_ffn_sw_gate"]], 1),
                            np.concatenate([flat(a["L0_ffn_w_up"]), a["L0_ffn_sw_up"]], 1),
                            np.concatenate([a["L0_ffn_w_down"].reshape(E * I, HID), a["L0_ffn_sw_down"]], 0), sel, NT)
    d["f0_router"] = by_chunk(a["L0_ffn_gate_w"].T)

    E, I, NT = 64, 64, 33
    sel = np.zeros((P, NT * P), np.float32)
    n = np.arange(E * I)
    for half in range(2):
        sel[n // I + E * half, n] = 1.0
        sel[half, E * I:E * I + I] = 1.0
    gu = a["L1_ffn_gu_w"]
    to_cols = lambda w: w.transpose(2, 0, 1).reshape(HID, -1)
    d["f1_stream"] = stream(np.concatenate([to_cols(gu[:, :I]), a["L1_ffn_sh_gate_w"].T], 1),
                            np.concatenate([to_cols(gu[:, I:]), a["L1_ffn_sh_up_w"].T], 1),
                            np.concatenate([a["L1_ffn_dp_w"].transpose(0, 2, 1).reshape(E * I, HID),
                                            a["L1_ffn_sh_down_w"].T], 0), sel, NT)
    router = np.concatenate([a["L1_ffn_gate_w"].T, a["L1_ffn_sh_gate1_w"].T, np.zeros((HID, 1), np.float32)], 1)
    d["f1_router"] = by_chunk(router)
    return d
```
